# Optimizing a Trainium2 kernel written in Bass

```python
import numpy as np
import jax
import jax.numpy as jnp

def _softmax(x, axis=-1):
    return jax.nn.softmax(x, axis=axis)

def _gelu(x):
    return jax.nn.gelu(x, approximate=True)

def _silu(x):
    return jax.nn.silu(x)

def _sigmoid(x):
    return jax.nn.sigmoid(x)

def _layernorm(x, axis=-1, eps=1e-05):
    m = jnp.mean(x, axis=axis, keepdims=True)
    v = jnp.var(x, axis=axis, keepdims=True)
    return (x - m) / jnp.sqrt(v + eps)

def _scatter_add(tgt, idx, src, axis=0):
    return tgt.at[idx].add(src)

def _segment_sum(src, seg, n):
    return jax.ops.segment_sum(src, seg, n)
kernel_name = 'mk_conv_attn_hybrid_d4_conv_nhwc768_r4_2fae20'

def setup_inputs(seed: int=0):
    np.random.seed(seed)
    _w = jnp.asarray

    def _rec_inputs():
        import jax
        import jax.numpy as jnp
        _gk = jax.random.key(seed)
        x = -0.0004039 + 1 * jax.random.normal(jax.random.fold_in(_gk, 1), (4, 16, 16, 192), jnp.float32)
        return x
    x = _rec_inputs()

    def _L0_conv_setup():
        import jax, jax.numpy as jnp
        import numpy as np
        B_, H_, W_, DM = (4, 16, 16, 192)
        DI = int(0.5 * DM)
        N = 16
        R = -(-DM // 16)
        K = 4

        def selective_scan(xs, dts, As, Bs, Cs, Dsk):
            u = jnp.moveaxis(xs, -1, 0)
            d = jnp.moveaxis(dts, -1, 0)
            Bt = jnp.moveaxis(Bs, -1, 0)
            Ct = jnp.moveaxis(Cs, -1, 0)

            def step(h, inp):
                u_t, d_t, B_t, C_t = inp
                dA = jnp.exp(d_t[..., None] * As)
                h = h * dA + (d_t * u_t)[..., None] * B_t[:, :, None, :]
                y = jnp.einsum('bkcn,bkn->bkc', h, C_t)
                return (h, y)
            h0 = jnp.zeros(u.shape[1:] + (As.shape[-1],), u.dtype)
            _, ys = jax.lax.scan(step, h0, (u, d, Bt, Ct))
            ys = jnp.moveaxis(ys, 0, -1)
            return ys + Dsk[None, :, :, None] * xs
        key = jax.random.key(seed)
        ks = jax.random.split(key, 8)
        s = lambda i, shape, sc=0.02: jax.random.normal(ks[i], shape, jnp.float32) * sc
        return dict(x=jax.random.normal(ks[0], (B_, H_, W_, DM), jnp.float32), in_proj_w=s(1, (2 * DI, DM)), conv_w=s(2, (DI, 1, 3, 3)), conv_b=jnp.zeros((DI,), jnp.float32), x_proj_w=s(3, (K, R + 2 * N, DI)), dt_projs_w=s(4, (K, DI, R)), dt_projs_b=s(5, (K, DI)), A_logs=jnp.log(jnp.tile(jnp.arange(1, N + 1, dtype=jnp.float32)[None, :], (K * DI, 1))), Ds=jnp.ones((K * DI,), jnp.float32), out_norm_g=jnp.ones((DI,), jnp.float32), out_norm_b=jnp.zeros((DI,), jnp.float32), out_proj_w=s(6, (DM, DI)))
    _L0_conv_all = _L0_conv_setup()
    _L0_conv_in = {k: v for k, v in _L0_conv_all.items() if k in ('in_proj_w', 'conv_w', 'conv_b', 'x_proj_w', 'dt_projs_w', 'dt_projs_b', 'A_logs', 'Ds', 'out_norm_g', 'out_norm_b', 'out_proj_w')}
    del _L0_conv_all

    def _L1_conv_setup():
        import jax, jax.numpy as jnp
        import numpy as np
        D_HEAD = 16
        KERNEL = 7

        def _neigh_idx(L, K):
            start = jnp.clip(jnp.arange(L) - K // 2, 0, L - K)
            return start[:, None] + jnp.arange(K)[None, :]
        key = jax.random.key(seed)
        k1, k2, k3 = jax.random.split(key, 3)
        B, H, W, D = (2, 48, 48, 192)
        x = jax.random.normal(k1, (B, H, W, D), jnp.float32)
        w_qkv = jax.random.normal(k2, (D, 3 * D), jnp.float32) / np.sqrt(D).astype(np.float32)
        w_out = jax.random.normal(k3, (D, D), jnp.float32) / np.sqrt(D).astype(np.float32)
        return {'x': x, 'w_qkv': w_qkv, 'w_out': w_out}
    _L1_conv_all = _L1_conv_setup()
    _L1_conv_in = {k: v for k, v in _L1_conv_all.items() if k in ('w_qkv', 'w_out')}
    del _L1_conv_all

    def _L2_attn_setup():
        import jax, jax.numpy as jnp
        import numpy as np
        NUM_HEADS = 12
        HEAD_DIM = 16
        ATTN_SCALE = HEAD_DIM ** (-0.5)
        OUT_BITS = 8
        EXP_N = 30

        def ste_round(x):
            return x + jax.lax.stop_gradient(jnp.round(x) - x)

        def ste_floor(x):
            return x + jax.lax.stop_gradient(jnp.floor(x) - x)

        def fq(x, s):
            return jnp.clip(ste_round(x / s), -128.0, 127.0) * s

        def layernorm(x, g, b, eps=1e-06):
            mu = jnp.mean(x, axis=-1, keepdims=True)
            var = jnp.mean(jnp.square(x - mu), axis=-1, keepdims=True)
            return (x - mu) * jax.lax.rsqrt(var + eps) * g + b

        def int_softmax(attn, s):
            x_int = ste_round(attn / s)
            x_int = x_int - jnp.max(x_int, axis=-1, keepdims=True)
            x0_int = jnp.floor(-0.6931 / s)
            x_int = jnp.maximum(x_int, EXP_N * x0_int)
            q = ste_floor(x_int / x0_int)
            r = x_int - x0_int * q
            b_int = jnp.floor(1.353 / s)
            c_int = jnp.floor(0.344 / (0.3585 * s * s))
            z = r + b_int
            exp_int = ste_floor((z * z + c_int) * jnp.exp2(EXP_N - q))
            exp_sum = jnp.sum(exp_int, axis=-1, keepdims=True)
            factor = ste_floor(2.0 ** 32 / exp_sum)
            out_int = ste_floor(exp_int * factor / 2.0 ** (32 - OUT_BITS + 1))
            return out_int / 2.0 ** (OUT_BITS - 1)
        key = jax.random.key(seed)
        ks = jax.random.split(key, 6)
        B, N, C = (16, 197, 192)
        inp = {'x': jax.random.normal(ks[0], (B, N, C), jnp.float32), 'w_qkv': jax.random.normal(ks[1], (3 * C, C), jnp.float32) * 0.02, 'b_qkv': jnp.zeros((3 * C,), jnp.float32), 'w_proj': jax.random.normal(ks[2], (C, C), jnp.float32) * 0.02, 'b_proj': jnp.zeros((C,), jnp.float32), 'w_fc1': jax.random.normal(ks[3], (4 * C, C), jnp.float32) * 0.02, 'b_fc1': jnp.zeros((4 * C,), jnp.float32), 'w_fc2': jax.random.normal(ks[4], (C, 4 * C), jnp.float32) * 0.02, 'b_fc2': jnp.zeros((C,), jnp.float32), 'g1': jnp.ones((C,), jnp.float32), 'beta1': jnp.zeros((C,), jnp.float32), 'g2': jnp.ones((C,), jnp.float32), 'beta2': jnp.zeros((C,), jnp.float32), 'scales': jnp.array([0.05, 0.01, 0.05, 0.05, 0.01, 0.05, 0.05, 0.05, 0.01, 0.05, 0.01, 0.05, 0.05], jnp.float32)}
        return inp
    _L2_attn_all = _L2_attn_setup()
    _L2_attn_in = {k: v for k, v in _L2_attn_all.items() if k in ('w_qkv', 'b_qkv', 'w_proj', 'b_proj', 'w_fc1', 'b_fc1', 'w_fc2', 'b_fc2', 'g1', 'beta1', 'g2', 'beta2', 'scales')}
    del _L2_attn_all

    def _L2_ffn_setup():
        import jax, jax.numpy as jnp
        import numpy as np
        DIM = 192
        MOE_INTER = 512
        N_EXPERTS = 16
        TOP_K = 2
        SHARED_INTER = 2 * 512
        ROUTE_SCALE = 1.0
        B, S = (8, 49)
        key = jax.random.key(seed)
        ks = jax.random.split(key, 8)
        sc = 0.02
        return {'x': jax.random.normal(ks[0], (B, S, DIM), jnp.float32), 'gate_w': jax.random.normal(ks[1], (N_EXPERTS, DIM), jnp.float32) * sc, 'w1': jax.random.normal(ks[2], (N_EXPERTS, MOE_INTER, DIM), jnp.float32) * sc, 'w2': jax.random.normal(ks[3], (N_EXPERTS, DIM, MOE_INTER), jnp.float32) * sc, 'w3': jax.random.normal(ks[4], (N_EXPERTS, MOE_INTER, DIM), jnp.float32) * sc, 'sw1': jax.random.normal(ks[5], (SHARED_INTER, DIM), jnp.float32) * sc, 'sw2': jax.random.normal(ks[6], (DIM, SHARED_INTER), jnp.float32) * sc, 'sw3': jax.random.normal(ks[7], (SHARED_INTER, DIM), jnp.float32) * sc}
    _L2_ffn_all = _L2_ffn_setup()
    _L2_ffn_in = {k: v for k, v in _L2_ffn_all.items() if k in ('gate_w', 'w1', 'w2', 'w3', 'sw1', 'sw2', 'sw3')}
    del _L2_ffn_all

    def _L3_attn_setup():
        import jax, jax.numpy as jnp
        import numpy as np
        D = 192
        key = jax.random.key(seed)
        k1, k2, k3 = jax.random.split(key, 3)
        s = 1.0 / np.sqrt(D)
        return {'x': jax.random.normal(k1, (8, 512, D), dtype=jnp.float32), 'w_qkv': jax.random.normal(k2, (D, 3 * D), dtype=jnp.float32) * s, 'b_qkv': jnp.zeros((3 * D,), dtype=jnp.float32), 'w_out': jax.random.normal(k3, (D, D), dtype=jnp.float32) * s, 'b_out': jnp.zeros((D,), dtype=jnp.float32)}
    _L3_attn_all = _L3_attn_setup()
    _L3_attn_in = {k: v for k, v in _L3_attn_all.items() if k in ('w_qkv', 'b_qkv', 'w_out', 'b_out')}
    del _L3_attn_all

    def _L3_ffn_setup():
        import jax, jax.numpy as jnp
        import numpy as np
        B, S, H, F, E, TOP_K = (4, 512, 192, 768, 8, 2)
        key = jax.random.key(seed)
        ks = jax.random.split(key, 6)
        x = jax.random.normal(ks[0], (B, S, H), dtype=jnp.float32)
        Wr = jax.random.normal(ks[1], (E, H), dtype=jnp.float32) * 0.02
        Wi = jax.random.normal(ks[2], (E, F, H), dtype=jnp.float32) * 0.02
        bi = jnp.zeros((E, F), dtype=jnp.float32)
        Wo = jax.random.normal(ks[3], (E, H, F), dtype=jnp.float32) * 0.02
        bo = jnp.zeros((E, H), dtype=jnp.float32)
        return {'x': x, 'Wr': Wr, 'Wi': Wi, 'bi': bi, 'Wo': Wo, 'bo': bo}
    _L3_ffn_all = _L3_ffn_setup()
    _L3_ffn_in = {k: v for k, v in _L3_ffn_all.items() if k in ('Wr', 'Wi', 'bi', 'Wo', 'bo')}
    del _L3_ffn_all
    return {'x': x, 'L0_conv_in_proj_w': _L0_conv_in['in_proj_w'], 'L0_conv_conv_w': _L0_conv_in['conv_w'], 'L0_conv_conv_b': _L0_conv_in['conv_b'], 'L0_conv_x_proj_w': _L0_conv_in['x_proj_w'], 'L0_conv_dt_projs_w': _L0_conv_in['dt_projs_w'], 'L0_conv_dt_projs_b': _L0_conv_in['dt_projs_b'], 'L0_conv_A_logs': _L0_conv_in['A_logs'], 'L0_conv_Ds': _L0_conv_in['Ds'], 'L0_conv_out_norm_g': _L0_conv_in['out_norm_g'], 'L0_conv_out_norm_b': _L0_conv_in['out_norm_b'], 'L0_conv_out_proj_w': _L0_conv_in['out_proj_w'], 'L1_conv_w_qkv': _L1_conv_in['w_qkv'], 'L1_conv_w_out': _L1_conv_in['w_out'], 'L2_attn_w_qkv': _L2_attn_in['w_qkv'], 'L2_attn_b_qkv': _L2_attn_in['b_qkv'], 'L2_attn_w_proj': _L2_attn_in['w_proj'], 'L2_attn_b_proj': _L2_attn_in['b_proj'], 'L2_attn_w_fc1': _L2_attn_in['w_fc1'], 'L2_attn_b_fc1': _L2_attn_in['b_fc1'], 'L2_attn_w_fc2': _L2_attn_in['w_fc2'], 'L2_attn_b_fc2': _L2_attn_in['b_fc2'], 'L2_attn_g1': _L2_attn_in['g1'], 'L2_attn_beta1': _L2_attn_in['beta1'], 'L2_attn_g2': _L2_attn_in['g2'], 'L2_attn_beta2': _L2_attn_in['beta2'], 'L2_attn_scales': _L2_attn_in['scales'], 'L2_ffn_gate_w': _L2_ffn_in['gate_w'], 'L2_ffn_w1': _L2_ffn_in['w1'], 'L2_ffn_w2': _L2_ffn_in['w2'], 'L2_ffn_w3': _L2_ffn_in['w3'], 'L2_ffn_sw1': _L2_ffn_in['sw1'], 'L2_ffn_sw2': _L2_ffn_in['sw2'], 'L2_ffn_sw3': _L2_ffn_in['sw3'], 'L3_attn_w_qkv': _L3_attn_in['w_qkv'], 'L3_attn_b_qkv': _L3_attn_in['b_qkv'], 'L3_attn_w_out': _L3_attn_in['w_out'], 'L3_attn_b_out': _L3_attn_in['b_out'], 'L3_ffn_Wr': _L3_ffn_in['Wr'], 'L3_ffn_Wi': _L3_ffn_in['Wi'], 'L3_ffn_bi': _L3_ffn_in['bi'], 'L3_ffn_Wo': _L3_ffn_in['Wo'], 'L3_ffn_bo': _L3_ffn_in['bo']}

def reference(x, L0_conv_in_proj_w, L0_conv_conv_w, L0_conv_conv_b, L0_conv_x_proj_w, L0_conv_dt_projs_w, L0_conv_dt_projs_b, L0_conv_A_logs, L0_conv_Ds, L0_conv_out_norm_g, L0_conv_out_norm_b, L0_conv_out_proj_w, L1_conv_w_qkv, L1_conv_w_out, L2_attn_w_qkv, L2_attn_b_qkv, L2_attn_w_proj, L2_attn_b_proj, L2_attn_w_fc1, L2_attn_b_fc1, L2_attn_w_fc2, L2_attn_b_fc2, L2_attn_g1, L2_attn_beta1, L2_attn_g2, L2_attn_beta2, L2_attn_scales, L2_ffn_gate_w, L2_ffn_w1, L2_ffn_w2, L2_ffn_w3, L2_ffn_sw1, L2_ffn_sw2, L2_ffn_sw3, L3_attn_w_qkv, L3_attn_b_qkv, L3_attn_w_out, L3_attn_b_out, L3_ffn_Wr, L3_ffn_Wi, L3_ffn_bi, L3_ffn_Wo, L3_ffn_bo):
    import jax
    import jax.numpy as jnp

    def _L0_conv_ref(x, in_proj_w, conv_w, conv_b, x_proj_w, dt_projs_w, dt_projs_b, A_logs, Ds, out_norm_g, out_norm_b, out_proj_w):
        import jax, jax.numpy as jnp
        import numpy as np
        B_, H_, W_, DM = (4, 16, 16, 192)
        DI = int(0.5 * DM)
        N = 16
        R = -(-DM // 16)
        K = 4

        def selective_scan(xs, dts, As, Bs, Cs, Dsk):
            u = jnp.moveaxis(xs, -1, 0)
            d = jnp.moveaxis(dts, -1, 0)
            Bt = jnp.moveaxis(Bs, -1, 0)
            Ct = jnp.moveaxis(Cs, -1, 0)

            def step(h, inp):
                u_t, d_t, B_t, C_t = inp
                dA = jnp.exp(d_t[..., None] * As)
                h = h * dA + (d_t * u_t)[..., None] * B_t[:, :, None, :]
                y = jnp.einsum('bkcn,bkn->bkc', h, C_t)
                return (h, y)
            h0 = jnp.zeros(u.shape[1:] + (As.shape[-1],), u.dtype)
            _, ys = jax.lax.scan(step, h0, (u, d, Bt, Ct))
            ys = jnp.moveaxis(ys, 0, -1)
            return ys + Dsk[None, :, :, None] * xs
        B, H, W, _ = x.shape
        L = H * W
        xz = x @ in_proj_w.T
        xh, z = jnp.split(xz, 2, axis=-1)
        xc = jnp.transpose(xh, (0, 3, 1, 2))
        xc = jax.lax.conv_general_dilated(xc, conv_w, (1, 1), 'SAME', feature_group_count=DI)
        xc = jax.nn.silu(xc + conv_b[None, :, None, None])
        x_flat = xc.reshape(B, DI, L)
        x_t = jnp.transpose(xc, (0, 1, 3, 2)).reshape(B, DI, L)
        x_hwwh = jnp.stack([x_flat, x_t], 1)
        xs = jnp.concatenate([x_hwwh, jnp.flip(x_hwwh, -1)], 1)
        x_dbl = jnp.einsum('bkdl,kcd->bkcl', xs, x_proj_w)
        dts, Bs, Cs = jnp.split(x_dbl, [R, R + N], axis=2)
        dts = jnp.einsum('bkrl,kdr->bkdl', dts, dt_projs_w)
        dts = jax.nn.softplus(dts + dt_projs_b[None, :, :, None])
        As = -jnp.exp(A_logs).reshape(K, DI, N)
        out_y = selective_scan(xs, dts, As, Bs, Cs, Ds.reshape(K, DI))
        inv_y = jnp.flip(out_y[:, 2:4], -1)
        wh_y = jnp.transpose(out_y[:, 1].reshape(B, DI, W, H), (0, 1, 3, 2)).reshape(B, DI, L)
        invwh_y = jnp.transpose(inv_y[:, 1].reshape(B, DI, W, H), (0, 1, 3, 2)).reshape(B, DI, L)
        y = out_y[:, 0] + inv_y[:, 0] + wh_y + invwh_y
        y = jnp.transpose(y, (0, 2, 1)).reshape(B, H, W, DI)
        mu = y.mean(-1, keepdims=True)
        var = y.var(-1, keepdims=True)
        y = (y - mu) / jnp.sqrt(var + 1e-05) * out_norm_g + out_norm_b
        y = y * jax.nn.silu(z)
        return y @ out_proj_w.T

    def _L1_conv_ref(x, w_qkv, w_out):
        import jax, jax.numpy as jnp
        import numpy as np
        D_HEAD = 16
        KERNEL = 7

        def _neigh_idx(L, K):
            start = jnp.clip(jnp.arange(L) - K // 2, 0, L - K)
            return start[:, None] + jnp.arange(K)[None, :]
        B, H, W, D = x.shape
        e = D_HEAD
        nh = D // e
        K = KERNEL
        qkv = (x @ w_qkv).reshape(B, H, W, 3, nh, e)
        qkv = jnp.transpose(qkv, (3, 0, 4, 1, 2, 5))
        q, k, v = (qkv[0], qkv[1], qkv[2])
        q = q * e ** (-0.5)
        ih = _neigh_idx(H, K)
        iw = _neigh_idx(W, K)
        kg = k[:, :, ih[:, :, None, None], iw[None, None, :, :], :]
        scores = jnp.einsum('nhije,nhiajbe->nhijab', q, kg)
        attn = jax.nn.softmax(scores.reshape(B, nh, H, W, K * K), axis=-1)
        attn = attn.reshape(B, nh, H, W, K, K)
        vg = v[:, :, ih[:, :, None, None], iw[None, None, :, :], :]
        o = jnp.einsum('nhijab,nhiajbe->nhije', attn, vg)
        o = jnp.transpose(o, (0, 2, 3, 1, 4)).reshape(B, H, W, D)
        return o @ w_out

    def _L2_attn_ref(x, w_qkv, b_qkv, w_proj, b_proj, w_fc1, b_fc1, w_fc2, b_fc2, g1, beta1, g2, beta2, scales):
        import jax, jax.numpy as jnp
        import numpy as np
        NUM_HEADS = 12
        HEAD_DIM = 16
        ATTN_SCALE = HEAD_DIM ** (-0.5)
        OUT_BITS = 8
        EXP_N = 30

        def ste_round(x):
            return x + jax.lax.stop_gradient(jnp.round(x) - x)

        def ste_floor(x):
            return x + jax.lax.stop_gradient(jnp.floor(x) - x)

        def fq(x, s):
            return jnp.clip(ste_round(x / s), -128.0, 127.0) * s

        def layernorm(x, g, b, eps=1e-06):
            mu = jnp.mean(x, axis=-1, keepdims=True)
            var = jnp.mean(jnp.square(x - mu), axis=-1, keepdims=True)
            return (x - mu) * jax.lax.rsqrt(var + eps) * g + b

        def int_softmax(attn, s):
            x_int = ste_round(attn / s)
            x_int = x_int - jnp.max(x_int, axis=-1, keepdims=True)
            x0_int = jnp.floor(-0.6931 / s)
            x_int = jnp.maximum(x_int, EXP_N * x0_int)
            q = ste_floor(x_int / x0_int)
            r = x_int - x0_int * q
            b_int = jnp.floor(1.353 / s)
            c_int = jnp.floor(0.344 / (0.3585 * s * s))
            z = r + b_int
            exp_int = ste_floor((z * z + c_int) * jnp.exp2(EXP_N - q))
            exp_sum = jnp.sum(exp_int, axis=-1, keepdims=True)
            factor = ste_floor(2.0 ** 32 / exp_sum)
            out_int = ste_floor(exp_int * factor / 2.0 ** (32 - OUT_BITS + 1))
            return out_int / 2.0 ** (OUT_BITS - 1)
        B, N, C = x.shape
        s_n1, s_wqkv, s_qkv, s_attn, s_wproj, s_sv, s_r1, s_n2, s_wfc1, s_act, s_wfc2, s_m2, s_r2 = [scales[i] for i in range(13)]
        x_norm = fq(layernorm(x, g1, beta1), s_n1)
        qkv = jnp.einsum('bnc,dc->bnd', x_norm, fq(w_qkv, s_wqkv)) + b_qkv
        qkv = fq(qkv, s_qkv)
        qkv = qkv.reshape(B, N, 3, NUM_HEADS, HEAD_DIM).transpose(2, 0, 3, 1, 4)
        q, k, v = (qkv[0], qkv[1], qkv[2])
        attn = jnp.einsum('bhnd,bhmd->bhnm', q, k) * ATTN_SCALE
        attn = fq(attn, s_attn)
        attn = int_softmax(attn, s_attn)
        x_attn = jnp.einsum('bhnm,bhmd->bhnd', attn, v)
        x_attn = x_attn.transpose(0, 2, 1, 3).reshape(B, N, C)
        x_attn = jnp.einsum('bnc,dc->bnd', x_attn, fq(w_proj, s_wproj)) + b_proj
        x_attn = fq(x_attn, s_sv)
        x = fq(x + x_attn, s_r1)
        x_norm = fq(layernorm(x, g2, beta2), s_n2)
        h = jnp.einsum('bnc,dc->bnd', x_norm, fq(w_fc1, s_wfc1)) + b_fc1
        h = fq(jax.nn.gelu(h, approximate=False), s_act)
        h = jnp.einsum('bnd,cd->bnc', h, fq(w_fc2, s_wfc2)) + b_fc2
        h = fq(h, s_m2)
        x = fq(x + h, s_r2)
        return x

    def _L2_ffn_ref(x, gate_w, w1, w2, w3, sw1, sw2, sw3):
        import jax, jax.numpy as jnp
        import numpy as np
        DIM = 192
        MOE_INTER = 512
        N_EXPERTS = 16
        TOP_K = 2
        SHARED_INTER = 2 * 512
        ROUTE_SCALE = 1.0
        B, S = (8, 49)
        Bb, Ss, D = x.shape
        xf = x.reshape(-1, D)
        T = xf.shape[0]
        scores = jax.nn.softmax(xf @ gate_w.T, axis=-1)
        topw, topi = jax.lax.top_k(scores, TOP_K)
        topw = topw * ROUTE_SCALE
        comb = jnp.zeros((T, N_EXPERTS), xf.dtype).at[jnp.arange(T)[:, None], topi].set(topw)
        h = jax.nn.silu(jnp.einsum('td,eid->tei', xf, w1)) * jnp.einsum('td,eid->tei', xf, w3)
        h = h * comb[:, :, None]
        y = jnp.einsum('tei,edi->td', h, w2)
        z = jax.nn.silu(xf @ sw1.T) * (xf @ sw3.T) @ sw2.T
        return (y + z).reshape(Bb, Ss, D)

    def _L3_attn_ref(x, w_qkv, b_qkv, w_out, b_out):
        import jax, jax.numpy as jnp
        import numpy as np
        D = 192
        qkv = x @ w_qkv + b_qkv
        q, k, v = jnp.split(qkv, 3, axis=-1)
        scale = 1.0 / jnp.sqrt(jnp.asarray(q.shape[-1], q.dtype))
        attn = jax.nn.softmax(jnp.einsum('bqd,bkd->bqk', q, k) * scale, axis=-1)
        out = jnp.einsum('bqk,bkd->bqd', attn, v)
        return out @ w_out + b_out

    def _L3_ffn_ref(x, Wr, Wi, bi, Wo, bo):
        import jax, jax.numpy as jnp
        import numpy as np
        B, S, H, F, E, TOP_K = (4, 512, 192, 768, 8, 2)
        xf = x.reshape(-1, x.shape[-1])
        router_logits = jnp.einsum('th,eh->te', xf, Wr)
        topk_vals, topk_idx = jax.lax.top_k(router_logits, TOP_K)
        routing_weights = jax.nn.softmax(topk_vals, axis=-1)
        h = jnp.einsum('th,efh->etf', xf, Wi) + bi[:, None, :]
        h = jax.nn.gelu(h, approximate=False)
        expert_out = jnp.einsum('etf,ehf->eth', h, Wo) + bo[:, None, :]
        expert_out = jnp.transpose(expert_out, (1, 0, 2))
        gathered = jnp.take_along_axis(expert_out, topk_idx[:, :, None], axis=1)
        out = jnp.einsum('tk,tkh->th', routing_weights, gathered)
        return out.reshape(x.shape)

    def _gn(v, G=32, eps=1e-05):
        B_, H_, W_, C_ = v.shape
        g = v.reshape(B_, H_, W_, G, C_ // G)
        m = jnp.mean(g, axis=(1, 2, 4), keepdims=True)
        s = jnp.var(g, axis=(1, 2, 4), keepdims=True)
        return ((g - m) / jnp.sqrt(s + eps)).reshape(v.shape)

    def _ln_c(v, eps=1e-06):
        m = jnp.mean(v, axis=-1, keepdims=True)
        s = jnp.var(v, axis=-1, keepdims=True)
        return (v - m) / jnp.sqrt(s + eps)

    def _ln_t(v, eps=1e-05):
        m = jnp.mean(v, axis=-1, keepdims=True)
        s = jnp.var(v, axis=-1, keepdims=True)
        return (v - m) / jnp.sqrt(s + eps)

    def _to_tokens(v):
        B_, H_, W_, C_ = v.shape
        return v.reshape(B_, H_ * W_, C_)

    def _from_tokens(t, like):
        return t.reshape(like.shape)
    x = x + _L0_conv_ref(_gn(x), L0_conv_in_proj_w, L0_conv_conv_w, L0_conv_conv_b, L0_conv_x_proj_w, L0_conv_dt_projs_w, L0_conv_dt_projs_b, L0_conv_A_logs, L0_conv_Ds, L0_conv_out_norm_g, L0_conv_out_norm_b, L0_conv_out_proj_w)
    x = x + _L1_conv_ref(_gn(x), L1_conv_w_qkv, L1_conv_w_out)
    t = _to_tokens(x)
    t = t + _L2_attn_ref(_ln_t(t), L2_attn_w_qkv, L2_attn_b_qkv, L2_attn_w_proj, L2_attn_b_proj, L2_attn_w_fc1, L2_attn_b_fc1, L2_attn_w_fc2, L2_attn_b_fc2, L2_attn_g1, L2_attn_beta1, L2_attn_g2, L2_attn_beta2, L2_attn_scales)
    t = t + _L2_ffn_ref(_ln_t(t), L2_ffn_gate_w, L2_ffn_w1, L2_ffn_w2, L2_ffn_w3, L2_ffn_sw1, L2_ffn_sw2, L2_ffn_sw3)
    t = t + _L3_attn_ref(_ln_t(t), L3_attn_w_qkv, L3_attn_b_qkv, L3_attn_w_out, L3_attn_b_out)
    t = t + _L3_ffn_ref(_ln_t(t), L3_ffn_Wr, L3_ffn_Wi, L3_ffn_bi, L3_ffn_Wo, L3_ffn_bo)
    x = _from_tokens(t, x)
    return x

_drawn_inputs = setup_inputs


def setup_inputs(seed=0):
    import zlib

    import numpy as np

    out = dict(_drawn_inputs(seed))
    spreads = {'L0_conv_conv_b': (0.0, 0.1),
     'L0_conv_Ds': (1.0, 0.6),
     'L0_conv_out_norm_g': (1.0, 0.6),
     'L0_conv_out_norm_b': (0.0, 0.728),
     'L2_attn_b_qkv': (0.0, 0.1),
     'L2_attn_b_proj': (0.0, 0.1),
     'L2_attn_b_fc1': (0.0, 0.401),
     'L2_attn_b_fc2': (0.0, 0.1),
     'L2_attn_g1': (1.0, 0.2),
     'L2_attn_beta1': (0.0, 0.1),
     'L2_attn_g2': (1.0, 0.6),
     'L2_attn_beta2': (0.0, 0.637),
     'L3_attn_b_qkv': (0.0, 0.546),
     'L3_attn_b_out': (0.0, 0.632),
     'L3_ffn_bi': (0.0, 2.0),
     'L3_ffn_bo': (0.0, 0.8)}
    factors = {'L0_conv_conv_w': 5.468,
     'L0_conv_x_proj_w': 33.754,
     'L0_conv_dt_projs_w': 30.351,
     'L0_conv_dt_projs_b': 38.358,
     'L0_conv_A_logs': 28.652,
     'L2_ffn_gate_w': 8.0,
     'L2_ffn_w1': 8.0,
     'L2_ffn_w2': 8.0,
     'L2_ffn_w3': 8.0,
     'L2_ffn_sw1': 4.317,
     'L2_ffn_sw2': 4.325,
     'L2_ffn_sw3': 4.241,
     'L3_attn_w_qkv': 3.196,
     'L3_ffn_Wi': 6.126}
    for name, (base, spread) in spreads.items():
        noise = np.random.default_rng([zlib.crc32(name.encode()), seed]).standard_normal(out[name].shape)
        drawn = base * np.exp(spread * noise) if base else spread * noise
        out[name] = jnp.asarray(drawn.astype(out[name].dtype))
    for name, factor in factors.items():
        out[name] = (out[name] * factor).astype(out[name].dtype)
    return out
```

```python
import concourse.bass as bass
from concourse import mybir
from contextlib import ExitStack

F32 = mybir.dt.float32
BF16 = mybir.dt.bfloat16
F16 = mybir.dt.float16
I16 = mybir.dt.int16
I32 = mybir.dt.int32
U32 = mybir.dt.uint32
ALU = mybir.AluOpType
ACT = mybir.ActivationFunctionType
AX = mybir.AxisListType
ds = bass.ds

NB = 4
HW = 16
L = HW * HW
T = NB * L
C = 192
P = 128
CH = C // 2
NT = T // P
BANK = 512
NHALF = T // BANK
MAGIC = 12582912.0


class Ctx:

    def __init__(self, nc, stack):
        self.nc, self.stack, self.sems = nc, stack, []

    def sb(self, name, shape, dt=F32):
        return self.stack.enter_context(self.nc.sbuf_tensor(name, shape, dt))

    def ps(self, name, shape, dt=F32):
        return self.stack.enter_context(self.nc.psum_tensor(name, shape, dt))

    def sem(self, name):
        self.sems.append(self.stack.enter_context(self.nc.semaphore(name)))
        return self.sems[-1]

    def clear(self):
        with self.nc.Block() as block:
            @block.sync
            def _(sync):
                for s in self.sems:
                    sync.sem_clear(s)


class Chain:

    def __init__(self, eng, sem):
        self.eng, self.sem, self.base, self.k = eng, sem, 0, 0

    def __call__(self, ins):
        ins.then_inc(self.sem, 1)
        self.k += 1
        self.eng.wait_ge(self.sem, self.base + self.k)

    def loop(self, i, steps):
        self.start, self.base, self.k, self.steps = self.k, self.k + i * steps, 0, steps

    def end(self, times):
        assert self.k == self.steps, (self.k, self.steps)
        self.base, self.k = 0, self.start + times * self.steps


class GroupNorm:
    N = 2 * NB

    def __init__(self, ctx, pre):
        s = lambda n: ctx.sem(f"{pre}_{n}")
        self.stats, self.gmean, self.spread, self.gvar = s("gn_stats"), s("gn_gmean"), s("gn_spread"), s("gn_gvar")
        self.var, self.std, self.scale, self.out = s("gn_var"), s("gn_std"), s("gn_scale"), s("gn_out")
        sb = lambda n, sh: ctx.sb(f"{pre}_{n}", sh)
        self.st = sb("gn_st", [CH, self.N, 6])
        self.mv = sb("gn_mv", [CH, self.N, 2])
        self.gm = sb("gn_gm", [CH, self.N])
        self.d = sb("gn_d", [CH, self.N])
        self.e = sb("gn_e", [CH, self.N])
        self.sd = sb("gn_sd", [CH, self.N])
        self.rs = sb("gn_rs", [CH, self.N])

    def vector(self, v, src, dst, ps, ready):
        N = self.N
        for i in range(N):
            h, b = divmod(i, NB)
            ready(v, i)
            v.bn_stats(self.st[:, i, :], src[:, h, b * L:(b + 1) * L]).then_inc(self.stats, 1)
        for i in range(N):
            v.wait_ge(self.stats, i + 1)
            v.bn_aggr(self.mv[:, i, :], self.st[:, i, :]).then_inc(self.stats, 1)
        v.wait_ge(self.gmean, 1)
        v.tensor_copy(self.gm[:, :], ps[:, 0:N]).then_inc(self.spread, 1)
        v.wait_ge(self.spread, 1)
        v.tensor_tensor(self.d[:, :], self.mv[:, :, 0], self.gm[:, :], ALU.subtract).then_inc(self.spread, 1)
        v.wait_ge(self.spread, 2)
        v.tensor_tensor(self.e[:, :], self.d[:, :], self.d[:, :], ALU.mult).then_inc(self.spread, 1)
        v.wait_ge(self.spread, 3)
        v.tensor_tensor(self.e[:, :], self.e[:, :], self.mv[:, :, 1], ALU.add).then_inc(self.spread, 1)
        v.wait_ge(self.gvar, 1)
        v.tensor_scalar(self.sd[:, :], ps[:, N:2 * N], 1e-5, None, ALU.add).then_inc(self.var, 1)
        v.wait_ge(self.std, 1)
        v.reciprocal(self.rs[:, :], self.sd[:, :]).then_inc(self.scale, 1)
        v.wait_ge(self.scale, 1)
        for i in range(N):
            h, b = divmod(i, NB)
            v.tensor_scalar(dst[:, h, b * L:(b + 1) * L], src[:, h, b * L:(b + 1) * L],
                            self.gm[:, i:i + 1], self.rs[:, i:i + 1], ALU.subtract, ALU.mult).then_inc(self.out, 1)

    def tensor(self, pe, group, ps):
        N = self.N
        pe.wait_ge(self.stats, 2 * N)
        pe.matmul(ps[:, 0:N], group[:, :], self.mv[:, :, 0], start=True, stop=True).then_inc(self.gmean, 1)
        pe.wait_ge(self.spread, 4)
        pe.matmul(ps[:, N:2 * N], group[:, :], self.e[:, :], start=True, stop=True).then_inc(self.gvar, 1)

    def scalar(self, act):
        act.wait_ge(self.var, 1)
        act.activation(self.sd[:, :], self.sd[:, :], ACT.Sqrt).then_inc(self.std, 1)


class LayerNorm:

    def __init__(self, ctx):
        self.stats, self.var, self.std, self.rstd, self.out = (
            ctx.sem(f"ln_{n}") for n in ("stats", "var", "std", "rstd", "out"))
        self.st = ctx.sb("ln_st", [P, NT, 6])
        self.mv = ctx.sb("ln_mv", [P, NT, 2])
        self.sd = ctx.sb("ln_sd", [P, NT])
        self.rs = ctx.sb("ln_rs", [P, NT])

    def vector(self, v, use, src, dst, eps, ready=None):
        if use:
            v.wait_ge(self.out, NT * use)
        for t in range(NT):
            if ready:
                ready(v, t)
            v.bn_stats(self.st[:, t, :], src[:, t, :]).then_inc(self.stats, 1)
        for t in range(NT):
            v.wait_ge(self.stats, 2 * NT * use + t + 1)
            v.bn_aggr(self.mv[:, t, :], self.st[:, t, :]).then_inc(self.stats, 1)
        v.wait_ge(self.stats, 2 * NT * (use + 1))
        v.tensor_scalar(self.sd[:, :], self.mv[:, :, 1], eps, None, ALU.add).then_inc(self.var, 1)
        v.wait_ge(self.std, use + 1)
        v.reciprocal(self.rs[:, :], self.sd[:, :]).then_inc(self.rstd, 1)
        v.wait_ge(self.rstd, use + 1)
        for t in range(NT):
            v.tensor_scalar(dst[:, t, :], src[:, t, :], self.mv[:, t, 0:1], self.rs[:, t:t + 1],
                            ALU.subtract, ALU.mult).then_inc(self.out, 1)

    def scalar(self, act, use):
        act.wait_ge(self.var, use + 1)
        act.activation(self.sd[:, :], self.sd[:, :], ACT.Sqrt).then_inc(self.std, 1)

    def done(self, eng, use, t):
        eng.wait_ge(self.out, NT * use + t + 1)


DI = C // 2
NS = 16
RK = C // 16
CG = P // NS
NG = DI // CG
KD = 4
PW = HW + 2
PR = NB * (HW + 1) + 2
OR = NB * (HW + 1)


def scan_layer(nc, const, X, D):
    with ExitStack() as stack:
        ctx = Ctx(nc, stack)
        xT = ctx.sb("xT", [CH, 2, T])
        xn = ctx.sb("xn", [CH, 2, T])
        w_in = ctx.sb("w_in", [CH, 2, 2 * DI])
        group = ctx.sb("group", [CH, CH])
        pad = ctx.sb("pad", [DI, PR, PW])
        cw = ctx.sb("cw", [DI, 9])
        cb = ctx.sb("cb", [DI, 1])
        conv = ctx.sb("conv", [DI, OR, HW])
        xc = ctx.sb("xc", [DI, 2, T])
        zs = ctx.sb("zs", [DI, T])
        wdt = ctx.sb("wdt", [DI, KD, RK])
        wB = ctx.sb("wB", [DI, KD, P])
        wC = ctx.sb("wC", [DI, KD, P])
        dtw = ctx.sb("dtw", [RK, KD, DI])
        dtb = ctx.sb("dtb", [DI, KD])
        Dk = ctx.sb("Dk", [DI, KD])
        Dsum = ctx.sb("Dsum", [DI, 1])
        Alog = ctx.sb("Alog", [P, KD * NG])
        Am = ctx.sb("Am", [P, KD * NG])
        sel = ctx.sb("sel", [DI, NG, P])
        selT = ctx.sb("selT", [P, NG, DI])
        dtr = ctx.sb("dtr", [RK, T])
        d_all = ctx.sb("d_all", [DI, KD, T])
        du_all = ctx.sb("du_all", [DI, KD, T])
        Bb = ctx.sb("Bb", [P, KD, T])
        Cb = ctx.sb("Cb", [P, KD, T])
        sp = ctx.sb("sp", [DI, 4, T])
        dA = ctx.sb("dA", [P, 2, 2, T])
        dBu = ctx.sb("dBu", [P, 2, T])
        hs = ctx.sb("hs", [P, 2, T])
        hC = ctx.sb("hC", [P, 2, T])
        ysum = ctx.sb("ysum", [DI, 2, T])
        gamma = ctx.sb("gamma", [DI, 1])
        beta = ctx.sb("beta", [DI, 1])
        avg = ctx.sb("avg", [DI, DI])
        w_out = ctx.sb("w_out", [DI, C])
        gn = GroupNorm(ctx, "l1")
        ps = ctx.ps("ps_l1", [P, 8, BANK])
        S = lambda n: ctx.sem(f"l1_{n}")
        loaded_x, loaded_w, loaded_p, loaded_s = S("loaded_x"), S("loaded_w"), S("loaded_p"), S("loaded_s")
        cleared, proj, padded, convd, activated, ordered = (
            S("cleared"), S("proj"), S("padded"), S("convd"), S("activated"), S("ordered"))
        dt_low, dt_low_sb, dt_full, bc_ps, bc_sb = S("dt_low"), S("dt_low_sb"), S("dt_full"), S("bc_ps"), S("bc_sb")
        sp_act, sp_vec, du_done, A_done = S("sp_act"), S("sp_vec"), S("du_done"), S("A_done")
        d_bc, du_bc, dA_done, dBu_done, scanned, weighted, y_added, y_out = (
            S("d_bc"), S("du_bc"), S("dA_done"), S("dBu_done"), S("scanned"), S("weighted"), S("y_added"),
            S("y_out"))
        act_past, pool_past = S("act_past"), S("pool_past")
        fin, fin_ps, fin_act, res_ps, res = S("fin"), S("fin_ps"), S("fin_act"), S("res_ps"), S("res")
        flat = lambda a: a[:, :, :].rearrange("p k t -> p (k t)")
        d_flat, du_flat, B_flat, C_flat, y_flat = flat(d_all), flat(du_all), flat(Bb), flat(Cb), flat(ysum)
        STEPS = 2 * NG

        with nc.Block() as block:
            @block.sync
            def _(sp_):
                for h in range(2):
                    sp_.dma_start(xT[:, h, :], D["xT"][:, h, :]).then_inc(loaded_x, 16)
                sp_.dma_start(group[:, :], D["group"]).then_inc(loaded_x, 16)
                for dst, src in ((w_in, "w_in"), (cw, "cw"), (cb, "cb")):
                    sp_.dma_start(dst[:], D[src]).then_inc(loaded_w, 16)
                for dst, src in ((wdt, "wdt"), (wB, "wB"), (wC, "wC"), (dtw, "dtw"), (dtb, "dtb")):
                    sp_.dma_start(dst[:], D[src]).then_inc(loaded_p, 16)
                for dst, src in ((Alog, "Alog"), (sel, "sel"), (selT, "selT"), (Dk, "Dk"), (gamma, "out_g"),
                                 (beta, "out_b"), (avg, "avg"), (w_out, "w_out0")):
                    sp_.dma_start(dst[:], D[src]).then_inc(loaded_s, 16)
                for t in range(NT):
                    sp_.dma_start(X[:, t, :], D["x"][t * P:(t + 1) * P, :]).then_inc(loaded_s, 16)

            @block.gpsimd
            def _(pool):
                pool.memset(pad[:], 0.0).then_inc(cleared, 1)
                pool.memset(dA[:], 0.0).then_inc(cleared, 1)
                with pool.Fori(0, 2) as r:
                    for m in range(STEPS):
                        pool.wait_ge(scanned, r * STEPS + m + 1)
                        pool.wait_ge(y_added, r * STEPS + max(m - 1, 0))
                        pool.sem_inc(pool_past, 1)
                        pool.tensor_tensor(hC[:, m % 2, :], hs[:, m % 2, :], C_flat[:, ds((r + 2 * (m // NG)) * T, T)],
                                           ALU.mult).then_inc(weighted, 1)

            @block.vector
            def _(v):
                gn.vector(v, xT, xn, ps[0:CH, 7, :], lambda e, i: e.wait_ge(loaded_x, 48))
                v.wait_ge(loaded_w, 48)
                v.wait_ge(padded, 4)
                for n in range(9):
                    tap = pad[:, n // 3:n // 3 + OR, n % 3:n % 3 + HW]
                    if n == 0:
                        v.tensor_scalar(conv[:, :, :], tap, cw[:, 0:1], None, ALU.mult).then_inc(convd, 1)
                    else:
                        v.wait_ge(convd, n)
                        v.scalar_tensor_tensor(conv[:, :, :], tap, cw[:, n:n + 1], conv[:, :, :],
                                               ALU.mult, ALU.add).then_inc(convd, 1)
                v.wait_ge(activated, NB)
                v.tensor_copy(xc[:, 1, :].rearrange("p (b w h) -> p b h w", b=NB, w=HW),
                              xc[:, 0, :].rearrange("p (b h w) -> p b h w", b=NB, h=HW)).then_inc(ordered, 1)
                v.wait_ge(loaded_s, 16 * (8 + NT))
                v.tensor_reduce(Dsum[:, :], Dk[:, :], AX.X, ALU.add).then_inc(ordered, 1)
                v.wait_ge(A_done, 1)
                v.tensor_scalar(Am[:, :], Am[:, :], -1.0, None, ALU.mult).then_inc(ordered, 1)
                v.wait_ge(ordered, 3)
                n = 0
                for k in range(KD):
                    v.wait_ge(sp_act, 3 * k + 2)
                    v.tensor_scalar(sp[:, 2, :], sp[:, 1, :], 1.0, None, ALU.add).then_inc(sp_vec, 1)
                    v.wait_ge(sp_vec, n + 1)
                    v.tensor_scalar(sp[:, 0, :], sp[:, 2, :], -1.0, 1e-30, ALU.add, ALU.add).then_inc(sp_vec, 1)
                    v.wait_ge(sp_vec, n + 2)
                    v.reciprocal(sp[:, 0, :], sp[:, 0, :]).then_inc(sp_vec, 1)
                    v.wait_ge(sp_vec, n + 3)
                    v.tensor_tensor(sp[:, 1, :], sp[:, 1, :], sp[:, 0, :], ALU.mult).then_inc(sp_vec, 1)
                    v.wait_ge(sp_vec, n + 4)
                    v.wait_ge(dt_full, k + 1)
                    v.tensor_scalar(sp[:, 0, :], ps[0:DI, 2:4, :].rearrange("p a b -> p (a b)"), dtb[:, k:k + 1], 0.0,
                                    ALU.add, ALU.max).then_inc(sp_vec, 1)
                    v.wait_ge(sp_act, 3 * k + 3)
                    v.wait_ge(sp_vec, n + 5)
                    v.scalar_tensor_tensor(sp[:, 3, :], sp[:, 3, :], 1e-30, sp[:, 1, :], ALU.add, ALU.mult).then_inc(sp_vec, 1)
                    v.wait_ge(sp_vec, n + 6)
                    v.tensor_tensor(d_all[:, k, :], sp[:, 3, :], sp[:, 0, :], ALU.add).then_inc(sp_vec, 1)
                    v.wait_ge(sp_vec, n + 7)
                    v.tensor_tensor(du_all[:, k, :], d_all[:, k, :], xc[:, k % 2, :], ALU.mult).then_inc(du_done, 1)
                    n += 7
                v.wait_ge(bc_sb, 4 * KD)
                with v.Fori(0, 2) as r:
                    for m in range(STEPS):
                        for half in range(NHALF):
                            u = NHALF * m + half
                            v.wait_ge(du_bc, r * NHALF * STEPS + u + 1)
                            v.tensor_tensor(dBu[:, m % 2, half * BANK:(half + 1) * BANK], ps[:, 3 + u % 3, :],
                                            B_flat[:, ds((r + 2 * (m // NG)) * T + half * BANK, BANK)],
                                            ALU.mult).then_inc(dBu_done, 1)
                        v.wait_ge(dBu_done, (r * STEPS + m + 1) * NHALF)
                        v.wait_ge(dA_done, (r * STEPS + m + 1) * NHALF)
                        v.wait_ge(weighted, r * STEPS + max(m - 1, 0))
                        step = 1 if m < NG else -1
                        v.tensor_tensor_scan(hs[:, m % 2, ::step], dA[:, m // NG, m % 2, ::step],
                                             dBu[:, m % 2, ::step], 0.0, ALU.mult, ALU.add).then_inc(scanned, 1)
                v.wait_ge(y_out, 4)
                v.scalar_tensor_tensor(sp[:, 0, :], xc[:, 0, :], Dsum[:, 0:1], ysum[:, 0, :], ALU.mult, ALU.add).then_inc(fin, 1)
                v.wait_ge(fin, 1)
                v.tensor_tensor(sp[:, 1, :].rearrange("p (b h w) -> p b h w", b=NB, h=HW),
                                sp[:, 0, :].rearrange("p (b h w) -> p b h w", b=NB, h=HW),
                                ysum[:, 1, :].rearrange("p (b w h) -> p b h w", b=NB, w=HW), ALU.add).then_inc(fin, 1)
                v.wait_ge(fin_ps, 2)
                v.tensor_tensor(sp[:, 0, :], sp[:, 1, :], ps[0:DI, 0:2, :].rearrange("p a b -> p (a b)"),
                                ALU.subtract).then_inc(fin, 1)
                v.wait_ge(fin_ps, 4)
                v.tensor_scalar(sp[:, 2, :], ps[0:DI, 2:4, :].rearrange("p a b -> p (a b)"), 1e-5, None, ALU.add).then_inc(fin, 1)
                v.wait_ge(fin_act, 2)
                v.reciprocal(sp[:, 3, :], sp[:, 3, :]).then_inc(fin, 1)
                v.wait_ge(fin, 5)
                v.tensor_tensor(sp[:, 0, :], sp[:, 0, :], sp[:, 3, :], ALU.mult).then_inc(fin, 1)
                v.wait_ge(fin, 6)
                v.tensor_scalar(sp[:, 1, :], sp[:, 0, :], gamma[:, 0:1], beta[:, 0:1], ALU.mult, ALU.add).then_inc(fin, 1)
                v.wait_ge(fin, 7)
                v.tensor_tensor(sp[:, 2, :], sp[:, 1, :], zs[:, :], ALU.mult).then_inc(fin, 1)
                for q in range(NT // 2):
                    v.wait_ge(res_ps, q + 1)
                    v.tensor_tensor(X[:, 2 * q:2 * q + 2, :], X[:, 2 * q:2 * q + 2, :],
                                    ps[:, 4 + q, 0:2 * C].rearrange("p (a c) -> p a c", a=2), ALU.add).then_inc(res, 1)

            @block.scalar
            def _(act):
                gn.scalar(act)
                act.wait_ge(cleared, 1)
                rows = pad[:, 1:1 + OR, 1:1 + HW].rearrange("p (b r) w -> p b r w", b=NB)
                for half in range(NHALF):
                    act.wait_ge(proj, half + 1)
                    for b in range(2):
                        act.activation(rows[:, 2 * half + b, 0:HW, :],
                                       ps[0:DI, half, b * L:(b + 1) * L].rearrange("p (h w) -> p h w", h=HW),
                                       ACT.Copy).then_inc(padded, 1)
                act.wait_ge(proj, 4)
                for half in range(NHALF):
                    act.activation(zs[:, half * BANK:(half + 1) * BANK], ps[0:DI, 2 + half, :], ACT.Silu).then_inc(padded, 1)
                act.wait_ge(convd, 9)
                cr = conv[:, :, :].rearrange("p (b r) w -> p b r w", b=NB)
                for b in range(NB):
                    act.activation(xc[:, 0, b * L:(b + 1) * L].rearrange("p (h w) -> p h w", h=HW),
                                   cr[:, b, 0:HW, :], ACT.Silu, bias=cb[:, 0:1]).then_inc(activated, 1)
                act.wait_ge(loaded_s, 16 * (8 + NT))
                act.activation(Am[:, :], Alog[:, :], ACT.Exp).then_inc(A_done, 1)
                for k in range(KD):
                    act.wait_ge(dt_low, k + 1)
                    act.activation(dtr[:, :], ps[0:RK, 0:2, :].rearrange("p a b -> p (a b)"), ACT.Copy).then_inc(dt_low_sb, 1)
                    for j in range(2):
                        act.wait_ge(bc_ps, 4 * k + 2 * j + 2)
                        for half in range(NHALF):
                            act.activation((Bb, Cb)[j][:, k, half * BANK:(half + 1) * BANK],
                                           ps[:, 4 + 2 * j + half, :], ACT.Copy).then_inc(bc_sb, 1)
                    act.wait_ge(dt_full, k + 1)
                    if k >= 1:
                        act.wait_ge(du_done, k)
                    act.activation(sp[:, 0, :], ps[0:DI, 2:4, :].rearrange("p a b -> p (a b)"), ACT.Abs,
                                   bias=dtb[:, k:k + 1]).then_inc(sp_act, 1)
                    act.wait_ge(sp_act, 3 * k + 1)
                    act.activation(sp[:, 1, :], sp[:, 0, :], ACT.Exp, scale=-1.0).then_inc(sp_act, 1)
                    act.wait_ge(sp_vec, 7 * k + 1)
                    act.activation(sp[:, 3, :], sp[:, 2, :], ACT.Ln).then_inc(sp_act, 1)
                act.wait_ge(ordered, 3)
                act.wait_ge(cleared, 2)
                with act.Fori(0, 2) as r:
                    for m in range(STEPS):
                        for half in range(NHALF):
                            u = NHALF * m + half
                            act.wait_ge(d_bc, r * NHALF * STEPS + u + 1)
                            act.wait_ge(scanned, r * STEPS + max(m - 1, 0))
                            act.sem_inc(act_past, 1)
                            o = 1 if m < NG else 0
                            dst = dA[:, m // NG, m % 2, half * BANK:(half + 1) * BANK].rearrange("p (b t) -> p b t", t=L)
                            src = ps[:, u % 3, :].rearrange("p (b t) -> p b t", t=L)
                            act.activation(dst[:, :, o:o + L - 1], src[:, :, o:o + L - 1], ACT.Exp,
                                           scale=Am[:, ds((r + 2 * (m // NG)) * NG + m % NG, 1)]).then_inc(dA_done, 1)
                    act.wait_ge(y_added, (r + 1) * STEPS)
                    for half in range(NHALF):
                        act.sem_inc(act_past, 1)
                        act.activation(y_flat[:, ds(r * T + half * BANK, BANK)], ps[0:DI, 6 + half, :],
                                       ACT.Copy).then_inc(y_out, 1)
                act.wait_ge(fin, 3)
                act.activation(sp[:, 2, :], sp[:, 0, :], ACT.Square).then_inc(fin_act, 1)
                act.wait_ge(fin, 4)
                act.activation(sp[:, 3, :], sp[:, 2, :], ACT.Sqrt).then_inc(fin_act, 1)

            @block.tensor
            def _(pe):
                gn.tensor(pe, group, ps[0:CH, 7, :])
                pe.wait_ge(loaded_w, 48)
                pe.wait_ge(gn.out, 8)
                for o in range(2):
                    for half in range(NHALF):
                        for h in range(2):
                            mm = pe.matmul(ps[0:DI, 2 * o + half, :], w_in[:, h, o * DI:(o + 1) * DI],
                                           xn[:, h, half * BANK:(half + 1) * BANK], start=(h == 0), stop=(h == 1))
                        mm.then_inc(proj, 1)
                pe.wait_ge(loaded_p, 80)
                pe.wait_ge(activated, NB)
                pe.wait_ge(padded, 6)
                pe.wait_ge(ordered, 1)
                for k in range(KD):
                    rhs = lambda half: xc[:, k % 2, half * BANK:(half + 1) * BANK]
                    if k >= 1:
                        pe.wait_ge(dt_low_sb, k)
                    for half in range(NHALF):
                        mm = pe.matmul(ps[0:RK, half, :], wdt[:, k, :], rhs(half), start=True, stop=True)
                    mm.then_inc(dt_low, 1)
                    for j, w in ((0, wB), (1, wC)):
                        if k >= 1:
                            pe.wait_ge(bc_sb, 4 * (k - 1) + 2 * j + 2)
                        for half in range(NHALF):
                            pe.matmul(ps[:, 4 + 2 * j + half, :], w[:, k, :], rhs(half), start=True, stop=True).then_inc(bc_ps, 1)
                    pe.wait_ge(dt_low_sb, k + 1)
                    if k >= 1:
                        pe.wait_ge(sp_act, 3 * k)
                        pe.wait_ge(sp_vec, 7 * k)
                    for half in range(NHALF):
                        mm = pe.matmul(ps[0:DI, 2 + half, :], dtw[:, k, :], dtr[:, half * BANK:(half + 1) * BANK],
                                       start=True, stop=True)
                    mm.then_inc(dt_full, 1)
                pe.wait_ge(bc_sb, 4 * KD)
                pe.wait_ge(du_done, KD)
                pe.wait_ge(loaded_s, 16 * (8 + NT))

                def spread(r, m):
                    for half in range(NHALF):
                        u = NHALF * m + half
                        at = ds((r + 2 * (m // NG)) * T + half * BANK, BANK)
                        pe.wait_ge(dA_done, r * NHALF * STEPS + max(u - 2, 0))
                        pe.matmul(ps[:, u % 3, :], sel[:, m % NG, :], d_flat[:, at], start=True, stop=True).then_inc(d_bc, 1)
                        pe.wait_ge(dBu_done, r * NHALF * STEPS + max(u - 2, 0))
                        pe.matmul(ps[:, 3 + u % 3, :], sel[:, m % NG, :], du_flat[:, at], start=True, stop=True).then_inc(du_bc, 1)

                def add(r, m):
                    pe.wait_ge(weighted, r * STEPS + m + 1)
                    for half in range(NHALF):
                        mm = pe.matmul(ps[0:DI, 6 + half, :], selT[:, m % NG, :], hC[:, m % 2, half * BANK:(half + 1) * BANK],
                                       start=(m == 0), stop=(m == STEPS - 1))
                    mm.then_inc(y_added, 1)

                with pe.Fori(0, 2) as r:
                    for m in range(STEPS):
                        spread(r, m)
                        if m == 2:
                            pe.wait_ge(y_out, r * 2)
                        if m >= 2:
                            add(r, m - 2)
                    add(r, STEPS - 2)
                    add(r, STEPS - 1)
                pe.wait_ge(fin, 2)
                pe.wait_ge(dA_done, 2 * 2 * NG * NHALF)
                for half in range(NHALF):
                    pe.matmul(ps[0:DI, half, :], avg[:, :], sp[:, 1, half * BANK:(half + 1) * BANK], start=True, stop=True).then_inc(fin_ps, 1)
                pe.wait_ge(fin_act, 1)
                pe.wait_ge(dBu_done, 2 * 2 * NG * NHALF)
                for half in range(NHALF):
                    pe.matmul(ps[0:DI, 2 + half, :], avg[:, :], sp[:, 2, half * BANK:(half + 1) * BANK], start=True, stop=True).then_inc(fin_ps, 1)
                pe.wait_ge(fin, 8)
                pe.wait_ge(y_out, 4)
                for t in range(NT):
                    mm = pe.matmul(ps[:, 4 + t // 2, (t % 2) * C:(t % 2 + 1) * C], sp[:, 2, t * P:(t + 1) * P], w_out[:, :],
                                   start=True, stop=True)
                    if t % 2:
                        mm.then_inc(res_ps, 1)
        ctx.clear()


NH = 12
HE = 16
HG = 4
HK = 7
QT = L // P


def neighbour_layer(nc, K, X, D):
    with ExitStack() as stack:
        ctx = Ctx(nc, stack)
        xT = ctx.sb("n_xT", [CH, 2, T])
        xn = ctx.sb("n_xn", [CH, 2, T])
        group = ctx.sb("n_group", [CH, CH])
        xb = ctx.sb("n_xb", [CH, 2, L])
        wqk = ctx.sb("n_wqk", [CH, 2, 6, P])
        wv = ctx.sb("n_wv", [CH, 2, C])
        wo = ctx.sb("n_wo", [CH, 2, C])
        maskf = ctx.sb("n_maskf", [P, QT, L])
        mask = ctx.sb("n_mask", [P, QT, L], BF16)
        qk = ctx.sb("n_qk", [P, 6, L])
        vt = ctx.sb("n_v", [P, QT, C])
        nm = ctx.sb("n_nm", [P, NH, QT])
        sums = ctx.sb("n_sums", [P, QT, NH])
        rs = ctx.sb("n_rs", [P, QT, NH])
        Pr = ctx.sb("n_P", [P, 2, QT, L])
        PT = ctx.sb("n_PT", [P, 2, QT, L])
        On = ctx.sb("n_On", [P, QT, C])
        OT = ctx.sb("n_OT", [CH, 2, L])
        gn = GroupNorm(ctx, "l2")
        ps = ctx.ps("ps_l2", [P, 8, BANK])
        S = lambda n: ctx.sem(f"l2_{n}")
        loaded, masked, x_turned, x_sb, taken, past = (
            S("loaded"), S("masked"), S("x_turned"), S("x_sb"), S("taken"), S("past"))
        proj, evac, scores, peak, expd, turned, turned_sb, summed, norm, added = (
            S("proj"), S("evac"), S("scores"), S("peak"), S("expd"), S("turned"), S("turned_sb"), S("summed"), S("norm"),
            S("added"))
        xn_flat = xn[:, :, :]
        X_flat = X[:, :, :].rearrange("p t c -> p (t c)")
        EV = 6
        PJ = 6

        with nc.Block() as block:
            @block.sync
            def _(sync):
                for dst, src in ((group, "group"), (wqk, "n_wqk"), (wv, "n_wv"), (wo, "n_wo"), (maskf, "n_mask")):
                    sync.dma_start(dst[:], D[src]).then_inc(loaded, 16)

            @block.gpsimd
            def _(pool):
                pool.wait_ge(loaded, 80)
                pool.tensor_copy(mask[:], maskf[:]).then_inc(masked, 1)
                with pool.Fori(0, NB) as b:
                    pool.wait_ge(gn.out, 8)
                    pool.wait_ge(proj, b * PJ)
                    pool.sem_inc(past, 1)
                    pool.tensor_copy(xb[:, :, :], xn_flat[:, :, ds(b * L, L)]).then_inc(taken, 1)

            @block.vector
            def _(v):
                gn.vector(v, xT, xn, ps[0:CH, 7, :], lambda e, i: e.wait_ge(x_sb, 2 * NHALF))
                with v.Fori(0, NB) as b:
                    v.wait_ge(expd, b * NH * QT)

                    def copy_turned(h):
                        v.wait_ge(turned, b * NH + h + 1)
                        v.wait_ge(summed, b * NH + max(h - 1, 0))
                        v.tensor_copy(PT[:, h % 2, :, :], ps[:, 3 + h % 2, :].rearrange("p (k q) -> p k q", k=QT)).then_inc(turned_sb, 1)

                    for s in range(NH + 2):
                        if s < NH:
                            v.wait_ge(scores, b * NH + s + 1)
                            v.tensor_reduce(nm[:, s, :], ps[:, s % 3, :].rearrange("p (q k) -> p q k", q=QT), AX.X, ALU.max,
                                            negate=True).then_inc(peak, 1)
                        if s >= 2:
                            copy_turned(s - 2)
                    v.wait_ge(expd, (b + 1) * NH * QT)
                    v.reciprocal(rs[:], sums[:]).then_inc(norm, 1)
                    v.wait_ge(norm, 2 * b + 1)
                    v.wait_ge(summed, (b + 1) * NH)
                    v.tensor_tensor(On[:, :, :].rearrange("p q (h e) -> p (q h) e", e=HE),
                                    ps[:, 5, 0:QT * C].rearrange("p (n e) -> p n e", e=HE),
                                    rs[:, :, :].rearrange("p q h -> p (q h)").unsqueeze(2).broadcast_to([P, QT * NH, HE]),
                                    ALU.mult).then_inc(norm, 1)
                    v.wait_ge(proj, (b + 1) * PJ)
                    v.tensor_tensor(X_flat[:, ds(b * QT * C, QT * C)], X_flat[:, ds(b * QT * C, QT * C)],
                                    ps[:, 7, 0:QT * C], ALU.add).then_inc(added, 1)

            @block.scalar
            def _(act):
                for n in range(2 * NHALF):
                    act.wait_ge(x_turned, n + 1)
                    act.activation(xT[:, n % 2, (n // 2) * BANK:(n // 2 + 1) * BANK], ps[0:CH, n, :], ACT.Copy).then_inc(x_sb, 1)
                gn.scalar(act)
                two = lambda n: ps[:, 6 + n % 2, :].rearrange("p (a t) -> p a t", a=2)
                with act.Fori(0, NB) as b:
                    act.wait_ge(scores, b * NH)
                    act.wait_ge(proj, b * PJ + 1)
                    act.activation(qk[:, 0:2, :], two(0), ACT.Copy, scale=HE ** -0.5).then_inc(evac, 1)
                    act.wait_ge(proj, b * PJ + 2)
                    act.activation(qk[:, 2, :], two(1)[:, 0, :], ACT.Copy, scale=HE ** -0.5).then_inc(evac, 1)
                    act.activation(qk[:, 3, :], two(1)[:, 1, :], ACT.Copy).then_inc(evac, 1)
                    act.wait_ge(proj, b * PJ + 3)
                    act.activation(qk[:, 4:6, :], two(2), ACT.Copy).then_inc(evac, 1)
                    act.wait_ge(summed, b * NH)
                    act.wait_ge(proj, b * PJ + 4)
                    act.activation(vt[:, :, :], ps[:, 7, 0:QT * C].rearrange("p (q c) -> p q c", q=QT), ACT.Copy).then_inc(evac, 1)
                    act.wait_ge(norm, 2 * b)
                    for s in range(NH):
                        act.wait_ge(peak, b * NH + s + 1)
                        act.wait_ge(turned, b * NH + max(s - 1, 0))
                        for q in range(QT):
                            act.activation(Pr[:, s % 2, q, :], ps[:, s % 3, q * L:(q + 1) * L], ACT.Exp,
                                           bias=nm[:, s, q:q + 1], accum_out=sums[:, q, s:s + 1]).then_inc(expd, 1)
                    act.wait_ge(proj, b * PJ + 5)
                    act.activation(OT[:, :, :], ps[0:CH, 6, :].rearrange("p (c t) -> p c t", c=2), ACT.Copy).then_inc(evac, 1)

            @block.tensor
            def _(pe):
                for n in range(2 * NHALF):
                    for t in range(4):
                        mm = pe.transpose(ps[0:CH, n, t * P:(t + 1) * P],
                                          X[:, (n // 2) * 4 + t, (n % 2) * CH:(n % 2 + 1) * CH], K["ident"][:, :])
                    mm.then_inc(x_turned, 1)
                pe.wait_ge(loaded, 80)
                gn.tensor(pe, group, ps[0:CH, 7, :])
                pe.wait_ge(masked, 1)
                pe.wait_ge(gn.var, 1)
                with pe.Fori(0, NB) as b:
                    pe.wait_ge(taken, b + 1)
                    pe.wait_ge(added, b)
                    for n in range(3):
                        if n == 2:
                            pe.wait_ge(evac, b * EV + 1)
                        for o in range(2):
                            for c in range(2):
                                mm = pe.matmul(ps[:, 6 + n % 2, o * L:(o + 1) * L], wqk[:, c, 2 * n + o, :], xb[:, c, :],
                                               start=(c == 0), stop=(c == 1))
                        mm.then_inc(proj, 1)
                    pe.wait_ge(evac, b * EV + 3)
                    for q in range(QT):
                        for c in range(2):
                            mm = pe.matmul(ps[:, 7, q * C:(q + 1) * C], xb[:, c, q * P:(q + 1) * P], wv[:, c, :],
                                           start=(c == 0), stop=(c == 1))
                    mm.then_inc(proj, 1)
                    pe.wait_ge(evac, b * EV + 4)

                    def score(h):
                        pe.wait_ge(expd, (b * NH + max(h - 2, 0)) * QT)
                        at = slice(32 * (h % HG), 32 * (h % HG) + HE)
                        for q in range(QT):
                            out = ps[:, h % 3, q * L:(q + 1) * L]
                            pe.matmul(out, K["identb"][:, :], mask[:, q, :], start=True, stop=False)
                            mm = pe.matmul(out, qk[at, h // HG, q * P:(q + 1) * P], qk[at, 3 + h // HG, :], start=False, stop=True)
                        mm.then_inc(scores, 1)

                    def turn(h):
                        pe.wait_ge(expd, (b * NH + h + 1) * QT)
                        pe.wait_ge(turned_sb, b * NH + max(h - 1, 0))
                        for k in range(QT):
                            for q in range(QT):
                                mm = pe.transpose(ps[:, 3 + h % 2, k * L + q * P:k * L + (q + 1) * P],
                                                  Pr[:, h % 2, q, k * P:(k + 1) * P], K["ident"][:, :])
                        mm.then_inc(turned, 1)

                    def output(h):
                        pe.wait_ge(turned_sb, b * NH + h + 1)
                        if h == 0:
                            pe.wait_ge(evac, b * EV + 5)
                            pe.wait_ge(norm, 2 * b)
                        for q in range(QT):
                            for k in range(QT):
                                mm = pe.matmul(ps[:, 5, q * C + h * HE:q * C + (h + 1) * HE], PT[:, h % 2, k, q * P:(q + 1) * P],
                                               vt[:, k, h * HE:(h + 1) * HE], start=(k == 0), stop=(k == QT - 1))
                        mm.then_inc(summed, 1)

                    for s in range(NH + 3):
                        if s < NH:
                            score(s)
                        if 2 <= s < NH + 2:
                            turn(s - 2)
                        if s >= 3:
                            output(s - 3)
                    pe.wait_ge(norm, 2 * b + 2)
                    for c in range(2):
                        for q in range(QT):
                            mm = pe.transpose(ps[0:CH, 6, c * L + q * P:c * L + (q + 1) * P], On[:, q, c * CH:(c + 1) * CH],
                                              K["ident"][:, :])
                    mm.then_inc(proj, 1)
                    pe.wait_ge(evac, (b + 1) * EV)
                    for q in range(QT):
                        for c in range(2):
                            mm = pe.matmul(ps[:, 7, q * C:(q + 1) * C], OT[:, c, q * P:(q + 1) * P], wo[:, c, :],
                                           start=(c == 0), stop=(c == 1))
                    mm.then_inc(proj, 1)


FF = 4 * C
FT = FF // P
EXP_N = 30
(S_N1, S_WQKV, S_QKV, S_ATTN, S_WPROJ, S_SV, S_R1, S_N2, S_WFC1, S_ACT, S_WFC2, S_M2, S_R2) = range(13)
(K_QKV, K_ATTN, K_X0, K_BI, K_CI, K_INV, K_QB, K_CLAMP, K_NX0, K_PROJ, K_FC1, K_FC2, K_T0, K_T1) = range(14)


def quantised_layer(nc, K, X, D, ln):
    with ExitStack() as stack:
        ctx = Ctx(nc, stack)
        U = ctx.sb("q_U", [P, NT, C])
        N = ctx.sb("q_N", [P, NT, C])
        Ni = ctx.sb("q_Ni", [P, NT, C], BF16)
        nT = ctx.sb("q_nT", [CH, 2, T], BF16)
        nb = ctx.sb("q_nb", [CH, 2, L], BF16)
        sc = ctx.sb("q_sc", [P, 13])
        rc = ctx.sb("q_rc", [P, 13])
        kf = ctx.sb("q_kf", [P, 14])
        rows = ctx.sb("q_rows", [P, 7, C])
        bqk = ctx.sb("q_bqk", [P, 6])
        b1 = ctx.sb("q_b1", [P, FT])
        wqk_f = ctx.sb("q_wqk_f", [CH, 2 * 6 * P])
        wqk = ctx.sb("q_wqk", [CH, 2 * 6 * P], BF16)
        wv_f = ctx.sb("q_wv_f", [CH, 2 * C])
        wv = ctx.sb("q_wv", [CH, 2 * C], BF16)
        wp_f = ctx.sb("q_wp_f", [CH, 2 * C])
        w1_f = ctx.sb("q_w1_f", [CH, 2 * FF])
        w1 = ctx.sb("q_w1", [CH, 2 * FF], BF16)
        w2_f = ctx.sb("q_w2_f", [P, FT * C])
        w2 = ctx.sb("q_w2", [P, FT * C], BF16)
        qf = ctx.sb("q_qf", [P, 6 * L])
        qk = ctx.sb("q_qk", [P, 6, L], BF16)
        vf = ctx.sb("q_vf", [P, QT, C])
        vi = ctx.sb("q_vi", [P, QT, C], BF16)
        t1 = ctx.sb("q_t1", [P, QT * L])
        t2 = ctx.sb("q_t2", [P, QT, L])
        nm = ctx.sb("q_nm", [P, QT])
        xi = ctx.sb("q_xi", [P, 2, QT, L], BF16)
        qv = ctx.sb("q_qv", [P, 2, QT * L])
        qi = ctx.sb("q_qi", [P, QT * L], BF16)
        ri = ctx.sb("q_ri", [P, 2, QT * L], BF16)
        e2 = ctx.sb("q_e2", [P, 2, QT, L], I16)
        zz = ctx.sb("q_zz", [P, 2, QT, L])
        ex = ctx.sb("q_ex", [P, NH, QT, L])
        sums = ctx.sb("q_sums", [P, NH, QT])
        f0 = ctx.sb("q_f0", [P, NH * QT])
        f1 = ctx.sb("q_f1", [P, NH * QT])
        fac = ctx.sb("q_fac", [P, NH, QT])
        pv = ctx.sb("q_pv", [P, 2, QT * L])
        pr = ctx.sb("q_pr", [P, 2, QT * L])
        pg = ctx.sb("q_pg", [P, 2, QT * L])
        pi = ctx.sb("q_pi", [P, 2, QT, L], BF16)
        PT = ctx.sb("q_PT", [P, 2, QT, L], BF16)
        Os = ctx.sb("q_Os", [P, QT, C])
        OT = ctx.sb("q_OT", [CH, 2, L])
        pj = ctx.sb("q_pj", [P, NT * C])
        hf = ctx.sb("q_hf", [P, 2, T])
        hi = ctx.sb("q_hi", [P, FT, T], BF16)
        ps = ctx.ps("ps_l3", [P, 8, BANK])
        S = lambda n: ctx.sem(f"l3_{n}")
        loaded, w_loaded, vec, pool_steps, quantised, first_ln = (
            S("loaded"), S("w_loaded"), S("vec"), S("pool_steps"), S("quantised"), S("first_ln"))
        scaled, normed, turned_n, n_sb, taken = S("scaled"), S("normed"), S("turned_n"), S("n_sb"), S("taken")
        past, act_past = S("past"), S("act_past")
        proj, evac, qk_ready, v_ready, scores, score_read = (
            S("proj"), S("evac"), S("qk_ready"), S("v_ready"), S("scores"), S("score_read"))
        diff, quot, rest, square, expd, factor, prob, rounded, floored, turned, turned_sb, summed = (
            S("diff"), S("quot"), S("rest"), S("square"), S("expd"), S("factor"), S("prob"), S("rounded"), S("floored"),
            S("turned"), S("turned_sb"), S("summed"))
        excess, resid, up, gelu, hq, down, down_read = S("excess"), S("resid"), S("up"), S("gelu"), S("hq"), S("down"), S("down_read")
        identb = K["identb"]
        flat = lambda a: a[:, :, :].rearrange("p a b -> p (a b)")
        VEC_LOOP = 3 + NH * 4 + 5
        EV = 9

        with nc.Block() as block:
            @block.sync
            def _(sync):
                for dst, src in ((sc, "q_scales"), (rows, "q_rows"), (bqk, "q_bqk"), (b1, "q_b1")):
                    sync.dma_start(dst[:], D[src].partition_broadcast(P) if src in ("q_scales", "q_rows") else D[src]).then_inc(loaded, 16)
                for dst, src in ((wqk_f, "q_wqk"), (wv_f, "q_wv"), (wp_f, "q_wp"), (w1_f, "q_w1"), (w2_f, "q_w2")):
                    sync.dma_start(dst[:], D[src]).then_inc(w_loaded, 16)

            @block.gpsimd
            def _(pool):
                step = Chain(pool, pool_steps)
                pool.wait_ge(scaled, 1)
                pool.wait_ge(w_loaded, 80)
                for f, i, r in ((wqk_f, wqk, S_WQKV), (wv_f, wv, S_WQKV), (wp_f, wp_f, S_WPROJ), (w1_f, w1, S_WFC1),
                                (w2_f, w2, S_WFC2)):
                    n = f.shape[0]
                    step(pool.tensor_scalar(f[:], f[:], rc[0:n, r:r + 1], 127.0, ALU.mult, ALU.min))
                    step(pool.tensor_scalar(f[:], f[:], -128.0, MAGIC, ALU.max, ALU.add))
                    pool.tensor_scalar(i[:], f[:], -MAGIC, None, ALU.add).then_inc(quantised, 1)
                with pool.Fori(0, NB) as b:
                    pool.wait_ge(n_sb, 2)
                    pool.wait_ge(proj, b * 6 + 0)
                    pool.sem_inc(past, 1)
                    pool.tensor_copy(nb[:, :, :], nT[:, :, ds(b * L, L)]).then_inc(taken, 1)
                    for h in range(NH):
                        pool.wait_ge(rounded, b * NH + h + 1)
                        pool.wait_ge(floored, b * NH + max(h - 1, 0))
                        pool.tensor_tensor(pg[:, h % 2, :], pr[:, h % 2, :], pv[:, h % 2, :], ALU.subtract).then_inc(excess, 1)

            @block.vector
            def _(v):
                step = Chain(v, vec)

                def clip_round(dst, src, signal):
                    step(v.tensor_scalar(src, src, 127.0, -128.0, ALU.min, ALU.max))
                    return v.tensor_scalar(dst, src, MAGIC, -MAGIC, ALU.add, ALU.add).then_inc(signal, 1)

                def floor_of(col):
                    c = kf[:, col:col + 1]
                    step(v.tensor_scalar(kf[:, K_T0:K_T0 + 1], c, MAGIC, -MAGIC, ALU.add, ALU.add))
                    step(v.tensor_tensor(kf[:, K_T1:K_T1 + 1], kf[:, K_T0:K_T0 + 1], c, ALU.is_gt))
                    step(v.tensor_tensor(c, kf[:, K_T0:K_T0 + 1], kf[:, K_T1:K_T1 + 1], ALU.subtract))

                k = lambda i: kf[:, i:i + 1]
                s = lambda i: sc[:, i:i + 1]
                r = lambda i: rc[:, i:i + 1]
                v.wait_ge(loaded, 64)
                v.reciprocal(rc[:], sc[:]).then_inc(scaled, 1)
                v.wait_ge(scaled, 1)
                for dst, a, m in ((K_QKV, S_N1, s(S_WQKV)), (K_ATTN, S_QKV, s(S_QKV)), (K_PROJ, S_QKV, s(S_WPROJ)),
                                  (K_FC1, S_N2, s(S_WFC1)), (K_FC2, S_ACT, s(S_WFC2))):
                    step(v.tensor_tensor(k(dst), s(a), m, ALU.mult))
                step(v.tensor_tensor(k(K_QKV), k(K_QKV), r(S_QKV), ALU.mult))
                step(v.tensor_scalar(k(K_ATTN), k(K_ATTN), r(S_ATTN), HE ** -0.5, ALU.mult, ALU.mult))
                step(v.tensor_scalar(k(K_PROJ), k(K_PROJ), r(S_SV), -1 / 128, ALU.mult, ALU.mult))
                step(v.tensor_scalar(k(K_FC2), k(K_FC2), r(S_M2), None, ALU.mult))
                step(v.tensor_scalar(k(K_X0), r(S_ATTN), -0.6931, None, ALU.mult))
                step(v.tensor_scalar(k(K_BI), r(S_ATTN), 1.353, None, ALU.mult))
                step(v.tensor_scalar(k(K_CI), r(S_ATTN), r(S_ATTN), 0.344 / 0.3585, ALU.mult, ALU.mult))
                for c in (K_X0, K_BI, K_CI):
                    floor_of(c)
                step(v.reciprocal(k(K_INV), k(K_X0)))
                step(v.tensor_scalar(k(K_QB), k(K_INV), -0.5, -0.5, ALU.mult, ALU.add))
                step(v.tensor_scalar(k(K_CLAMP), k(K_X0), float(EXP_N), None, ALU.mult))
                step(v.tensor_scalar(k(K_NX0), k(K_X0), -1.0, None, ALU.mult))
                step(v.tensor_scalar(bqk[:], bqk[:], r(S_QKV), None, ALU.mult))
                for row, unit in ((4, S_QKV), (5, S_SV), (6, S_M2)):
                    step(v.tensor_scalar(rows[:, row, :], rows[:, row, :], r(unit), None, ALU.mult))

                def row(i):
                    return rows[:, i, :].unsqueeze(1).broadcast_to([P, NT, C])

                ln.vector(v, 0, X, U, 1e-5)

                def normed_ints(use, g, beta, unit):
                    v.wait_ge(ln.out, NT * use)
                    ln.vector(v, use, U, N, 1e-6)
                    v.wait_ge(ln.out, NT * (use + 1))
                    step(v.tensor_tensor(N[:], N[:], row(g), ALU.mult))
                    step(v.tensor_tensor(N[:], N[:], row(beta), ALU.add))
                    step(v.tensor_scalar(N[:], N[:], r(unit), None, ALU.mult))
                    clip_round(Ni[:], N[:], normed)

                normed_ints(1, 0, 1, S_N1)

                with v.Fori(0, NB) as b:
                    step.loop(b, VEC_LOOP)
                    v.wait_ge(evac, b * EV + 6)
                    v.wait_ge(scores, b * NH)
                    clip_round(flat(qk), qf[:, :], qk_ready)
                    v.wait_ge(proj, b * 6 + 4)
                    v.wait_ge(summed, b * NH)
                    step(v.scalar_tensor_tensor(vf[:], ps[:, 4, 0:QT * C].rearrange("p (q c) -> p q c", q=QT), k(K_QKV),
                                                rows[:, 4, :].unsqueeze(1).broadcast_to([P, QT, C]), ALU.mult, ALU.add))
                    clip_round(vi[:], vf[:], v_ready)
                    v.wait_ge(v_ready, b + 1)
                    v.wait_ge(qk_ready, b + 1)

                    def differences(h):
                        v.wait_ge(scores, b * NH + h + 1)
                        step(v.tensor_scalar(t1[:, :], ps[:, h % 2, :], k(K_ATTN), 127.0, ALU.mult, ALU.min))
                        v.tensor_scalar(t2[:, :, :].rearrange("p q k -> p (q k)"), t1[:, :], -128.0, MAGIC, ALU.max,
                                        ALU.add).then_inc(score_read, 1)
                        v.wait_ge(score_read, b * NH + h + 1)
                        step(v.tensor_reduce(nm[:, :], t2[:, :, :], AX.X, ALU.max, negate=True))
                        for q in range(QT):
                            v.tensor_scalar(xi[:, h % 2, q, :], t2[:, q, :], nm[:, q:q + 1], k(K_CLAMP), ALU.add, ALU.max).then_inc(diff, 1)
                        v.wait_ge(diff, (b * NH + h + 1) * QT)

                    def remainders(h):
                        v.wait_ge(quot, b * NH + h + 1)
                        step(v.tensor_scalar(qi[:, :], qv[:, h % 2, :], MAGIC, -MAGIC, ALU.add, ALU.add))
                        v.scalar_tensor_tensor(ri[:, h % 2, :], qi[:, :], k(K_NX0), xi[:, h % 2, :, :].rearrange("p q k -> p (q k)"),
                                               ALU.mult, ALU.add).then_inc(rest, 1)
                        v.wait_ge(rest, b * NH + h + 1)
                        step(v.tensor_scalar(e2[:, h % 2, :, :].rearrange("p q k -> p (q k)"), qi[:, :], -128.0,
                                             float((127 + EXP_N) * 128), ALU.mult, ALU.add))

                    def exponentials(h):
                        v.wait_ge(square, b * NH + h + 1)
                        for q in range(QT):
                            v.scalar_tensor_tensor(ex[:, h, q, :], zz[:, h % 2, q, :], k(K_CI), e2[:, h % 2, q, :].bitcast(BF16),
                                                   ALU.add, ALU.mult, accum_out=sums[:, h, q:q + 1]).then_inc(expd, 1)
                        v.wait_ge(expd, (b * NH + h + 1) * QT)

                    v.wait_ge(prob, b * NH * QT)
                    for n in range(NH + 2):
                        if n < NH:
                            differences(n)
                        if 1 <= n <= NH:
                            remainders(n - 1)
                        if n >= 2:
                            exponentials(n - 2)
                    sf = sums[:, :, :].rearrange("p h q -> p (h q)")
                    step(v.reciprocal(f0[:, :], sf))
                    step(v.tensor_scalar(f0[:, :], f0[:, :], 2.0 ** 32, None, ALU.mult))
                    step(v.tensor_scalar(f1[:, :], f0[:, :], MAGIC, -MAGIC, ALU.add, ALU.add))
                    step(v.tensor_tensor(f0[:, :], f1[:, :], f0[:, :], ALU.is_gt))
                    step(v.tensor_tensor(f1[:, :], f1[:, :], f0[:, :], ALU.subtract))
                    v.tensor_scalar(fac[:, :, :].rearrange("p h q -> p (h q)"), f1[:, :], 2.0 ** -25, None, ALU.mult).then_inc(factor, 1)
                    for n in range(NH + 2):
                        if n < NH:
                            v.wait_ge(prob, (b * NH + n + 1) * QT)
                            v.wait_ge(floored, b * NH + max(n - 1, 0))
                            v.tensor_scalar(pr[:, n % 2, :], pv[:, n % 2, :], MAGIC, -MAGIC, ALU.add, ALU.add).then_inc(rounded, 1)
                        if 1 <= n <= NH:
                            h = n - 1
                            v.wait_ge(excess, b * NH + h + 1)
                            v.wait_ge(rounded, b * NH + h + 1)
                            v.wait_ge(turned, b * NH + max(h - 1, 0))
                            v.scalar_tensor_tensor(pi[:, h % 2, :, :].rearrange("p q k -> p (q k)"), pg[:, h % 2, :], 0.0,
                                                   pr[:, h % 2, :], ALU.is_gt, ALU.subtract).then_inc(floored, 1)
                        if n >= 2:
                            h = n - 2
                            v.wait_ge(turned, b * NH + h + 1)
                            v.wait_ge(summed, b * NH + max(h - 1, 0))
                            v.tensor_copy(PT[:, h % 2, :, :], ps[:, 2 + h % 2, 0:L].bitcast(BF16).rearrange("p (k q) -> p k q", k=QT)).then_inc(turned_sb, 1)
                step.end(NB)
                v.wait_ge(factor, NB)

                def requantised(src, units, unit, add_to, out_unit):
                    step(v.tensor_scalar(src, src, 127.0, -128.0, ALU.min, ALU.max))
                    step(v.tensor_scalar(src, src, MAGIC, -MAGIC, ALU.add, ALU.add))
                    step(v.scalar_tensor_tensor(src, src, s(unit), add_to, ALU.mult, ALU.add))
                    step(v.tensor_scalar(src, src, r(out_unit), 127.0, ALU.mult, ALU.min))
                    step(v.tensor_scalar(src, src, -128.0, MAGIC, ALU.max, ALU.add))
                    v.tensor_scalar(add_to, src, -MAGIC, s(out_unit), ALU.add, ALU.mult).then_inc(resid, 1)

                v.wait_ge(evac, NB * EV)
                step(v.scalar_tensor_tensor(pj[:, :].rearrange("p (t c) -> p t c", c=C), pj[:, :].rearrange("p (t c) -> p t c", c=C),
                                            k(K_PROJ), row(5), ALU.mult, ALU.add))
                requantised(pj[:, :], None, S_SV, flat(U), S_R1)
                v.wait_ge(resid, 1)
                v.wait_ge(turned_n, 2)
                normed_ints(2, 2, 3, S_N2)
                for n in range(FT * NHALF):
                    src = hf[:, n % 2, 0:BANK]
                    v.wait_ge(gelu, n + 1)
                    step(v.tensor_scalar(src, src, r(S_ACT), 127.0, ALU.mult, ALU.min))
                    step(v.tensor_scalar(src, src, -128.0, MAGIC, ALU.max, ALU.add))
                    v.tensor_scalar(hi[:, n // 2, (n % 2) * BANK:(n % 2 + 1) * BANK], src, -MAGIC, None, ALU.add).then_inc(hq, 1)
                v.wait_ge(hq, FT * NHALF)
                pj3 = pj[:, :].rearrange("p (t c) -> p t c", c=C)
                for t in range(NT):
                    v.wait_ge(down, t + 1)
                    v.scalar_tensor_tensor(pj3[:, t, :], ps[:, 4 + t % 4, 0:C], k(K_FC2), rows[:, 6, :], ALU.mult, ALU.add).then_inc(down_read, 1)
                v.wait_ge(down_read, NT)
                requantised(pj[:, :], None, S_M2, flat(U), S_R2)
                v.wait_ge(resid, 2)
                step(v.tensor_tensor(flat(X), flat(X), flat(U), ALU.add))

            @block.scalar
            def _(act):
                ln.scalar(act, 0)
                ln.scalar(act, 1)
                act.wait_ge(scaled, 1)
                act.wait_ge(normed, 1)

                def turned_input(n):
                    for c in range(2):
                        act.wait_ge(turned_n, 2 * n + c + 1)
                        act.activation(nT[:, c, :], ps[0:CH, 6 + c, :].bitcast(BF16), ACT.Copy).then_inc(n_sb, 1)

                turned_input(0)
                with act.Fori(0, NB) as b:
                    act.wait_ge(qk_ready, b)
                    for o in range(6):
                        if o % 2 == 0:
                            act.wait_ge(proj, b * 6 + o // 2 + 1)
                        act.activation(qf[:, o * L:(o + 1) * L], ps[:, 5 + o // 2, (o % 2) * L:(o % 2 + 1) * L], ACT.Identity,
                                       scale=kf[:, K_QKV:K_QKV + 1], bias=bqk[:, o:o + 1]).then_inc(evac, 1)
                    for n in range(NH + 1):
                        if n < NH:
                            act.wait_ge(diff, (b * NH + n + 1) * QT)
                            act.wait_ge(rest, b * NH + max(n - 1, 0))
                            act.activation(qv[:, n % 2, :], xi[:, n % 2, :, :].rearrange("p q k -> p (q k)"), ACT.Identity,
                                           scale=kf[:, K_INV:K_INV + 1], bias=kf[:, K_QB:K_QB + 1]).then_inc(quot, 1)
                        if n >= 1:
                            h = n - 1
                            act.wait_ge(rest, b * NH + h + 1)
                            act.wait_ge(expd, (b * NH + max(h - 1, 0)) * QT)
                            act.activation(zz[:, h % 2, :, :].rearrange("p q k -> p (q k)"), ri[:, h % 2, :], ACT.Square,
                                           bias=kf[:, K_BI:K_BI + 1]).then_inc(square, 1)
                    act.wait_ge(factor, b + 1)
                    for h in range(NH):
                        act.wait_ge(floored, b * NH + max(h - 1, 0))
                        for q in range(QT):
                            act.activation(pv[:, h % 2, q * L:(q + 1) * L], ex[:, h, q, :], ACT.Identity,
                                           scale=fac[:, h, q:q + 1]).then_inc(prob, 1)
                    act.wait_ge(summed, (b + 1) * NH)
                    act.activation(Os[:, :, :], ps[:, 4, 0:QT * C].rearrange("p (q c) -> p q c", q=QT), ACT.Copy).then_inc(evac, 1)
                    act.wait_ge(proj, b * 6 + 5)
                    act.activation(OT[:, :, :], ps[0:CH, 5, :].rearrange("p (c t) -> p c t", c=2), ACT.Copy).then_inc(evac, 1)
                    act.wait_ge(proj, b * 6 + 6)
                    act.sem_inc(act_past, 1)
                    act.activation(pj[:, ds(b * QT * C, QT * C)], ps[:, 6, 0:QT * C], ACT.Copy).then_inc(evac, 1)
                ln.scalar(act, 2)
                turned_input(1)
                for n in range(FT * NHALF):
                    act.wait_ge(up, n + 1)
                    act.wait_ge(hq, max(n - 1, 0))
                    act.activation(hf[:, n % 2, 0:BANK], ps[:, n % 4, :], ACT.Gelu, scale=kf[:, K_FC1:K_FC1 + 1],
                                   bias=b1[:, n // 2:n // 2 + 1]).then_inc(gelu, 1)

            @block.tensor
            def _(pe):
                def turn_input(n):
                    pe.wait_ge(normed, n + 1)
                    for c in range(2):
                        for t in range(NT):
                            mm = pe.transpose(ps[0:CH, 6 + c, :].bitcast(BF16)[:, t * P:(t + 1) * P], Ni[:, t, c * CH:(c + 1) * CH],
                                              identb[:, :])
                        mm.then_inc(turned_n, 1)

                turn_input(0)
                pe.wait_ge(quantised, 5)
                pe.wait_ge(n_sb, 2)
                with pe.Fori(0, NB) as b:
                    pe.wait_ge(taken, b + 1)
                    pe.wait_ge(evac, b * EV)
                    for n in range(3):
                        for o in range(2):
                            for c in range(2):
                                mm = pe.matmul(ps[:, 5 + n, o * L:(o + 1) * L], wqk[:, (c * 6 + 2 * n + o) * P:(c * 6 + 2 * n + o + 1) * P],
                                               nb[:, c, :], start=(c == 0), stop=(c == 1))
                        mm.then_inc(proj, 1)
                    for q in range(QT):
                        for c in range(2):
                            mm = pe.matmul(ps[:, 4, q * C:(q + 1) * C], nb[:, c, q * P:(q + 1) * P], wv[:, c * C:(c + 1) * C],
                                           start=(c == 0), stop=(c == 1))
                    mm.then_inc(proj, 1)
                    pe.wait_ge(qk_ready, b + 1)
                    for h in range(NH):
                        pe.wait_ge(score_read, b * NH + max(h - 1, 0))
                        at = slice(32 * (h % HG), 32 * (h % HG) + HE)
                        for q in range(QT):
                            mm = pe.matmul(ps[:, h % 2, q * L:(q + 1) * L], qk[at, h // HG, q * P:(q + 1) * P],
                                           qk[at, 3 + h // HG, :], start=True, stop=True)
                        mm.then_inc(scores, 1)
                    pe.wait_ge(v_ready, b + 1)
                    for n in range(NH + 1):
                        if n < NH:
                            pe.wait_ge(floored, b * NH + n + 1)
                            pe.wait_ge(turned_sb, b * NH + max(n - 1, 0))
                            for kt in range(QT):
                                for q in range(QT):
                                    mm = pe.transpose(ps[:, 2 + n % 2, 0:L].bitcast(BF16)[:, kt * L + q * P:kt * L + (q + 1) * P],
                                                      pi[:, n % 2, q, kt * P:(kt + 1) * P], identb[:, :])
                            mm.then_inc(turned, 1)
                        if n >= 1:
                            h = n - 1
                            pe.wait_ge(turned_sb, b * NH + h + 1)
                            for q in range(QT):
                                for kt in range(QT):
                                    mm = pe.matmul(ps[:, 4, q * C + h * HE:q * C + (h + 1) * HE], PT[:, h % 2, kt, q * P:(q + 1) * P],
                                                   vi[:, kt, h * HE:(h + 1) * HE], start=(kt == 0), stop=(kt == QT - 1))
                            mm.then_inc(summed, 1)
                    pe.wait_ge(evac, b * EV + 7)
                    for c in range(2):
                        for q in range(QT):
                            mm = pe.transpose(ps[0:CH, 5, c * L + q * P:c * L + (q + 1) * P], Os[:, q, c * CH:(c + 1) * CH],
                                              K["ident"][:, :])
                    mm.then_inc(proj, 1)
                    pe.wait_ge(evac, b * EV + 8)
                    for q in range(QT):
                        for c in range(2):
                            mm = pe.matmul(ps[:, 6, q * C:(q + 1) * C], OT[:, c, q * P:(q + 1) * P], wp_f[:, c * C:(c + 1) * C],
                                           start=(c == 0), stop=(c == 1))
                    mm.then_inc(proj, 1)
                turn_input(1)
                pe.wait_ge(n_sb, 4)
                for n in range(FT * NHALF):
                    f, half = divmod(n, 2)
                    if n >= 4:
                        pe.wait_ge(gelu, n - 3)
                    for c in range(2):
                        mm = pe.matmul(ps[:, n % 4, :], w1[:, c * FF + f * P:c * FF + (f + 1) * P],
                                       nT[:, c, half * BANK:(half + 1) * BANK], start=(c == 0), stop=(c == 1))
                    mm.then_inc(up, 1)
                pe.wait_ge(hq, FT * NHALF)
                for t in range(NT):
                    if t >= 4:
                        pe.wait_ge(down_read, t - 3)
                    for f in range(FT):
                        mm = pe.matmul(ps[:, 4 + t % 4, 0:C], hi[:, f, t * P:(t + 1) * P], w2[:, f * C:(f + 1) * C],
                                       start=(f == 0), stop=(f == FT - 1))
                    mm.then_inc(down, 1)


class Turned:

    def __init__(self, ctx):
        self.turned, self.copied = ctx.sem("uT_turned"), ctx.sem("uT_copied")

    def tensor(self, pe, use, ln, ln_use, U, ps, ident):
        for n in range(4):
            for t in range(4):
                ln.done(pe, ln_use, (n // 2) * 4 + t)
                mm = pe.transpose(ps[0:CH, n, t * P:(t + 1) * P], U[:, (n // 2) * 4 + t, (n % 2) * CH:(n % 2 + 1) * CH],
                                  ident[:, :])
            mm.then_inc(self.turned, 1)

    def scalar(self, act, use, uT, ps):
        for n in range(4):
            act.wait_ge(self.turned, 4 * use + n + 1)
            act.activation(uT[:, n % 2, (n // 2) * BANK:(n // 2 + 1) * BANK], ps[0:CH, n, :], ACT.Copy).then_inc(self.copied, 1)

    def wait(self, eng, use):
        eng.wait_ge(self.copied, 4 * (use + 1))


def expert_layer(nc, K, X, D, ln, tr, pre, use, experts, routed, tiles, gated):
    WU = 2 if gated else 1
    MI = 4 * tiles
    with ExitStack() as stack:
        ctx = Ctx(nc, stack)
        U = ctx.sb(f"{pre}_U", [P, NT, C])
        uT = ctx.sb(f"{pre}_uT", [CH, 2, T])
        gate = ctx.sb(f"{pre}_gate", [CH, 2 * routed])
        iota = ctx.sb(f"{pre}_iota", [P, routed])
        lg = ctx.sb(f"{pre}_lg", [P, NT, routed])
        mx = ctx.sb(f"{pre}_mx", [P, NT])
        best = ctx.sb(f"{pre}_best", [P, NT, 8])
        besti = ctx.sb(f"{pre}_besti", [P, NT, 8], U32)
        bestf = ctx.sb(f"{pre}_bestf", [P, NT, 8])
        wts = ctx.sb(f"{pre}_wts", [P, NT, 2])
        t0 = ctx.sb(f"{pre}_t0", [P, NT, routed])
        t1 = ctx.sb(f"{pre}_t1", [P, NT, routed])
        comb = ctx.sb(f"{pre}_comb", [P, experts * NT])
        w_up = [ctx.sb(f"{pre}_wup{a}", [CH, 2 * WU * tiles * P]) for a in range(2)]
        w_dn = [ctx.sb(f"{pre}_wdn{a}", [P, tiles * C]) for a in range(2)]
        b_up = [ctx.sb(f"{pre}_bup{a}", [P, tiles]) for a in range(2)]
        act_out = ctx.sb(f"{pre}_act", [P, 2, BANK])
        h = ctx.sb(f"{pre}_h", [P, 2, tiles, BANK])
        bo = ctx.sb(f"{pre}_bo", [routed, C])
        combT = ctx.sb(f"{pre}_combT", [routed, T])
        ps = ctx.ps(f"ps_{pre}", [P, 8, BANK])
        S = lambda n: ctx.sem(f"{pre}_{n}")
        loaded, logits, route, route_act, top = S("loaded"), S("logits"), S("route"), S("route_act"), S("top")
        comb_turned, comb_sb, bias_ps, bias_added = S("comb_turned"), S("comb_sb"), S("bias_ps"), S("bias_added")
        w_ready = [S(f"w_ready{a}") for a in range(2)]
        up, activated, h_done, down, acc = S("up"), S("activated"), S("h_done"), S("down"), S("acc")
        WD = 3 if not gated else 2
        PAIRS = experts // 2
        comb3 = comb[:, 0:routed * NT].rearrange("p (e t) -> p t e", t=NT)

        with nc.Block() as block:
            @block.sync
            def _(sync):
                def load(i, a):
                    sync.dma_start(w_up[a][:, :], D[f"{pre}_up"][ds((2 * i + a) * CH, CH), :]).then_inc(w_ready[a], 16)
                    sync.dma_start(w_dn[a][:, :], D[f"{pre}_dn"][ds((2 * i + a) * P, P), :]).then_inc(w_ready[a], 16)
                    if not gated:
                        sync.dma_start(b_up[a][:, :], D[f"{pre}_b"][ds((2 * i + a) * P, P), :]).then_inc(w_ready[a], 16)

                for dst, src in ((gate, f"{pre}_gate"), (iota, "iota")):
                    sync.dma_start(dst[:], D[src][:, 0:dst.shape[1]]).then_inc(loaded, 16)
                if not gated:
                    sync.dma_start(bo[:, :], D[f"{pre}_bo"]).then_inc(loaded, 16)
                for a in range(2):
                    load(0, a)
                with sync.Fori(0, PAIRS - 1) as i:
                    for a in range(2):
                        sync.wait_ge(up, i * MI + (a + 1) * 2 * tiles)
                        sync.wait_ge(down, (i * 2 + a + 1) * NT)
                        load(i + 1, a)

            @block.vector
            def _(v):
                step = Chain(v, route)
                ln.vector(v, use, X, U, 1e-5)
                v.wait_ge(loaded, 32 if gated else 48)
                v.wait_ge(logits, 1)
                lp = ps[:, 4, 0:NT * routed].rearrange("p (t e) -> p t e", t=NT)
                if gated:
                    step(v.tensor_reduce(mx[:, :], lp, AX.X, ALU.max))
                    step(v.tensor_tensor(lg[:], lp, mx[:, :].unsqueeze(2).broadcast_to([P, NT, routed]), ALU.subtract))
                    v.wait_ge(route_act, 1)
                    step(v.tensor_reduce(mx[:, :], lg[:], AX.X, ALU.add))
                    step(v.reciprocal(mx[:, :], mx[:, :]))
                    step(v.tensor_tensor(lg[:], lg[:], mx[:, :].unsqueeze(2).broadcast_to([P, NT, routed]), ALU.mult))
                else:
                    step(v.tensor_copy(lg[:], lp))
                for t in range(NT):
                    v.max(best[:, t, :], lg[:, t, :]).then_inc(top, 1)
                for t in range(NT):
                    v.wait_ge(top, t + 1)
                    v.max_index(besti[:, t, :], best[:, t, :], lg[:, t, :]).then_inc(top, 1)
                v.wait_ge(top, 2 * NT)
                step(v.tensor_copy(bestf[:], besti[:]))
                if gated:
                    step(v.tensor_copy(wts[:], best[:, :, 0:2]))
                else:
                    step(v.tensor_tensor(wts[:, :, 1], best[:, :, 1], best[:, :, 0], ALU.subtract))
                    v.wait_ge(route_act, 1)
                    step(v.tensor_scalar(wts[:, :, 0], wts[:, :, 1], 1.0, None, ALU.add))
                    step(v.reciprocal(wts[:, :, 0], wts[:, :, 0]))
                    step(v.tensor_tensor(wts[:, :, 1], wts[:, :, 1], wts[:, :, 0], ALU.mult))
                grid = iota[:, :].unsqueeze(1).broadcast_to([P, NT, routed])
                for j, dst in ((0, t0), (1, t1)):
                    step(v.tensor_tensor(dst[:], grid, bestf[:, :, j:j + 1].broadcast_to([P, NT, routed]), ALU.is_equal))
                    step(v.tensor_tensor(dst[:], dst[:], wts[:, :, j:j + 1].broadcast_to([P, NT, routed]), ALU.mult))
                step(v.tensor_tensor(comb3, t0[:], t1[:], ALU.add))
                if experts > routed:
                    step(v.memset(comb[:, routed * NT:experts * NT], 1.0))
                if not gated:
                    for half in range(NHALF):
                        v.wait_ge(comb_turned, half + 1)
                        v.tensor_copy(combT[:, half * BANK:(half + 1) * BANK], ps[0:routed, half, :]).then_inc(comb_sb, 1)
                    for q in range(NT // 2):
                        v.wait_ge(bias_ps, q + 1)
                        v.tensor_tensor(X[:, 2 * q:2 * q + 2, :], X[:, 2 * q:2 * q + 2, :],
                                        ps[:, 4 + q, 0:2 * C].rearrange("p (a c) -> p a c", a=2), ALU.add).then_inc(bias_added, 1)
                    v.wait_ge(bias_added, NT // 2)
                with v.Fori(0, PAIRS) as i:
                    def hidden(u):
                        v.wait_ge(down, i * 2 * NT + 4 * max(u - 1, 0))
                        for f in range(tiles):
                            m = u * tiles + f
                            v.wait_ge(activated, i * MI + m + 1)
                            v.tensor_tensor(h[:, u % 2, f, :], act_out[:, m % 2, :], ps[:, 2 * (m % 2) + 1, :],
                                            ALU.mult).then_inc(h_done, 1)

                    def accumulate(u):
                        for t in range(4):
                            n = 4 * u + t
                            tok = 4 * (u % 2) + t
                            v.wait_ge(down, i * 2 * NT + n + 1)
                            v.wait_ge(acc, i * 2 * NT + max(n - 7, 0))
                            v.scalar_tensor_tensor(X[:, tok, :], ps[:, 4 + t, 0:C],
                                                   comb[:, ds(i * 2 * NT + (u // 2) * NT + tok, 1)], X[:, tok, :],
                                                   ALU.mult, ALU.add).then_inc(acc, 1)

                    for u in range(4):
                        if gated:
                            hidden(u)
                        if u >= 1:
                            accumulate(u - 1)
                    accumulate(3)
                v.wait_ge(acc, PAIRS * 2 * NT)

            @block.scalar
            def _(act):
                ln.scalar(act, use)
                tr.scalar(act, use - 3, uT, ps)
                if gated:
                    act.wait_ge(route, 2)
                    act.activation(lg[:], lg[:], ACT.Exp).then_inc(route_act, 1)
                else:
                    act.wait_ge(route, 3)
                    act.activation(wts[:, :, 1], wts[:, :, 1], ACT.Exp).then_inc(route_act, 1)
                with act.Fori(0, PAIRS) as i:
                    for u in range(4):
                        a = u // 2
                        if not gated:
                            act.wait_ge(w_ready[a], (i + 1) * 16 * WD)
                            act.wait_ge(down, i * 2 * NT + 4 * max(u - 1, 0))
                        for f in range(tiles):
                            m = u * tiles + f
                            act.wait_ge(up, i * MI + m + 1)
                            if gated:
                                act.wait_ge(h_done, i * MI + max(m - 1, 0))
                                act.activation(act_out[:, m % 2, :], ps[:, 2 * (m % 2), :], ACT.Silu).then_inc(activated, 1)
                            else:
                                act.activation(h[:, u % 2, f, :], ps[:, m % 4, :], ACT.Gelu, bias=b_up[a][:, f:f + 1]).then_inc(h_done, 1)

            @block.tensor
            def _(pe):
                tr.tensor(pe, use - 3, ln, use, U, ps, K["ident"])
                tr.wait(pe, use - 3)
                pe.wait_ge(loaded, 32 if gated else 48)
                for t in range(NT):
                    for c in range(2):
                        mm = pe.matmul(ps[:, 4, t * routed:(t + 1) * routed], uT[:, c, t * P:(t + 1) * P],
                                       gate[:, c * routed:(c + 1) * routed], start=(c == 0), stop=(c == 1))
                mm.then_inc(logits, 1)
                if not gated:
                    pe.wait_ge(route, 11)
                    for t in range(NT):
                        mm = pe.transpose(ps[0:routed, t // 4, (t % 4) * P:(t % 4 + 1) * P], comb3[:, t, :], K["ident"][:, :])
                        if t % 4 == 3:
                            mm.then_inc(comb_turned, 1)
                    pe.wait_ge(comb_sb, 2)
                    for t in range(NT):
                        mm = pe.matmul(ps[:, 4 + t // 2, (t % 2) * C:(t % 2 + 1) * C], combT[:, t * P:(t + 1) * P], bo[:, :],
                                       start=True, stop=True)
                        if t % 2:
                            mm.then_inc(bias_ps, 1)
                    pe.wait_ge(bias_added, NT // 2)
                else:
                    pe.wait_ge(route, 1)
                    pe.wait_ge(route, 2)
                with pe.Fori(0, PAIRS) as i:
                    def up_unit(u):
                        a, half = divmod(u, 2)
                        if half == 0:
                            pe.wait_ge(w_ready[a], (i + 1) * 16 * WD)
                        for f in range(tiles):
                            m = u * tiles + f
                            pe.wait_ge(h_done, i * MI + max(m - (1 if gated else 3), 0))
                            for w in range(WU):
                                bank = 2 * (m % 2) + w if gated else m % 4
                                for c in range(2):
                                    col = ((c * WU + w) * tiles + f) * P
                                    mm = pe.matmul(ps[:, bank, :], w_up[a][:, col:col + P], uT[:, c, half * BANK:(half + 1) * BANK],
                                                   start=(c == 0), stop=(c == 1))
                            mm.then_inc(up, 1)

                    def down_unit(u):
                        a, half = divmod(u, 2)
                        pe.wait_ge(h_done, i * MI + (u + 1) * tiles)
                        for t in range(4):
                            pe.wait_ge(acc, i * 2 * NT + max(4 * u + t - 3, 0))
                            for f in range(tiles):
                                mm = pe.matmul(ps[:, 4 + t, 0:C], h[:, u % 2, f, t * P:(t + 1) * P], w_dn[a][:, f * C:(f + 1) * C],
                                               start=(f == 0), stop=(f == tiles - 1))
                            mm.then_inc(down, 1)

                    for u in range(4):
                        up_unit(u)
                        if u >= 1:
                            down_unit(u - 1)
                    down_unit(3)


def attention_layer(nc, K, X, D, ln, tr, use):
    with ExitStack() as stack:
        ctx = Ctx(nc, stack)
        U = ctx.sb("a_U", [P, NT, C])
        uT = ctx.sb("a_uT", [CH, 2, T])
        wqk = ctx.sb("a_wqk", [CH, 2, 4 * CH])
        wv = ctx.sb("a_wv", [CH, 2, C])
        wo = ctx.sb("a_wo", [CH, 2, C])
        bqk = ctx.sb("a_bqk", [CH, 4])
        rows = ctx.sb("a_rows", [P, 2, C])
        qk = ctx.sb("a_qk", [CH, 4, T])
        vt = ctx.sb("a_v", [P, NT, C])
        nm = ctx.sb("a_nm", [P, NT])
        sums = ctx.sb("a_sums", [P, NT])
        rs = ctx.sb("a_rs", [P, NT])
        Pr = ctx.sb("a_P", [P, 2, QT, L])
        Pn = ctx.sb("a_Pn", [P, 2, QT, L])
        PT = ctx.sb("a_PT", [P, 2, QT, L])
        OT = ctx.sb("a_OT", [CH, 2, 2, L])
        ps = ctx.ps("ps_l5", [P, 8, BANK])
        S = lambda n: ctx.sem(f"l5_{n}")
        loaded, biased, proj, evac, vals, v_sb = S("loaded"), S("biased"), S("proj"), S("evac"), S("vals"), S("v_sb")
        scores, peak, expd, norm, normed, turned, turned_sb, out_ps, out_sb, res_ps, res = (
            S("scores"), S("peak"), S("expd"), S("norm"), S("normed"), S("turned"), S("turned_sb"), S("out_ps"), S("out_sb"),
            S("res_ps"), S("res"))

        with nc.Block() as block:
            @block.sync
            def _(sync):
                for dst, src in ((wqk, "a_wqk"), (wv, "a_wv"), (wo, "a_wo"), (bqk, "a_bqk")):
                    sync.dma_start(dst[:], D[src]).then_inc(loaded, 16)
                sync.dma_start(rows[:], D["a_rows"].partition_broadcast(P)).then_inc(loaded, 16)

            @block.vector
            def _(v):
                ln.vector(v, use, X, U, 1e-5)
                v.wait_ge(ln.out, NT * (use + 1))
                v.wait_ge(loaded, 80)
                v.tensor_tensor(X[:], X[:], rows[:, 1, :].unsqueeze(1).broadcast_to([P, NT, C]), ALU.add).then_inc(biased, 1)
                v.tensor_scalar(bqk[:, 0:2], bqk[:, 0:2], C ** -0.5, None, ALU.mult).then_inc(biased, 1)
                for q in range(NT // 2):
                    v.wait_ge(vals, q + 1)
                    v.tensor_tensor(vt[:, 2 * q:2 * q + 2, :], ps[:, 4 + q, 0:2 * C].rearrange("p (a c) -> p a c", a=2),
                                    rows[:, 0, :].unsqueeze(1).broadcast_to([P, 2, C]), ALU.add).then_inc(v_sb, 1)
                v.wait_ge(biased, 2)
                for n in range(NB + 2):
                    if n < NB:
                        b = n
                        v.wait_ge(scores, b + 1)
                        v.tensor_reduce(nm[:, 2 * b:2 * b + 2], ps[:, b % 2, :].rearrange("p (q k) -> p q k", q=QT), AX.X, ALU.max,
                                        negate=True).then_inc(peak, 1)
                    if 1 <= n <= NB:
                        b = n - 1
                        v.wait_ge(expd, 2 * b + 2)
                        v.reciprocal(rs[:, 2 * b:2 * b + 2], sums[:, 2 * b:2 * b + 2]).then_inc(norm, 1)
                        v.wait_ge(norm, b + 1)
                        if b >= 2:
                            v.wait_ge(turned, b - 1)
                        for q in range(QT):
                            v.tensor_scalar(Pn[:, b % 2, q, :], Pr[:, b % 2, q, :], rs[:, 2 * b + q:2 * b + q + 1], None,
                                            ALU.mult).then_inc(normed, 1)
                        v.wait_ge(turned, b + 1)
                        if b >= 2:
                            v.wait_ge(out_ps, b - 1)
                        v.tensor_copy(PT[:, b % 2, :, :], ps[:, 2 + b % 2, :].rearrange("p (k q) -> p k q", k=QT)).then_inc(turned_sb, 1)
                    if n >= 2:
                        b = n - 2
                        v.wait_ge(res_ps, b + 1)
                        v.tensor_tensor(X[:, 2 * b:2 * b + 2, :], X[:, 2 * b:2 * b + 2, :],
                                        ps[:, 6 + b % 2, 0:2 * C].rearrange("p (a c) -> p a c", a=2), ALU.add).then_inc(res, 1)

            @block.scalar
            def _(act):
                ln.scalar(act, use)
                tr.scalar(act, use - 3, uT, ps)
                act.wait_ge(biased, 2)
                for o in range(4):
                    for half in range(NHALF):
                        n = 2 * o + half
                        act.wait_ge(proj, n + 1)
                        act.activation(qk[:, o, half * BANK:(half + 1) * BANK], ps[0:CH, n % 4, :], ACT.Identity,
                                       scale=C ** -0.5 if o < 2 else 1.0, bias=bqk[:, o:o + 1]).then_inc(evac, 1)
                for n in range(NB + 1):
                    if n < NB:
                        b = n
                        act.wait_ge(peak, b + 1)
                        if b >= 2:
                            act.wait_ge(normed, 2 * b - 2)
                        for q in range(QT):
                            act.activation(Pr[:, b % 2, q, :], ps[:, b % 2, q * L:(q + 1) * L], ACT.Exp,
                                           bias=nm[:, 2 * b + q:2 * b + q + 1],
                                           accum_out=sums[:, 2 * b + q:2 * b + q + 1]).then_inc(expd, 1)
                    if n >= 1:
                        b = n - 1
                        act.wait_ge(out_ps, b + 1)
                        if b >= 2:
                            act.wait_ge(res_ps, b - 1)
                        act.activation(OT[:, b % 2, :, :], ps[0:CH, 4 + b % 2, :].rearrange("p (c t) -> p c t", c=2),
                                       ACT.Copy).then_inc(out_sb, 1)

            @block.tensor
            def _(pe):
                tr.tensor(pe, use - 3, ln, use, U, ps, K["ident"])
                tr.wait(pe, use - 3)
                pe.wait_ge(loaded, 80)
                for o in range(4):
                    for half in range(NHALF):
                        n = 2 * o + half
                        if n >= 4:
                            pe.wait_ge(evac, n - 3)
                        for c in range(2):
                            mm = pe.matmul(ps[0:CH, n % 4, :], wqk[:, c, o * CH:(o + 1) * CH], uT[:, c, half * BANK:(half + 1) * BANK],
                                           start=(c == 0), stop=(c == 1))
                        mm.then_inc(proj, 1)
                for t in range(NT):
                    for c in range(2):
                        mm = pe.matmul(ps[:, 4 + t // 2, (t % 2) * C:(t % 2 + 1) * C], uT[:, c, t * P:(t + 1) * P], wv[:, c, :],
                                       start=(c == 0), stop=(c == 1))
                    if t % 2:
                        mm.then_inc(vals, 1)
                pe.wait_ge(evac, 8)
                pe.wait_ge(v_sb, NT // 2)
                for n in range(NB + 1):
                    if n < NB:
                        b = n
                        if b >= 2:
                            pe.wait_ge(expd, 2 * b - 2)
                        for q in range(QT):
                            for c in range(2):
                                mm = pe.matmul(ps[:, b % 2, q * L:(q + 1) * L], qk[:, c, b * L + q * P:b * L + (q + 1) * P],
                                               qk[:, 2 + c, b * L:(b + 1) * L], start=(c == 0), stop=(c == 1))
                        mm.then_inc(scores, 1)
                    if n >= 1:
                        b = n - 1
                        pe.wait_ge(normed, 2 * b + 2)
                        if b >= 2:
                            pe.wait_ge(turned_sb, b - 1)
                        for k in range(QT):
                            for q in range(QT):
                                mm = pe.transpose(ps[:, 2 + b % 2, k * L + q * P:k * L + (q + 1) * P],
                                                  Pn[:, b % 2, q, k * P:(k + 1) * P], K["ident"][:, :])
                        mm.then_inc(turned, 1)
                        pe.wait_ge(turned_sb, b + 1)
                        if b >= 2:
                            pe.wait_ge(out_sb, b - 1)
                        for c in range(2):
                            for k in range(QT):
                                mm = pe.matmul(ps[0:CH, 4 + b % 2, c * L:(c + 1) * L], vt[:, 2 * b + k, c * CH:(c + 1) * CH],
                                               PT[:, b % 2, k, :], start=(k == 0), stop=(k == QT - 1))
                        mm.then_inc(out_ps, 1)
                        pe.wait_ge(out_sb, b + 1)
                        if b >= 2:
                            pe.wait_ge(res, b - 1)
                        for q in range(QT):
                            for c in range(2):
                                mm = pe.matmul(ps[:, 6 + b % 2, q * C:(q + 1) * C], OT[:, b % 2, c, q * P:(q + 1) * P], wo[:, c, :],
                                               start=(c == 0), stop=(c == 1))
                        mm.then_inc(res_ps, 1)


LAYERS = 6


def program(nc, D, out):
    with ExitStack() as stack:
        ctx = Ctx(nc, stack)
        X = ctx.sb("X", [P, NT, C])
        K = {"ident": ctx.sb("ident", [P, P]), "identb": ctx.sb("identb", [P, P], BF16)}
        constants = ctx.sem("constants")
        with nc.Block() as block:
            @block.sync
            def _(sync):
                sync.dma_start(K["ident"][:, :], D["ident"]).then_inc(constants, 16)

            @block.vector
            def _(v):
                v.wait_ge(constants, 16)
                v.tensor_copy(K["identb"][:, :], K["ident"][:, :]).then_inc(constants, 1)
        scan_layer(nc, K, X, D)
        if LAYERS > 1:
            neighbour_layer(nc, K, X, D)
        ln = LayerNorm(ctx)
        tr = Turned(ctx)
        if LAYERS > 2:
            quantised_layer(nc, K, X, D, ln)
        if LAYERS > 3:
            expert_layer(nc, K, X, D, ln, tr, "m", 3, 18, 16, 4, True)
        if LAYERS > 4:
            attention_layer(nc, K, X, D, ln, tr, 4)
        if LAYERS > 5:
            expert_layer(nc, K, X, D, ln, tr, "g", 5, 8, 8, 6, False)
        stored = ctx.sem("stored")
        with nc.Block() as block:
            @block.sync
            def _(sync):
                for t in range(NT):
                    sync.dma_start(out[t * P:(t + 1) * P, :], X[:, t, :]).then_inc(stored, 16)
                sync.wait_ge(stored, 16 * NT)


def _layouts(i):
    import numpy as np
    g = lambda n: np.asarray(i[n])
    con = np.ascontiguousarray
    halves = lambda a: con(a.reshape(2, CH, -1).transpose(1, 0, 2))
    o = {}
    x = g("x").reshape(T, C)
    o["x"] = con(x)
    o["xT"] = halves(x.T)
    o["w_in"] = halves(g("L0_conv_in_proj_w").T)
    o["cw"] = con(g("L0_conv_conv_w").reshape(DI, 9))
    o["cb"] = con(g("L0_conv_conv_b").reshape(DI, 1))
    xp = g("L0_conv_x_proj_w")
    o["wdt"] = con(xp[:, :RK].transpose(2, 0, 1))
    o["wB"] = con(np.repeat(xp[:, RK:RK + NS], CG, axis=1).transpose(2, 0, 1))
    o["wC"] = con(np.repeat(xp[:, RK + NS:], CG, axis=1).transpose(2, 0, 1))
    o["dtw"] = con(g("L0_conv_dt_projs_w").transpose(2, 0, 1))
    o["dtb"] = con(g("L0_conv_dt_projs_b").T)
    o["Alog"] = con(g("L0_conv_A_logs").reshape(KD, NG, CG, NS).transpose(3, 2, 0, 1).reshape(P, KD * NG))
    o["Dk"] = con(g("L0_conv_Ds").reshape(KD, DI).T)
    o["out_g"] = con(g("L0_conv_out_norm_g").reshape(DI, 1))
    o["out_b"] = con(g("L0_conv_out_norm_b").reshape(DI, 1))
    o["w_out0"] = con(g("L0_conv_out_proj_w").T)
    def padded_heads(w):
        z = np.zeros((C, 3, HG, 32), w.dtype)
        z[..., :HE] = w.reshape(C, 3, HG, HE)
        return z.reshape(2, CH, 3, P).transpose(1, 0, 2, 3)
    w = g("L1_conv_w_qkv")
    o["n_wqk"] = con(np.concatenate([padded_heads(w[:, :C]), padded_heads(w[:, C:2 * C])], axis=2))
    o["n_wv"] = halves(w[:, 2 * C:])
    o["n_wo"] = halves(g("L1_conv_w_out"))
    w = g("L2_attn_w_qkv").T
    o["q_wqk"] = con(np.concatenate([padded_heads(w[:, :C]), padded_heads(w[:, C:2 * C])], axis=2).reshape(CH, -1))
    o["q_wv"] = halves(w[:, 2 * C:]).reshape(CH, -1)
    o["q_wp"] = halves(g("L2_attn_w_proj").T).reshape(CH, -1)
    o["q_w1"] = halves(g("L2_attn_w_fc1").T).reshape(CH, -1)
    o["q_w2"] = con(g("L2_attn_w_fc2").T.reshape(FT, P, C).transpose(1, 0, 2).reshape(P, -1))
    o["q_scales"] = con(g("L2_attn_scales"))
    bq = g("L2_attn_b_qkv")
    z = np.zeros((2, 3, HG, 32), bq.dtype)
    z[..., :HE] = bq[:2 * C].reshape(2, 3, HG, HE)
    o["q_bqk"] = con(z.reshape(6, P).T)
    o["q_b1"] = con(g("L2_attn_b_fc1").reshape(FT, P).T)
    o["q_rows"] = con(np.stack([g("L2_attn_g1"), g("L2_attn_beta1"), g("L2_attn_g2"), g("L2_attn_beta2"), bq[2 * C:],
                                g("L2_attn_b_proj"), g("L2_attn_b_fc2")]))
    w1 = np.concatenate([g("L2_ffn_w1"), g("L2_ffn_sw1").reshape(2, -1, C)])
    w3 = np.concatenate([g("L2_ffn_w3"), g("L2_ffn_sw3").reshape(2, -1, C)])
    w2 = np.concatenate([g("L2_ffn_w2"), g("L2_ffn_sw2").reshape(C, 2, -1).transpose(1, 0, 2)])
    E, F = w1.shape[:2]
    up = np.stack([w1, w3], 1).reshape(E, 2, F, 2, CH)
    o["m_up"] = con(up.transpose(0, 4, 3, 1, 2).reshape(E * CH, -1))
    o["m_dn"] = con(w2.transpose(0, 2, 1).reshape(E, F // P, P, C).transpose(0, 2, 1, 3).reshape(E * P, -1))
    o["m_gate"] = halves(g("L2_ffn_gate_w").T).reshape(CH, -1)
    w = g("L3_attn_w_qkv")
    o["a_wqk"] = halves(w[:, :2 * C])
    o["a_wv"] = halves(w[:, 2 * C:])
    o["a_wo"] = halves(g("L3_attn_w_out"))
    bq = g("L3_attn_b_qkv")
    o["a_bqk"] = con(bq[:2 * C].reshape(4, CH).T)
    o["a_rows"] = con(np.stack([bq[2 * C:], g("L3_attn_b_out")]))
    wi = g("L3_ffn_Wi")
    E, F = wi.shape[:2]
    o["g_up"] = con(wi.reshape(E, F, 2, CH).transpose(0, 3, 2, 1).reshape(E * CH, -1))
    o["g_dn"] = con(g("L3_ffn_Wo").transpose(0, 2, 1).reshape(E, F // P, P, C).transpose(0, 2, 1, 3).reshape(E * P, -1))
    o["g_b"] = con(g("L3_ffn_bi").reshape(E, F // P, P).transpose(0, 2, 1).reshape(E * P, -1))
    o["g_bo"] = con(g("L3_ffn_bo"))
    o["g_gate"] = halves(g("L3_ffn_Wr").T).reshape(CH, -1)
    o["iota"] = con(np.tile(np.arange(16, dtype=np.float32), (P, 1)))
    ch = np.arange(CH)
    p = np.arange(P)
    f = lambda a: con(a.astype(np.float32))
    o["group"] = f((ch[:, None] // 6 == ch[None, :] // 6) / np.float32(6))
    o["avg"] = f(np.ones((DI, DI)) / DI)
    sel = ch[:, None, None] == CG * np.arange(NG)[None, :, None] + p[None, None, :] % CG
    o["sel"] = f(sel)
    o["selT"] = f(sel.transpose(2, 1, 0))
    o["ident"] = f(np.eye(P))
    start = np.clip(np.arange(HW) - HK // 2, 0, HW - HK)
    near = (np.arange(HW)[None, :] >= start[:, None]) & (np.arange(HW)[None, :] < start[:, None] + HK)
    inside = (near[:, None, :, None] & near[None, :, None, :]).reshape(QT, P, L)
    o["n_mask"] = f(np.where(inside, 0, -1e30).transpose(1, 0, 2))
    return o


def kernel(**inputs):
    import numpy as _np
    import concourse.bacc as _bacc
    from concourse.bass_utils import run_bass_kernel_spmd as _run

    nc = _bacc.Bacc("TRN2", target_bir_lowering=False, num_devices=1)
    arrays = _layouts(inputs)
    D = {n: nc.dram_tensor(f"in_{n}", a.shape, mybir.dt.from_np(a.dtype), kind="ExternalInput").ap()
         for n, a in arrays.items()}
    out = nc.dram_tensor("out", (T, C), F32, kind="ExternalOutput").ap()
    program(nc, D, out)
    r = _run(nc, [{f"in_{n}": a for n, a in arrays.items()}], core_ids=[0])
    return r.results[0]["out"].reshape(NB, HW, HW, C)
```

```python
import concourse.bass as bass
from concourse import mybir
from contextlib import ExitStack

F32 = mybir.dt.float32
BF16 = mybir.dt.bfloat16
F16 = mybir.dt.float16
I16 = mybir.dt.int16
I32 = mybir.dt.int32
U32 = mybir.dt.uint32
ALU = mybir.AluOpType
ACT = mybir.ActivationFunctionType
AX = mybir.AxisListType
ds = bass.ds

NB = 4
HW = 16
L = HW * HW
T = NB * L
C = 192
P = 128
CH = C // 2
NT = T // P
BANK = 512
NHALF = T // BANK
MAGIC = 12582912.0


class Ctx:

    def __init__(self, nc, stack):
        self.nc, self.stack, self.sems = nc, stack, []

    def sb(self, name, shape, dt=F32):
        return self.stack.enter_context(self.nc.sbuf_tensor(name, shape, dt))

    def ps(self, name, shape, dt=F32):
        return self.stack.enter_context(self.nc.psum_tensor(name, shape, dt))

    def sem(self, name):
        self.sems.append(self.stack.enter_context(self.nc.semaphore(name)))
        return self.sems[-1]

    def clear(self):
        with self.nc.Block() as block:
            @block.sync
            def _(sync):
                for s in self.sems:
                    sync.sem_clear(s)


class Chain:

    def __init__(self, eng, sem):
        self.eng, self.sem, self.base, self.k = eng, sem, 0, 0

    def __call__(self, ins):
        ins.then_inc(self.sem, 1)
        self.k += 1
        self.eng.wait_ge(self.sem, self.base + self.k)

    def loop(self, i, steps):
        self.start, self.base, self.k, self.steps = self.k, self.k + i * steps, 0, steps

    def end(self, times):
        assert self.k == self.steps, (self.k, self.steps)
        self.base, self.k = 0, self.start + times * self.steps


class GroupNorm:
    N = 2 * NB

    def __init__(self, ctx, pre, buffers=None):
        s = lambda n: ctx.sem(f"{pre}_{n}")
        self.stats, self.gmean, self.spread, self.gvar = s("gn_stats"), s("gn_gmean"), s("gn_spread"), s("gn_gvar")
        self.var, self.std, self.scale, self.out = s("gn_var"), s("gn_std"), s("gn_scale"), s("gn_out")
        sb = lambda n, sh: (buffers or ctx).sb(f"{pre}_{n}", sh)
        self.st = sb("gn_st", [CH, self.N, 6])
        self.mv = sb("gn_mv", [CH, self.N, 2])
        self.gm = sb("gn_gm", [CH, self.N])
        self.d = sb("gn_d", [CH, self.N])
        self.e = sb("gn_e", [CH, self.N])
        self.sd = sb("gn_sd", [CH, self.N])
        self.rs = sb("gn_rs", [CH, self.N])

    def vector(self, v, src, dst, ps, ready):
        N = self.N
        for i in range(N):
            h, b = divmod(i, NB)
            ready(v, i)
            v.bn_stats(self.st[:, i, :], src[:, h, b * L:(b + 1) * L]).then_inc(self.stats, 1)
        for i in range(N):
            v.wait_ge(self.stats, i + 1)
            v.bn_aggr(self.mv[:, i, :], self.st[:, i, :]).then_inc(self.stats, 1)
        v.wait_ge(self.gmean, 1)
        v.tensor_copy(self.gm[:, :], ps[:, 0:N]).then_inc(self.spread, 1)
        v.wait_ge(self.spread, 1)
        v.tensor_tensor(self.d[:, :], self.mv[:, :, 0], self.gm[:, :], ALU.subtract).then_inc(self.spread, 1)
        v.wait_ge(self.spread, 2)
        v.tensor_tensor(self.e[:, :], self.d[:, :], self.d[:, :], ALU.mult).then_inc(self.spread, 1)
        v.wait_ge(self.spread, 3)
        v.tensor_tensor(self.e[:, :], self.e[:, :], self.mv[:, :, 1], ALU.add).then_inc(self.spread, 1)
        v.wait_ge(self.gvar, 1)
        v.tensor_scalar(self.sd[:, :], ps[:, N:2 * N], 1e-5, None, ALU.add).then_inc(self.var, 1)
        v.wait_ge(self.std, 1)
        v.reciprocal(self.rs[:, :], self.sd[:, :]).then_inc(self.scale, 1)
        v.wait_ge(self.scale, 1)
        for i in range(N):
            h, b = divmod(i, NB)
            v.tensor_scalar(dst[:, h, b * L:(b + 1) * L], src[:, h, b * L:(b + 1) * L],
                            self.gm[:, i:i + 1], self.rs[:, i:i + 1], ALU.subtract, ALU.mult).then_inc(self.out, 1)

    def tensor(self, pe, group, ps):
        N = self.N
        pe.wait_ge(self.stats, 2 * N)
        pe.matmul(ps[:, 0:N], group[:, :], self.mv[:, :, 0], start=True, stop=True).then_inc(self.gmean, 1)
        pe.wait_ge(self.spread, 4)
        pe.matmul(ps[:, N:2 * N], group[:, :], self.e[:, :], start=True, stop=True).then_inc(self.gvar, 1)

    def scalar(self, act):
        act.wait_ge(self.var, 1)
        act.activation(self.sd[:, :], self.sd[:, :], ACT.Sqrt).then_inc(self.std, 1)


class LayerNorm:

    def __init__(self, ctx):
        self.stats, self.var, self.std, self.rstd, self.out = (
            ctx.sem(f"ln_{n}") for n in ("stats", "var", "std", "rstd", "out"))
        self.st = ctx.sb("ln_st", [P, NT, 6])
        self.mv = ctx.sb("ln_mv", [P, NT, 2])
        self.sd = ctx.sb("ln_sd", [P, NT])
        self.rs = ctx.sb("ln_rs", [P, NT])

    def vector(self, v, use, src, dst, eps, ready=None):
        if use:
            v.wait_ge(self.out, NT * use)
        for t in range(NT):
            if ready:
                ready(v, t)
            v.bn_stats(self.st[:, t, :], src[:, t, :]).then_inc(self.stats, 1)
        for t in range(NT):
            v.wait_ge(self.stats, 2 * NT * use + t + 1)
            v.bn_aggr(self.mv[:, t, :], self.st[:, t, :]).then_inc(self.stats, 1)
        v.wait_ge(self.stats, 2 * NT * (use + 1))
        v.tensor_scalar(self.sd[:, :], self.mv[:, :, 1], eps, None, ALU.add).then_inc(self.var, 1)
        v.wait_ge(self.std, use + 1)
        v.reciprocal(self.rs[:, :], self.sd[:, :]).then_inc(self.rstd, 1)
        v.wait_ge(self.rstd, use + 1)
        for t in range(NT):
            v.tensor_scalar(dst[:, t, :], src[:, t, :], self.mv[:, t, 0:1], self.rs[:, t:t + 1],
                            ALU.subtract, ALU.mult).then_inc(self.out, 1)

    def scalar(self, act, use):
        act.wait_ge(self.var, use + 1)
        act.activation(self.sd[:, :], self.sd[:, :], ACT.Sqrt).then_inc(self.std, 1)

    def done(self, eng, use, t):
        eng.wait_ge(self.out, NT * use + t + 1)


DI = C // 2
NS = 16
RK = C // 16
CG = P // NS
NG = DI // CG
KD = 4
PW = HW + 2
PR = NB * (HW + 1) + 2
OR = NB * (HW + 1)


SG = 32
NSET = DI // SG
PARTS = 3


def scan_layer(nc, const, X, D):
    with ExitStack() as stack:
        ctx = Ctx(nc, stack)
        wdt = ctx.sb("wdt", [DI, KD, RK])
        wB = ctx.sb("wB", [DI, KD, P])
        wC = ctx.sb("wC", [DI, KD, P])
        dtw = ctx.sb("dtw", [RK, KD, DI])
        dtb = ctx.sb("dtb", [DI, KD])
        Dk = ctx.sb("Dk", [DI, KD])
        Dsum = ctx.sb("Dsum", [DI, 1])
        Alog = ctx.sb("Alog", [P, KD * NG])
        Am = ctx.sb("Am", [P, KD * NG])
        sel32 = ctx.sb("sel32", [PARTS * SG, SG // CG * P])
        sel = ctx.sb("sel", [PARTS * SG, SG // CG * P], BF16)
        selT = ctx.sb("selT", [P, NG, DI])
        gamma = ctx.sb("gamma", [DI, 1])
        beta = ctx.sb("beta", [DI, 1])
        avg = ctx.sb("avg", [DI, DI])
        w_out = ctx.sb("w_out", [DI, C])
        xc = ctx.sb("xc", [DI, 2, T])
        zs = ctx.sb("zs", [DI, T])
        Bb = ctx.sb("Bb", [P, KD, T])
        Cb = ctx.sb("Cb", [P, KD, T])
        d_st = ctx.sb("d_st", [PARTS * SG, KD, NSET, T], BF16)
        du_st = ctx.sb("du_st", [PARTS * SG, KD, NSET, T], BF16)
        ps = ctx.ps("ps_l1", [P, 8, BANK])
        S = lambda n: ctx.sem(f"l1_{n}")
        loaded_x, loaded_w, loaded_p, loaded_s = S("loaded_x"), S("loaded_w"), S("loaded_p"), S("loaded_s")
        cleared, proj, padded, convd, activated, ordered = (
            S("cleared"), S("proj"), S("padded"), S("convd"), S("activated"), S("ordered"))
        dt_low, dt_low_sb, dt_full, bc_ps, bc_sb = S("dt_low"), S("dt_low_sb"), S("dt_full"), S("bc_ps"), S("bc_sb")
        sp_act, sp_vec, sp_pool, A_done = S("sp_act"), S("sp_vec"), S("sp_pool"), S("A_done")
        stacked = [S(f"stacked{b}") for b in range(2)]
        d_bc, du_bc, dA_done, dBu_done, scanned, weighted, y_added, y_out = (
            S("d_bc"), S("du_bc"), S("dA_done"), S("dBu_done"), S("scanned"), S("weighted"), S("y_added"),
            S("y_out"))
        act_past, pool_past = S("act_past"), S("pool_past")
        fin, fin_ps, fin_act, res_ps, res = S("fin"), S("fin_ps"), S("fin_act"), S("res_ps"), S("res")
        flat = lambda a: a[:, :, :].rearrange("p k t -> p (k t)")
        B_flat, C_flat = flat(Bb), flat(Cb)
        STEPS = 2 * NG

        front = stack.enter_context(ExitStack())
        inner = Ctx(nc, front)
        xT = inner.sb("xT", [CH, 2, T])
        xn = inner.sb("xn", [CH, 2, T])
        w_in = inner.sb("w_in", [CH, 2, 2 * DI])
        group = inner.sb("group", [CH, CH])
        pad = inner.sb("pad", [DI, PR, PW])
        cw = inner.sb("cw", [DI, 9])
        cb = inner.sb("cb", [DI, 1])
        conv = inner.sb("conv", [DI, OR, HW])
        gn = GroupNorm(ctx, "l1", inner)
        with nc.Block() as block:
            @block.sync
            def _(sp_):
                for h in range(2):
                    sp_.dma_start(xT[:, h, :], D["xT"][:, h, :]).then_inc(loaded_x, 16)
                sp_.dma_start(group[:, :], D["group"]).then_inc(loaded_x, 16)
                for dst, src in ((w_in, "w_in"), (cw, "cw"), (cb, "cb")):
                    sp_.dma_start(dst[:], D[src]).then_inc(loaded_w, 16)
                for dst, src in ((wdt, "wdt"), (wB, "wB"), (wC, "wC"), (dtw, "dtw"), (dtb, "dtb")):
                    sp_.dma_start(dst[:], D[src]).then_inc(loaded_p, 16)
                for dst, src in ((Alog, "Alog"), (sel32, "sel"), (selT, "selT"), (Dk, "Dk"), (gamma, "out_g"),
                                 (beta, "out_b"), (avg, "avg"), (w_out, "w_out0")):
                    sp_.dma_start(dst[:], D[src]).then_inc(loaded_s, 16)
                for t in range(NT):
                    sp_.dma_start(X[:, t, :], D["x"][t * P:(t + 1) * P, :]).then_inc(loaded_s, 16)

            @block.gpsimd
            def _(pool):
                pool.memset(pad[:], 0.0).then_inc(cleared, 1)

            @block.vector
            def _(v):
                gn.vector(v, xT, xn, ps[0:CH, 7, :], lambda e, i: e.wait_ge(loaded_x, 48))
                v.wait_ge(loaded_w, 48)
                v.wait_ge(padded, 4)
                for n in range(9):
                    tap = pad[:, n // 3:n // 3 + OR, n % 3:n % 3 + HW]
                    if n == 0:
                        v.tensor_scalar(conv[:, :, :], tap, cw[:, 0:1], None, ALU.mult).then_inc(convd, 1)
                    else:
                        v.wait_ge(convd, n)
                        v.scalar_tensor_tensor(conv[:, :, :], tap, cw[:, n:n + 1], conv[:, :, :],
                                               ALU.mult, ALU.add).then_inc(convd, 1)
                v.wait_ge(activated, NB)
                v.tensor_copy(xc[:, 1, :].rearrange("p (b w h) -> p b h w", b=NB, w=HW),
                              xc[:, 0, :].rearrange("p (b h w) -> p b h w", b=NB, h=HW)).then_inc(ordered, 1)
                v.wait_ge(loaded_s, 16 * (8 + NT))
                v.tensor_reduce(Dsum[:, :], Dk[:, :], AX.X, ALU.add).then_inc(ordered, 1)
                v.wait_ge(A_done, 1)
                v.tensor_scalar(Am[:, :], Am[:, :], -1.0, None, ALU.mult).then_inc(ordered, 1)
                v.tensor_copy(sel[:, :], sel32[:, :]).then_inc(ordered, 1)

            @block.scalar
            def _(act):
                gn.scalar(act)
                act.wait_ge(cleared, 1)
                rows = pad[:, 1:1 + OR, 1:1 + HW].rearrange("p (b r) w -> p b r w", b=NB)
                for half in range(NHALF):
                    act.wait_ge(proj, half + 1)
                    for b in range(2):
                        act.activation(rows[:, 2 * half + b, 0:HW, :],
                                       ps[0:DI, half, b * L:(b + 1) * L].rearrange("p (h w) -> p h w", h=HW),
                                       ACT.Copy).then_inc(padded, 1)
                act.wait_ge(proj, 4)
                for half in range(NHALF):
                    act.activation(zs[:, half * BANK:(half + 1) * BANK], ps[0:DI, 2 + half, :], ACT.Silu).then_inc(padded, 1)
                act.wait_ge(convd, 9)
                cr = conv[:, :, :].rearrange("p (b r) w -> p b r w", b=NB)
                for b in range(NB):
                    act.activation(xc[:, 0, b * L:(b + 1) * L].rearrange("p (h w) -> p h w", h=HW),
                                   cr[:, b, 0:HW, :], ACT.Silu, bias=cb[:, 0:1]).then_inc(activated, 1)
                act.wait_ge(loaded_s, 16 * (8 + NT))
                act.activation(Am[:, :], Alog[:, :], ACT.Exp).then_inc(A_done, 1)

            @block.tensor
            def _(pe):
                gn.tensor(pe, group, ps[0:CH, 7, :])
                pe.wait_ge(loaded_w, 48)
                pe.wait_ge(gn.out, 8)
                for o in range(2):
                    for half in range(NHALF):
                        for h in range(2):
                            mm = pe.matmul(ps[0:DI, 2 * o + half, :], w_in[:, h, o * DI:(o + 1) * DI],
                                           xn[:, h, half * BANK:(half + 1) * BANK], start=(h == 0), stop=(h == 1))
                        mm.then_inc(proj, 1)
        front.close()

        mids = stack.enter_context(ExitStack())
        inner = Ctx(nc, mids)
        dtr = inner.sb("dtr", [RK, T])
        ab = inner.sb("ab", [DI, 2, T])
        rl = inner.sb("rl", [DI, 2, T])
        up = inner.sb("up", [DI, 2, T])
        du = inner.sb("du", [DI, 2, T])
        tmp = inner.sb("tmp", [DI, T])
        d_pt = inner.sb("d_pt", [DI, 2, PARTS, T], BF16)
        du_pt = inner.sb("du_pt", [DI, 2, PARTS, T], BF16)
        VS, AS, PS = 11, 4, 3
        MOVES = 2 * PARTS * NSET
        with nc.Block() as block:
            @block.sync
            def _(sync):
                def move(k, part, dst, src):
                    for s in range(NSET):
                        sync.dma_start(dst[part * SG:(part + 1) * SG, k, s, :],
                                       src[s * SG:(s + 1) * SG, k % 2, part, :]).then_inc(stacked[k % 2], 16)

                for k in range(KD):
                    sync.wait_ge(sp_vec, k * VS + 6)
                    move(k, 0, d_st, d_pt)
                    sync.wait_ge(sp_vec, k * VS + 8)
                    move(k, 0, du_st, du_pt)
                    sync.wait_ge(sp_vec, k * VS + 11)
                    move(k, 1, du_st, du_pt)
                    move(k, 1, d_st, d_pt)
                    sync.wait_ge(sp_pool, k * PS + 3)
                    move(k, 2, du_st, du_pt)
                    move(k, 2, d_st, d_pt)
                for b in range(2):
                    sync.wait_ge(stacked[b], KD // 2 * MOVES * 16)

            @block.gpsimd
            def _(pool):
                for k in range(KD):
                    b = k % 2
                    pool.wait_ge(sp_vec, k * VS + 6)
                    pool.tensor_tensor(ab[:, b, :], rl[:, b, :], d_pt[:, b, 0, :], ALU.subtract).then_inc(sp_pool, 1)
                    pool.wait_ge(sp_vec, k * VS + 10)
                    pool.tensor_tensor(du_pt[:, b, 2, :], up[:, b, :], du_pt[:, b, 1, :], ALU.subtract).then_inc(sp_pool, 1)
                    pool.wait_ge(sp_vec, k * VS + 11)
                    pool.tensor_tensor(d_pt[:, b, 2, :], ab[:, b, :], d_pt[:, b, 1, :], ALU.subtract).then_inc(sp_pool, 1)

            @block.vector
            def _(v):
                step = Chain(v, sp_vec)
                for k in range(KD):
                    b = k % 2
                    v.wait_ge(sp_act, k * AS + 3)
                    if k >= 2:
                        v.wait_ge(sp_pool, (k - 1) * PS)
                        v.wait_ge(stacked[b], k // 2 * MOVES * 16)
                    step(v.tensor_scalar(up[:, b, :], ab[:, b, :], 1.0, None, ALU.add))
                    step(v.tensor_scalar(tmp[:, :], up[:, b, :], -1.0, None, ALU.add))
                    step(v.tensor_tensor(ab[:, b, :], ab[:, b, :], tmp[:, :], ALU.subtract))
                    v.wait_ge(sp_act, k * AS + 4)
                    step(v.tensor_tensor(tmp[:, :], up[:, b, :], ab[:, b, :], ALU.add))
                    step(v.tensor_tensor(rl[:, b, :], tmp[:, :], rl[:, b, :], ALU.add))
                    step(v.tensor_copy(d_pt[:, b, 0, :], rl[:, b, :]))
                    step(v.tensor_tensor(du[:, b, :], rl[:, b, :], xc[:, k % 2, :], ALU.mult))
                    step(v.tensor_copy(du_pt[:, b, 0, :], du[:, b, :]))
                    step(v.tensor_tensor(up[:, b, :], du[:, b, :], du_pt[:, b, 0, :], ALU.subtract))
                    step(v.tensor_copy(du_pt[:, b, 1, :], up[:, b, :]))
                    v.wait_ge(sp_pool, k * PS + 1)
                    step(v.tensor_copy(d_pt[:, b, 1, :], ab[:, b, :]))

            @block.scalar
            def _(act):
                act.wait_ge(loaded_p, 80)
                dt = ps[0:DI, 2:4, :].rearrange("p a b -> p (a b)")
                for k in range(KD):
                    b = k % 2
                    act.wait_ge(dt_low, k + 1)
                    act.activation(dtr[:, :], ps[0:RK, 0:2, :].rearrange("p a b -> p (a b)"), ACT.Copy).then_inc(dt_low_sb, 1)
                    act.wait_ge(dt_full, k + 1)
                    if k >= 2:
                        act.wait_ge(sp_vec, (k - 1) * VS)
                        act.wait_ge(sp_pool, (k - 1) * PS)
                    act.activation(ab[:, b, :], dt, ACT.Abs, bias=dtb[:, k:k + 1]).then_inc(sp_act, 1)
                    act.activation(rl[:, b, :], dt, ACT.Relu, bias=dtb[:, k:k + 1]).then_inc(sp_act, 1)
                    act.wait_ge(sp_act, k * AS + 1)
                    act.activation(ab[:, b, :], ab[:, b, :], ACT.Exp, scale=-1.0).then_inc(sp_act, 1)
                    for j in range(2):
                        act.wait_ge(bc_ps, 4 * k + 2 * j + 2)
                        act.activation((Bb, Cb)[j][:, k, :], ps[:, 4 + 2 * j:6 + 2 * j, :].rearrange("p a b -> p (a b)"),
                                       ACT.Copy).then_inc(bc_sb, 1)
                    act.wait_ge(sp_vec, k * VS + 2)
                    act.activation(up[:, b, :], up[:, b, :], ACT.Ln).then_inc(sp_act, 1)

            @block.tensor
            def _(pe):
                pe.wait_ge(loaded_p, 80)
                for k in range(KD):
                    rhs = lambda half: xc[:, k % 2, half * BANK:(half + 1) * BANK]
                    if k >= 1:
                        pe.wait_ge(dt_low_sb, k)
                    for half in range(NHALF):
                        mm = pe.matmul(ps[0:RK, half, :], wdt[:, k, :], rhs(half), start=True, stop=True)
                    mm.then_inc(dt_low, 1)

                    def spread_rows(j, w):
                        if k >= 1:
                            pe.wait_ge(bc_sb, 2 * (k - 1) + j + 1)
                        for half in range(NHALF):
                            pe.matmul(ps[:, 4 + 2 * j + half, :], w[:, k, :], rhs(half), start=True, stop=True).then_inc(bc_ps, 1)

                    spread_rows(0, wB)
                    pe.wait_ge(dt_low_sb, k + 1)
                    if k >= 1:
                        pe.wait_ge(sp_act, (k - 1) * AS + 2)
                    for half in range(NHALF):
                        mm = pe.matmul(ps[0:DI, 2 + half, :], dtw[:, k, :], dtr[:, half * BANK:(half + 1) * BANK],
                                       start=True, stop=True)
                    mm.then_inc(dt_full, 1)
                    spread_rows(1, wC)
        mids.close()

        sp = ctx.sb("sp", [DI, 4, T])
        dA = ctx.sb("dA", [P, 2, 2, T])
        dBu = ctx.sb("dBu", [P, 2, T])
        hs = ctx.sb("hs", [P, 2, T])
        hC = ctx.sb("hC", [P, 2, T])
        ysum = ctx.sb("ysum", [DI, 2, T])
        y_flat = flat(ysum)
        with nc.Block() as block:
            @block.gpsimd
            def _(pool):
                starts = dA[:].rearrange("p d n (b t) -> p d n b t", t=L)
                for d in range(2):
                    for n in range(2):
                        at = 0 if d == 0 else L - 1
                        pool.memset(starts[:, d, n, :, at:at + 1], 0.0).then_inc(cleared, 1)
                with pool.Fori(0, 2) as r:
                    for m in range(STEPS):
                        pool.wait_ge(scanned, r * STEPS + m + 1)
                        pool.wait_ge(y_added, r * STEPS + max(m - 1, 0))
                        pool.sem_inc(pool_past, 1)
                        pool.tensor_tensor(hC[:, m % 2, :], hs[:, m % 2, :], C_flat[:, ds((r + 2 * (m // NG)) * T, T)],
                                           ALU.mult).then_inc(weighted, 1)

            @block.vector
            def _(v):
                with v.Fori(0, 2) as r:
                    for m in range(STEPS):
                        for half in range(NHALF):
                            u = NHALF * m + half
                            v.wait_ge(du_bc, r * NHALF * STEPS + u + 1)
                            v.tensor_tensor(dBu[:, m % 2, half * BANK:(half + 1) * BANK], ps[:, 3 + u % 3, :],
                                            B_flat[:, ds((r + 2 * (m // NG)) * T + half * BANK, BANK)],
                                            ALU.mult).then_inc(dBu_done, 1)
                        v.wait_ge(dBu_done, (r * STEPS + m + 1) * NHALF)
                        v.wait_ge(dA_done, (r * STEPS + m + 1) * NHALF)
                        v.wait_ge(weighted, r * STEPS + max(m - 1, 0))
                        step = 1 if m < NG else -1
                        v.tensor_tensor_scan(hs[:, m % 2, ::step], dA[:, m // NG, m % 2, ::step],
                                             dBu[:, m % 2, ::step], 0.0, ALU.mult, ALU.add).then_inc(scanned, 1)
                v.wait_ge(y_out, 4)
                v.scalar_tensor_tensor(sp[:, 0, :], xc[:, 0, :], Dsum[:, 0:1], ysum[:, 0, :], ALU.mult, ALU.add).then_inc(fin, 1)
                v.wait_ge(fin, 1)
                v.tensor_tensor(sp[:, 1, :].rearrange("p (b h w) -> p b h w", b=NB, h=HW),
                                sp[:, 0, :].rearrange("p (b h w) -> p b h w", b=NB, h=HW),
                                ysum[:, 1, :].rearrange("p (b w h) -> p b h w", b=NB, w=HW), ALU.add).then_inc(fin, 1)
                v.wait_ge(fin_ps, 2)
                v.tensor_tensor(sp[:, 0, :], sp[:, 1, :], ps[0:DI, 0:2, :].rearrange("p a b -> p (a b)"),
                                ALU.subtract).then_inc(fin, 1)
                v.wait_ge(fin_ps, 4)
                v.tensor_scalar(sp[:, 2, :], ps[0:DI, 2:4, :].rearrange("p a b -> p (a b)"), 1e-5, None, ALU.add).then_inc(fin, 1)
                v.wait_ge(fin_act, 2)
                v.reciprocal(sp[:, 3, :], sp[:, 3, :]).then_inc(fin, 1)
                v.wait_ge(fin, 5)
                v.tensor_tensor(sp[:, 0, :], sp[:, 0, :], sp[:, 3, :], ALU.mult).then_inc(fin, 1)
                v.wait_ge(fin, 6)
                v.tensor_scalar(sp[:, 1, :], sp[:, 0, :], gamma[:, 0:1], beta[:, 0:1], ALU.mult, ALU.add).then_inc(fin, 1)
                v.wait_ge(fin, 7)
                v.tensor_tensor(sp[:, 2, :], sp[:, 1, :], zs[:, :], ALU.mult).then_inc(fin, 1)
                for q in range(NT // 2):
                    v.wait_ge(res_ps, q + 1)
                    v.tensor_tensor(X[:, 2 * q:2 * q + 2, :], X[:, 2 * q:2 * q + 2, :],
                                    ps[:, 4 + q, 0:2 * C].rearrange("p (a c) -> p a c", a=2), ALU.add).then_inc(res, 1)

            @block.scalar
            def _(act):
                act.wait_ge(cleared, 5)
                with act.Fori(0, 2) as r:
                    for m in range(STEPS):
                        for half in range(NHALF):
                            u = NHALF * m + half
                            act.wait_ge(d_bc, r * NHALF * STEPS + u + 1)
                            act.wait_ge(scanned, r * STEPS + max(m - 1, 0))
                            act.sem_inc(act_past, 1)
                            o = 1 if m < NG else 0
                            dst = dA[:, m // NG, m % 2, half * BANK:(half + 1) * BANK].rearrange("p (b t) -> p b t", t=L)
                            src = ps[:, u % 3, :].rearrange("p (b t) -> p b t", t=L)
                            act.activation(dst[:, :, o:o + L - 1], src[:, :, o:o + L - 1], ACT.Exp,
                                           scale=Am[:, ds((r + 2 * (m // NG)) * NG + m % NG, 1)]).then_inc(dA_done, 1)
                    act.wait_ge(y_added, (r + 1) * STEPS)
                    for half in range(NHALF):
                        act.sem_inc(act_past, 1)
                        act.activation(y_flat[:, ds(r * T + half * BANK, BANK)], ps[0:DI, 6 + half, :],
                                       ACT.Copy).then_inc(y_out, 1)
                act.wait_ge(fin, 3)
                act.activation(sp[:, 2, :], sp[:, 0, :], ACT.Square).then_inc(fin_act, 1)
                act.wait_ge(fin, 4)
                act.activation(sp[:, 3, :], sp[:, 2, :], ACT.Sqrt).then_inc(fin_act, 1)

            @block.tensor
            def _(pe):
                d_flat = d_st[:, :, :, :].rearrange("p k s t -> p (k s t)")
                du_flat = du_st[:, :, :, :].rearrange("p k s t -> p (k s t)")

                def spread(r, m):
                    for half in range(NHALF):
                        u = NHALF * m + half
                        g = m % NG
                        s, j = divmod(g, SG // CG)
                        at = ds((r + 2 * (m // NG)) * NSET * T + s * T + half * BANK, BANK)
                        spreading = sel[:, j * P:(j + 1) * P]
                        pe.wait_ge(dA_done, r * NHALF * STEPS + max(u - 2, 0))
                        pe.matmul(ps[:, u % 3, :], spreading, d_flat[:, at], start=True, stop=True).then_inc(d_bc, 1)
                        pe.wait_ge(dBu_done, r * NHALF * STEPS + max(u - 2, 0))
                        pe.matmul(ps[:, 3 + u % 3, :], spreading, du_flat[:, at], start=True, stop=True).then_inc(du_bc, 1)

                def add(r, m):
                    pe.wait_ge(weighted, r * STEPS + m + 1)
                    for half in range(NHALF):
                        mm = pe.matmul(ps[0:DI, 6 + half, :], selT[:, m % NG, :], hC[:, m % 2, half * BANK:(half + 1) * BANK],
                                       start=(m == 0), stop=(m == STEPS - 1))
                    mm.then_inc(y_added, 1)

                with pe.Fori(0, 2) as r:
                    for m in range(STEPS):
                        spread(r, m)
                        if m == 2:
                            pe.wait_ge(y_out, r * 2)
                        if m >= 2:
                            add(r, m - 2)
                    add(r, STEPS - 2)
                    add(r, STEPS - 1)
                pe.wait_ge(fin, 2)
                pe.wait_ge(dA_done, 2 * 2 * NG * NHALF)
                for half in range(NHALF):
                    pe.matmul(ps[0:DI, half, :], avg[:, :], sp[:, 1, half * BANK:(half + 1) * BANK], start=True, stop=True).then_inc(fin_ps, 1)
                pe.wait_ge(fin_act, 1)
                pe.wait_ge(dBu_done, 2 * 2 * NG * NHALF)
                for half in range(NHALF):
                    pe.matmul(ps[0:DI, 2 + half, :], avg[:, :], sp[:, 2, half * BANK:(half + 1) * BANK], start=True, stop=True).then_inc(fin_ps, 1)
                pe.wait_ge(fin, 8)
                pe.wait_ge(y_out, 4)
                for t in range(NT):
                    mm = pe.matmul(ps[:, 4 + t // 2, (t % 2) * C:(t % 2 + 1) * C], sp[:, 2, t * P:(t + 1) * P], w_out[:, :],
                                   start=True, stop=True)
                    if t % 2:
                        mm.then_inc(res_ps, 1)
        ctx.clear()


NH = 12
HE = 16
HG = 4
HK = 7
QT = L // P


def neighbour_layer(nc, K, X, D):
    with ExitStack() as stack:
        ctx = Ctx(nc, stack)
        xT = ctx.sb("n_xT", [CH, 2, T])
        xn = ctx.sb("n_xn", [CH, 2, T])
        group = ctx.sb("n_group", [CH, CH])
        xb = ctx.sb("n_xb", [CH, 2, L])
        wqk = ctx.sb("n_wqk", [CH, 2, 6, P])
        wv = ctx.sb("n_wv", [CH, 2, C])
        wo = ctx.sb("n_wo", [CH, 2, C])
        maskf = ctx.sb("n_maskf", [P, QT, L])
        mask = ctx.sb("n_mask", [P, QT, L], BF16)
        qk = ctx.sb("n_qk", [P, 6, L])
        vt = ctx.sb("n_v", [P, QT, C])
        nm = ctx.sb("n_nm", [P, NH, QT])
        sums = ctx.sb("n_sums", [P, QT, NH])
        rs = ctx.sb("n_rs", [P, QT, NH])
        Pr = ctx.sb("n_P", [P, 2, QT, L])
        PT = ctx.sb("n_PT", [P, 2, QT, L])
        On = ctx.sb("n_On", [P, QT, C])
        OT = ctx.sb("n_OT", [CH, 2, L])
        gn = GroupNorm(ctx, "l2")
        ps = ctx.ps("ps_l2", [P, 8, BANK])
        S = lambda n: ctx.sem(f"l2_{n}")
        loaded, masked, x_turned, x_sb, taken, past = (
            S("loaded"), S("masked"), S("x_turned"), S("x_sb"), S("taken"), S("past"))
        proj, evac, scores, peak, expd, turned, turned_sb, summed, norm, added = (
            S("proj"), S("evac"), S("scores"), S("peak"), S("expd"), S("turned"), S("turned_sb"), S("summed"), S("norm"),
            S("added"))
        xn_flat = xn[:, :, :]
        X_flat = X[:, :, :].rearrange("p t c -> p (t c)")
        EV = 6
        PJ = 6

        with nc.Block() as block:
            @block.sync
            def _(sync):
                for dst, src in ((group, "group"), (wqk, "n_wqk"), (wv, "n_wv"), (wo, "n_wo"), (maskf, "n_mask")):
                    sync.dma_start(dst[:], D[src]).then_inc(loaded, 16)

            @block.gpsimd
            def _(pool):
                pool.wait_ge(loaded, 80)
                pool.tensor_copy(mask[:], maskf[:]).then_inc(masked, 1)
                with pool.Fori(0, NB) as b:
                    pool.wait_ge(gn.out, 8)
                    pool.wait_ge(proj, b * PJ)
                    pool.sem_inc(past, 1)
                    pool.tensor_copy(xb[:, :, :], xn_flat[:, :, ds(b * L, L)]).then_inc(taken, 1)

            @block.vector
            def _(v):
                gn.vector(v, xT, xn, ps[0:CH, 7, :], lambda e, i: e.wait_ge(x_sb, 2 * NHALF))
                with v.Fori(0, NB) as b:
                    v.wait_ge(expd, b * NH * QT)

                    def copy_turned(h):
                        v.wait_ge(turned, b * NH + h + 1)
                        v.wait_ge(summed, b * NH + max(h - 1, 0))
                        v.tensor_copy(PT[:, h % 2, :, :], ps[:, 3 + h % 2, :].rearrange("p (k q) -> p k q", k=QT)).then_inc(turned_sb, 1)

                    for s in range(NH + 2):
                        if s < NH:
                            v.wait_ge(scores, b * NH + s + 1)
                            v.tensor_reduce(nm[:, s, :], ps[:, s % 3, :].rearrange("p (q k) -> p q k", q=QT), AX.X, ALU.max,
                                            negate=True).then_inc(peak, 1)
                        if s >= 2:
                            copy_turned(s - 2)
                    v.wait_ge(expd, (b + 1) * NH * QT)
                    v.reciprocal(rs[:], sums[:]).then_inc(norm, 1)
                    v.wait_ge(norm, 2 * b + 1)
                    v.wait_ge(summed, (b + 1) * NH)
                    v.tensor_tensor(On[:, :, :].rearrange("p q (h e) -> p (q h) e", e=HE),
                                    ps[:, 5, 0:QT * C].rearrange("p (n e) -> p n e", e=HE),
                                    rs[:, :, :].rearrange("p q h -> p (q h)").unsqueeze(2).broadcast_to([P, QT * NH, HE]),
                                    ALU.mult).then_inc(norm, 1)
                    v.wait_ge(proj, (b + 1) * PJ)
                    v.tensor_tensor(X_flat[:, ds(b * QT * C, QT * C)], X_flat[:, ds(b * QT * C, QT * C)],
                                    ps[:, 7, 0:QT * C], ALU.add).then_inc(added, 1)

            @block.scalar
            def _(act):
                for n in range(2 * NHALF):
                    act.wait_ge(x_turned, n + 1)
                    act.activation(xT[:, n % 2, (n // 2) * BANK:(n // 2 + 1) * BANK], ps[0:CH, n, :], ACT.Copy).then_inc(x_sb, 1)
                gn.scalar(act)
                two = lambda n: ps[:, 6 + n % 2, :].rearrange("p (a t) -> p a t", a=2)
                with act.Fori(0, NB) as b:
                    act.wait_ge(scores, b * NH)
                    act.wait_ge(proj, b * PJ + 1)
                    act.activation(qk[:, 0:2, :], two(0), ACT.Copy, scale=HE ** -0.5).then_inc(evac, 1)
                    act.wait_ge(proj, b * PJ + 2)
                    act.activation(qk[:, 2, :], two(1)[:, 0, :], ACT.Copy, scale=HE ** -0.5).then_inc(evac, 1)
                    act.activation(qk[:, 3, :], two(1)[:, 1, :], ACT.Copy).then_inc(evac, 1)
                    act.wait_ge(proj, b * PJ + 3)
                    act.activation(qk[:, 4:6, :], two(2), ACT.Copy).then_inc(evac, 1)
                    act.wait_ge(summed, b * NH)
                    act.wait_ge(proj, b * PJ + 4)
                    act.activation(vt[:, :, :], ps[:, 7, 0:QT * C].rearrange("p (q c) -> p q c", q=QT), ACT.Copy).then_inc(evac, 1)
                    act.wait_ge(norm, 2 * b)
                    for s in range(NH):
                        act.wait_ge(peak, b * NH + s + 1)
                        act.wait_ge(turned, b * NH + max(s - 1, 0))
                        for q in range(QT):
                            act.activation(Pr[:, s % 2, q, :], ps[:, s % 3, q * L:(q + 1) * L], ACT.Exp,
                                           bias=nm[:, s, q:q + 1], accum_out=sums[:, q, s:s + 1]).then_inc(expd, 1)
                    act.wait_ge(proj, b * PJ + 5)
                    act.activation(OT[:, :, :], ps[0:CH, 6, :].rearrange("p (c t) -> p c t", c=2), ACT.Copy).then_inc(evac, 1)

            @block.tensor
            def _(pe):
                for n in range(2 * NHALF):
                    for t in range(4):
                        mm = pe.transpose(ps[0:CH, n, t * P:(t + 1) * P],
                                          X[:, (n // 2) * 4 + t, (n % 2) * CH:(n % 2 + 1) * CH], K["ident"][:, :])
                    mm.then_inc(x_turned, 1)
                pe.wait_ge(loaded, 80)
                gn.tensor(pe, group, ps[0:CH, 7, :])
                pe.wait_ge(masked, 1)
                pe.wait_ge(gn.var, 1)
                with pe.Fori(0, NB) as b:
                    pe.wait_ge(taken, b + 1)
                    pe.wait_ge(added, b)
                    for n in range(3):
                        if n == 2:
                            pe.wait_ge(evac, b * EV + 1)
                        for o in range(2):
                            for c in range(2):
                                mm = pe.matmul(ps[:, 6 + n % 2, o * L:(o + 1) * L], wqk[:, c, 2 * n + o, :], xb[:, c, :],
                                               start=(c == 0), stop=(c == 1))
                        mm.then_inc(proj, 1)
                    pe.wait_ge(evac, b * EV + 3)
                    for q in range(QT):
                        for c in range(2):
                            mm = pe.matmul(ps[:, 7, q * C:(q + 1) * C], xb[:, c, q * P:(q + 1) * P], wv[:, c, :],
                                           start=(c == 0), stop=(c == 1))
                    mm.then_inc(proj, 1)
                    pe.wait_ge(evac, b * EV + 4)

                    def score(h):
                        pe.wait_ge(expd, (b * NH + max(h - 2, 0)) * QT)
                        at = slice(32 * (h % HG), 32 * (h % HG) + HE)
                        for q in range(QT):
                            out = ps[:, h % 3, q * L:(q + 1) * L]
                            pe.matmul(out, K["identb"][:, :], mask[:, q, :], start=True, stop=False)
                            mm = pe.matmul(out, qk[at, h // HG, q * P:(q + 1) * P], qk[at, 3 + h // HG, :], start=False, stop=True)
                        mm.then_inc(scores, 1)

                    def turn(h):
                        pe.wait_ge(expd, (b * NH + h + 1) * QT)
                        pe.wait_ge(turned_sb, b * NH + max(h - 1, 0))
                        for k in range(QT):
                            for q in range(QT):
                                mm = pe.transpose(ps[:, 3 + h % 2, k * L + q * P:k * L + (q + 1) * P],
                                                  Pr[:, h % 2, q, k * P:(k + 1) * P], K["ident"][:, :])
                        mm.then_inc(turned, 1)

                    def output(h):
                        pe.wait_ge(turned_sb, b * NH + h + 1)
                        if h == 0:
                            pe.wait_ge(evac, b * EV + 5)
                            pe.wait_ge(norm, 2 * b)
                        for q in range(QT):
                            for k in range(QT):
                                mm = pe.matmul(ps[:, 5, q * C + h * HE:q * C + (h + 1) * HE], PT[:, h % 2, k, q * P:(q + 1) * P],
                                               vt[:, k, h * HE:(h + 1) * HE], start=(k == 0), stop=(k == QT - 1))
                        mm.then_inc(summed, 1)

                    for s in range(NH + 3):
                        if s < NH:
                            score(s)
                        if 2 <= s < NH + 2:
                            turn(s - 2)
                        if s >= 3:
                            output(s - 3)
                    pe.wait_ge(norm, 2 * b + 2)
                    for c in range(2):
                        for q in range(QT):
                            mm = pe.transpose(ps[0:CH, 6, c * L + q * P:c * L + (q + 1) * P], On[:, q, c * CH:(c + 1) * CH],
                                              K["ident"][:, :])
                    mm.then_inc(proj, 1)
                    pe.wait_ge(evac, (b + 1) * EV)
                    for q in range(QT):
                        for c in range(2):
                            mm = pe.matmul(ps[:, 7, q * C:(q + 1) * C], OT[:, c, q * P:(q + 1) * P], wo[:, c, :],
                                           start=(c == 0), stop=(c == 1))
                    mm.then_inc(proj, 1)


FF = 4 * C
FT = FF // P
EXP_N = 30
(S_N1, S_WQKV, S_QKV, S_ATTN, S_WPROJ, S_SV, S_R1, S_N2, S_WFC1, S_ACT, S_WFC2, S_M2, S_R2) = range(13)
(K_QKV, K_ATTN, K_X0, K_BI, K_CI, K_INV, K_QB, K_CLAMP, K_NX0, K_PROJ, K_FC1, K_FC2, K_T0, K_T1) = range(14)


def quantised_layer(nc, K, X, D, ln):
    with ExitStack() as stack:
        ctx = Ctx(nc, stack)
        U = ctx.sb("q_U", [P, NT, C])
        N = ctx.sb("q_N", [P, NT, C])
        Ni = ctx.sb("q_Ni", [P, NT, C], BF16)
        nT = ctx.sb("q_nT", [CH, 2, T], BF16)
        nb = ctx.sb("q_nb", [CH, 2, L], BF16)
        sc = ctx.sb("q_sc", [P, 13])
        rc = ctx.sb("q_rc", [P, 13])
        kf = ctx.sb("q_kf", [P, 14])
        rows = ctx.sb("q_rows", [P, 7, C])
        bqk = ctx.sb("q_bqk", [P, 6])
        b1 = ctx.sb("q_b1", [P, FT])
        wqk_f = ctx.sb("q_wqk_f", [CH, 2 * 6 * P])
        wqk = ctx.sb("q_wqk", [CH, 2 * 6 * P], BF16)
        wv_f = ctx.sb("q_wv_f", [CH, 2 * C])
        wv = ctx.sb("q_wv", [CH, 2 * C], BF16)
        wp_f = ctx.sb("q_wp_f", [CH, 2 * C])
        w1_f = ctx.sb("q_w1_f", [CH, 2 * FF])
        w1 = ctx.sb("q_w1", [CH, 2 * FF], BF16)
        w2_f = ctx.sb("q_w2_f", [P, FT * C])
        w2 = ctx.sb("q_w2", [P, FT * C], BF16)
        qf = ctx.sb("q_qf", [P, 6 * L])
        qk = ctx.sb("q_qk", [P, 6, L], BF16)
        vf = ctx.sb("q_vf", [P, QT, C])
        vi = ctx.sb("q_vi", [P, QT, C], BF16)
        t1 = ctx.sb("q_t1", [P, QT * L])
        t2 = ctx.sb("q_t2", [P, QT, L])
        nm = ctx.sb("q_nm", [P, QT])
        xi = ctx.sb("q_xi", [P, 2, QT, L], BF16)
        qv = ctx.sb("q_qv", [P, 2, QT * L])
        qi = ctx.sb("q_qi", [P, QT * L], BF16)
        ri = ctx.sb("q_ri", [P, 2, QT * L], BF16)
        e2 = ctx.sb("q_e2", [P, 2, QT, L], I16)
        zz = ctx.sb("q_zz", [P, 2, QT, L])
        ex = ctx.sb("q_ex", [P, NH, QT, L])
        sums = ctx.sb("q_sums", [P, NH, QT])
        f0 = ctx.sb("q_f0", [P, NH * QT])
        f1 = ctx.sb("q_f1", [P, NH * QT])
        fac = ctx.sb("q_fac", [P, NH, QT])
        pv = ctx.sb("q_pv", [P, 2, QT * L])
        pr = ctx.sb("q_pr", [P, 2, QT * L])
        pg = ctx.sb("q_pg", [P, 2, QT * L])
        pi = ctx.sb("q_pi", [P, 2, QT, L], BF16)
        PT = ctx.sb("q_PT", [P, 2, QT, L], BF16)
        Os = ctx.sb("q_Os", [P, QT, C])
        OT = ctx.sb("q_OT", [CH, 2, L])
        pj = ctx.sb("q_pj", [P, NT * C])
        hf = ctx.sb("q_hf", [P, 2, T])
        hi = ctx.sb("q_hi", [P, FT, T], BF16)
        ps = ctx.ps("ps_l3", [P, 8, BANK])
        S = lambda n: ctx.sem(f"l3_{n}")
        loaded, w_loaded, vec, pool_steps, quantised, first_ln = (
            S("loaded"), S("w_loaded"), S("vec"), S("pool_steps"), S("quantised"), S("first_ln"))
        scaled, normed, turned_n, n_sb, taken = S("scaled"), S("normed"), S("turned_n"), S("n_sb"), S("taken")
        past, act_past = S("past"), S("act_past")
        proj, evac, qk_ready, v_ready, scores, score_read = (
            S("proj"), S("evac"), S("qk_ready"), S("v_ready"), S("scores"), S("score_read"))
        diff, quot, rest, square, expd, factor, prob, rounded, floored, turned, turned_sb, summed = (
            S("diff"), S("quot"), S("rest"), S("square"), S("expd"), S("factor"), S("prob"), S("rounded"), S("floored"),
            S("turned"), S("turned_sb"), S("summed"))
        excess, resid, up, gelu, hq, down, down_read = S("excess"), S("resid"), S("up"), S("gelu"), S("hq"), S("down"), S("down_read")
        identb = K["identb"]
        flat = lambda a: a[:, :, :].rearrange("p a b -> p (a b)")
        VEC_LOOP = 3 + NH * 4 + 5
        EV = 9

        with nc.Block() as block:
            @block.sync
            def _(sync):
                for dst, src in ((sc, "q_scales"), (rows, "q_rows"), (bqk, "q_bqk"), (b1, "q_b1")):
                    sync.dma_start(dst[:], D[src].partition_broadcast(P) if src in ("q_scales", "q_rows") else D[src]).then_inc(loaded, 16)
                for dst, src in ((wqk_f, "q_wqk"), (wv_f, "q_wv"), (wp_f, "q_wp"), (w1_f, "q_w1"), (w2_f, "q_w2")):
                    sync.dma_start(dst[:], D[src]).then_inc(w_loaded, 16)

            @block.gpsimd
            def _(pool):
                step = Chain(pool, pool_steps)
                pool.wait_ge(scaled, 1)
                pool.wait_ge(w_loaded, 80)
                for f, i, r in ((wqk_f, wqk, S_WQKV), (wv_f, wv, S_WQKV), (wp_f, wp_f, S_WPROJ), (w1_f, w1, S_WFC1),
                                (w2_f, w2, S_WFC2)):
                    n = f.shape[0]
                    step(pool.tensor_scalar(f[:], f[:], rc[0:n, r:r + 1], 127.0, ALU.mult, ALU.min))
                    step(pool.tensor_scalar(f[:], f[:], -128.0, MAGIC, ALU.max, ALU.add))
                    pool.tensor_scalar(i[:], f[:], -MAGIC, None, ALU.add).then_inc(quantised, 1)
                with pool.Fori(0, NB) as b:
                    pool.wait_ge(n_sb, 2)
                    pool.wait_ge(proj, b * 6 + 0)
                    pool.sem_inc(past, 1)
                    pool.tensor_copy(nb[:, :, :], nT[:, :, ds(b * L, L)]).then_inc(taken, 1)
                    for h in range(NH):
                        pool.wait_ge(rounded, b * NH + h + 1)
                        pool.wait_ge(floored, b * NH + max(h - 1, 0))
                        pool.tensor_tensor(pg[:, h % 2, :], pr[:, h % 2, :], pv[:, h % 2, :], ALU.subtract).then_inc(excess, 1)

            @block.vector
            def _(v):
                step = Chain(v, vec)

                def clip_round(dst, src, signal):
                    step(v.tensor_scalar(src, src, 127.0, -128.0, ALU.min, ALU.max))
                    return v.tensor_scalar(dst, src, MAGIC, -MAGIC, ALU.add, ALU.add).then_inc(signal, 1)

                def floor_of(col):
                    c = kf[:, col:col + 1]
                    step(v.tensor_scalar(kf[:, K_T0:K_T0 + 1], c, MAGIC, -MAGIC, ALU.add, ALU.add))
                    step(v.tensor_tensor(kf[:, K_T1:K_T1 + 1], kf[:, K_T0:K_T0 + 1], c, ALU.is_gt))
                    step(v.tensor_tensor(c, kf[:, K_T0:K_T0 + 1], kf[:, K_T1:K_T1 + 1], ALU.subtract))

                k = lambda i: kf[:, i:i + 1]
                s = lambda i: sc[:, i:i + 1]
                r = lambda i: rc[:, i:i + 1]
                v.wait_ge(loaded, 64)
                v.reciprocal(rc[:], sc[:]).then_inc(scaled, 1)
                v.wait_ge(scaled, 1)
                for dst, a, m in ((K_QKV, S_N1, s(S_WQKV)), (K_ATTN, S_QKV, s(S_QKV)), (K_PROJ, S_QKV, s(S_WPROJ)),
                                  (K_FC1, S_N2, s(S_WFC1)), (K_FC2, S_ACT, s(S_WFC2))):
                    step(v.tensor_tensor(k(dst), s(a), m, ALU.mult))
                step(v.tensor_tensor(k(K_QKV), k(K_QKV), r(S_QKV), ALU.mult))
                step(v.tensor_scalar(k(K_ATTN), k(K_ATTN), r(S_ATTN), HE ** -0.5, ALU.mult, ALU.mult))
                step(v.tensor_scalar(k(K_PROJ), k(K_PROJ), r(S_SV), -1 / 128, ALU.mult, ALU.mult))
                step(v.tensor_scalar(k(K_FC2), k(K_FC2), r(S_M2), None, ALU.mult))
                step(v.tensor_scalar(k(K_X0), r(S_ATTN), -0.6931, None, ALU.mult))
                step(v.tensor_scalar(k(K_BI), r(S_ATTN), 1.353, None, ALU.mult))
                step(v.tensor_scalar(k(K_CI), r(S_ATTN), r(S_ATTN), 0.344 / 0.3585, ALU.mult, ALU.mult))
                for c in (K_X0, K_BI, K_CI):
                    floor_of(c)
                step(v.reciprocal(k(K_INV), k(K_X0)))
                step(v.tensor_scalar(k(K_QB), k(K_INV), -0.5, -0.5, ALU.mult, ALU.add))
                step(v.tensor_scalar(k(K_CLAMP), k(K_X0), float(EXP_N), None, ALU.mult))
                step(v.tensor_scalar(k(K_NX0), k(K_X0), -1.0, None, ALU.mult))
                step(v.tensor_scalar(bqk[:], bqk[:], r(S_QKV), None, ALU.mult))
                for row, unit in ((4, S_QKV), (5, S_SV), (6, S_M2)):
                    step(v.tensor_scalar(rows[:, row, :], rows[:, row, :], r(unit), None, ALU.mult))

                def row(i):
                    return rows[:, i, :].unsqueeze(1).broadcast_to([P, NT, C])

                ln.vector(v, 0, X, U, 1e-5)

                def normed_ints(use, g, beta, unit):
                    v.wait_ge(ln.out, NT * use)
                    ln.vector(v, use, U, N, 1e-6)
                    v.wait_ge(ln.out, NT * (use + 1))
                    step(v.tensor_tensor(N[:], N[:], row(g), ALU.mult))
                    step(v.tensor_tensor(N[:], N[:], row(beta), ALU.add))
                    step(v.tensor_scalar(N[:], N[:], r(unit), None, ALU.mult))
                    clip_round(Ni[:], N[:], normed)

                normed_ints(1, 0, 1, S_N1)

                with v.Fori(0, NB) as b:
                    step.loop(b, VEC_LOOP)
                    v.wait_ge(evac, b * EV + 6)
                    v.wait_ge(scores, b * NH)
                    clip_round(flat(qk), qf[:, :], qk_ready)
                    v.wait_ge(proj, b * 6 + 4)
                    v.wait_ge(summed, b * NH)
                    step(v.scalar_tensor_tensor(vf[:], ps[:, 4, 0:QT * C].rearrange("p (q c) -> p q c", q=QT), k(K_QKV),
                                                rows[:, 4, :].unsqueeze(1).broadcast_to([P, QT, C]), ALU.mult, ALU.add))
                    clip_round(vi[:], vf[:], v_ready)
                    v.wait_ge(v_ready, b + 1)
                    v.wait_ge(qk_ready, b + 1)

                    def differences(h):
                        v.wait_ge(scores, b * NH + h + 1)
                        step(v.tensor_scalar(t1[:, :], ps[:, h % 2, :], k(K_ATTN), 127.0, ALU.mult, ALU.min))
                        v.tensor_scalar(t2[:, :, :].rearrange("p q k -> p (q k)"), t1[:, :], -128.0, MAGIC, ALU.max,
                                        ALU.add).then_inc(score_read, 1)
                        v.wait_ge(score_read, b * NH + h + 1)
                        step(v.tensor_reduce(nm[:, :], t2[:, :, :], AX.X, ALU.max, negate=True))
                        for q in range(QT):
                            v.tensor_scalar(xi[:, h % 2, q, :], t2[:, q, :], nm[:, q:q + 1], k(K_CLAMP), ALU.add, ALU.max).then_inc(diff, 1)
                        v.wait_ge(diff, (b * NH + h + 1) * QT)

                    def remainders(h):
                        v.wait_ge(quot, b * NH + h + 1)
                        step(v.tensor_scalar(qi[:, :], qv[:, h % 2, :], MAGIC, -MAGIC, ALU.add, ALU.add))
                        v.scalar_tensor_tensor(ri[:, h % 2, :], qi[:, :], k(K_NX0), xi[:, h % 2, :, :].rearrange("p q k -> p (q k)"),
                                               ALU.mult, ALU.add).then_inc(rest, 1)
                        v.wait_ge(rest, b * NH + h + 1)
                        step(v.tensor_scalar(e2[:, h % 2, :, :].rearrange("p q k -> p (q k)"), qi[:, :], -128.0,
                                             float((127 + EXP_N) * 128), ALU.mult, ALU.add))

                    def exponentials(h):
                        v.wait_ge(square, b * NH + h + 1)
                        for q in range(QT):
                            v.scalar_tensor_tensor(ex[:, h, q, :], zz[:, h % 2, q, :], k(K_CI), e2[:, h % 2, q, :].bitcast(BF16),
                                                   ALU.add, ALU.mult, accum_out=sums[:, h, q:q + 1]).then_inc(expd, 1)
                        v.wait_ge(expd, (b * NH + h + 1) * QT)

                    v.wait_ge(prob, b * NH * QT)
                    for n in range(NH + 2):
                        if n < NH:
                            differences(n)
                        if 1 <= n <= NH:
                            remainders(n - 1)
                        if n >= 2:
                            exponentials(n - 2)
                    sf = sums[:, :, :].rearrange("p h q -> p (h q)")
                    step(v.reciprocal(f0[:, :], sf))
                    step(v.tensor_scalar(f0[:, :], f0[:, :], 2.0 ** 32, None, ALU.mult))
                    step(v.tensor_scalar(f1[:, :], f0[:, :], MAGIC, -MAGIC, ALU.add, ALU.add))
                    step(v.tensor_tensor(f0[:, :], f1[:, :], f0[:, :], ALU.is_gt))
                    step(v.tensor_tensor(f1[:, :], f1[:, :], f0[:, :], ALU.subtract))
                    v.tensor_scalar(fac[:, :, :].rearrange("p h q -> p (h q)"), f1[:, :], 2.0 ** -25, None, ALU.mult).then_inc(factor, 1)
                    for n in range(NH + 2):
                        if n < NH:
                            v.wait_ge(prob, (b * NH + n + 1) * QT)
                            v.wait_ge(floored, b * NH + max(n - 1, 0))
                            v.tensor_scalar(pr[:, n % 2, :], pv[:, n % 2, :], MAGIC, -MAGIC, ALU.add, ALU.add).then_inc(rounded, 1)
                        if 1 <= n <= NH:
                            h = n - 1
                            v.wait_ge(excess, b * NH + h + 1)
                            v.wait_ge(rounded, b * NH + h + 1)
                            v.wait_ge(turned, b * NH + max(h - 1, 0))
                            v.scalar_tensor_tensor(pi[:, h % 2, :, :].rearrange("p q k -> p (q k)"), pg[:, h % 2, :], 0.0,
                                                   pr[:, h % 2, :], ALU.is_gt, ALU.subtract).then_inc(floored, 1)
                        if n >= 2:
                            h = n - 2
                            v.wait_ge(turned, b * NH + h + 1)
                            v.wait_ge(summed, b * NH + max(h - 1, 0))
                            v.tensor_copy(PT[:, h % 2, :, :], ps[:, 2 + h % 2, 0:L].bitcast(BF16).rearrange("p (k q) -> p k q", k=QT)).then_inc(turned_sb, 1)
                step.end(NB)
                v.wait_ge(factor, NB)

                def requantised(src, units, unit, add_to, out_unit):
                    step(v.tensor_scalar(src, src, 127.0, -128.0, ALU.min, ALU.max))
                    step(v.tensor_scalar(src, src, MAGIC, -MAGIC, ALU.add, ALU.add))
                    step(v.scalar_tensor_tensor(src, src, s(unit), add_to, ALU.mult, ALU.add))
                    step(v.tensor_scalar(src, src, r(out_unit), 127.0, ALU.mult, ALU.min))
                    step(v.tensor_scalar(src, src, -128.0, MAGIC, ALU.max, ALU.add))
                    v.tensor_scalar(add_to, src, -MAGIC, s(out_unit), ALU.add, ALU.mult).then_inc(resid, 1)

                v.wait_ge(evac, NB * EV)
                step(v.scalar_tensor_tensor(pj[:, :].rearrange("p (t c) -> p t c", c=C), pj[:, :].rearrange("p (t c) -> p t c", c=C),
                                            k(K_PROJ), row(5), ALU.mult, ALU.add))
                requantised(pj[:, :], None, S_SV, flat(U), S_R1)
                v.wait_ge(resid, 1)
                v.wait_ge(turned_n, 2)
                normed_ints(2, 2, 3, S_N2)
                for n in range(FT * NHALF):
                    src = hf[:, n % 2, 0:BANK]
                    v.wait_ge(gelu, n + 1)
                    step(v.tensor_scalar(src, src, r(S_ACT), 127.0, ALU.mult, ALU.min))
                    step(v.tensor_scalar(src, src, -128.0, MAGIC, ALU.max, ALU.add))
                    v.tensor_scalar(hi[:, n // 2, (n % 2) * BANK:(n % 2 + 1) * BANK], src, -MAGIC, None, ALU.add).then_inc(hq, 1)
                v.wait_ge(hq, FT * NHALF)
                pj3 = pj[:, :].rearrange("p (t c) -> p t c", c=C)
                for t in range(NT):
                    v.wait_ge(down, t + 1)
                    v.scalar_tensor_tensor(pj3[:, t, :], ps[:, 4 + t % 4, 0:C], k(K_FC2), rows[:, 6, :], ALU.mult, ALU.add).then_inc(down_read, 1)
                v.wait_ge(down_read, NT)
                requantised(pj[:, :], None, S_M2, flat(U), S_R2)
                v.wait_ge(resid, 2)
                step(v.tensor_tensor(flat(X), flat(X), flat(U), ALU.add))

            @block.scalar
            def _(act):
                ln.scalar(act, 0)
                ln.scalar(act, 1)
                act.wait_ge(scaled, 1)
                act.wait_ge(normed, 1)

                def turned_input(n):
                    for c in range(2):
                        act.wait_ge(turned_n, 2 * n + c + 1)
                        act.activation(nT[:, c, :], ps[0:CH, 6 + c, :].bitcast(BF16), ACT.Copy).then_inc(n_sb, 1)

                turned_input(0)
                with act.Fori(0, NB) as b:
                    act.wait_ge(qk_ready, b)
                    for o in range(6):
                        if o % 2 == 0:
                            act.wait_ge(proj, b * 6 + o // 2 + 1)
                        act.activation(qf[:, o * L:(o + 1) * L], ps[:, 5 + o // 2, (o % 2) * L:(o % 2 + 1) * L], ACT.Identity,
                                       scale=kf[:, K_QKV:K_QKV + 1], bias=bqk[:, o:o + 1]).then_inc(evac, 1)
                    for n in range(NH + 1):
                        if n < NH:
                            act.wait_ge(diff, (b * NH + n + 1) * QT)
                            act.wait_ge(rest, b * NH + max(n - 1, 0))
                            act.activation(qv[:, n % 2, :], xi[:, n % 2, :, :].rearrange("p q k -> p (q k)"), ACT.Identity,
                                           scale=kf[:, K_INV:K_INV + 1], bias=kf[:, K_QB:K_QB + 1]).then_inc(quot, 1)
                        if n >= 1:
                            h = n - 1
                            act.wait_ge(rest, b * NH + h + 1)
                            act.wait_ge(expd, (b * NH + max(h - 1, 0)) * QT)
                            act.activation(zz[:, h % 2, :, :].rearrange("p q k -> p (q k)"), ri[:, h % 2, :], ACT.Square,
                                           bias=kf[:, K_BI:K_BI + 1]).then_inc(square, 1)
                    act.wait_ge(factor, b + 1)
                    for h in range(NH):
                        act.wait_ge(floored, b * NH + max(h - 1, 0))
                        for q in range(QT):
                            act.activation(pv[:, h % 2, q * L:(q + 1) * L], ex[:, h, q, :], ACT.Identity,
                                           scale=fac[:, h, q:q + 1]).then_inc(prob, 1)
                    act.wait_ge(summed, (b + 1) * NH)
                    act.activation(Os[:, :, :], ps[:, 4, 0:QT * C].rearrange("p (q c) -> p q c", q=QT), ACT.Copy).then_inc(evac, 1)
                    act.wait_ge(proj, b * 6 + 5)
                    act.activation(OT[:, :, :], ps[0:CH, 5, :].rearrange("p (c t) -> p c t", c=2), ACT.Copy).then_inc(evac, 1)
                    act.wait_ge(proj, b * 6 + 6)
                    act.sem_inc(act_past, 1)
                    act.activation(pj[:, ds(b * QT * C, QT * C)], ps[:, 6, 0:QT * C], ACT.Copy).then_inc(evac, 1)
                ln.scalar(act, 2)
                turned_input(1)
                for n in range(FT * NHALF):
                    act.wait_ge(up, n + 1)
                    act.wait_ge(hq, max(n - 1, 0))
                    act.activation(hf[:, n % 2, 0:BANK], ps[:, n % 4, :], ACT.Gelu, scale=kf[:, K_FC1:K_FC1 + 1],
                                   bias=b1[:, n // 2:n // 2 + 1]).then_inc(gelu, 1)

            @block.tensor
            def _(pe):
                def turn_input(n):
                    pe.wait_ge(normed, n + 1)
                    for c in range(2):
                        for t in range(NT):
                            mm = pe.transpose(ps[0:CH, 6 + c, :].bitcast(BF16)[:, t * P:(t + 1) * P], Ni[:, t, c * CH:(c + 1) * CH],
                                              identb[:, :])
                        mm.then_inc(turned_n, 1)

                turn_input(0)
                pe.wait_ge(quantised, 5)
                pe.wait_ge(n_sb, 2)
                with pe.Fori(0, NB) as b:
                    pe.wait_ge(taken, b + 1)
                    pe.wait_ge(evac, b * EV)
                    for n in range(3):
                        for o in range(2):
                            for c in range(2):
                                mm = pe.matmul(ps[:, 5 + n, o * L:(o + 1) * L], wqk[:, (c * 6 + 2 * n + o) * P:(c * 6 + 2 * n + o + 1) * P],
                                               nb[:, c, :], start=(c == 0), stop=(c == 1))
                        mm.then_inc(proj, 1)
                    for q in range(QT):
                        for c in range(2):
                            mm = pe.matmul(ps[:, 4, q * C:(q + 1) * C], nb[:, c, q * P:(q + 1) * P], wv[:, c * C:(c + 1) * C],
                                           start=(c == 0), stop=(c == 1))
                    mm.then_inc(proj, 1)
                    pe.wait_ge(qk_ready, b + 1)
                    for h in range(NH):
                        pe.wait_ge(score_read, b * NH + max(h - 1, 0))
                        at = slice(32 * (h % HG), 32 * (h % HG) + HE)
                        for q in range(QT):
                            mm = pe.matmul(ps[:, h % 2, q * L:(q + 1) * L], qk[at, h // HG, q * P:(q + 1) * P],
                                           qk[at, 3 + h // HG, :], start=True, stop=True)
                        mm.then_inc(scores, 1)
                    pe.wait_ge(v_ready, b + 1)
                    for n in range(NH + 1):
                        if n < NH:
                            pe.wait_ge(floored, b * NH + n + 1)
                            pe.wait_ge(turned_sb, b * NH + max(n - 1, 0))
                            for kt in range(QT):
                                for q in range(QT):
                                    mm = pe.transpose(ps[:, 2 + n % 2, 0:L].bitcast(BF16)[:, kt * L + q * P:kt * L + (q + 1) * P],
                                                      pi[:, n % 2, q, kt * P:(kt + 1) * P], identb[:, :])
                            mm.then_inc(turned, 1)
                        if n >= 1:
                            h = n - 1
                            pe.wait_ge(turned_sb, b * NH + h + 1)
                            for q in range(QT):
                                for kt in range(QT):
                                    mm = pe.matmul(ps[:, 4, q * C + h * HE:q * C + (h + 1) * HE], PT[:, h % 2, kt, q * P:(q + 1) * P],
                                                   vi[:, kt, h * HE:(h + 1) * HE], start=(kt == 0), stop=(kt == QT - 1))
                            mm.then_inc(summed, 1)
                    pe.wait_ge(evac, b * EV + 7)
                    for c in range(2):
                        for q in range(QT):
                            mm = pe.transpose(ps[0:CH, 5, c * L + q * P:c * L + (q + 1) * P], Os[:, q, c * CH:(c + 1) * CH],
                                              K["ident"][:, :])
                    mm.then_inc(proj, 1)
                    pe.wait_ge(evac, b * EV + 8)
                    for q in range(QT):
                        for c in range(2):
                            mm = pe.matmul(ps[:, 6, q * C:(q + 1) * C], OT[:, c, q * P:(q + 1) * P], wp_f[:, c * C:(c + 1) * C],
                                           start=(c == 0), stop=(c == 1))
                    mm.then_inc(proj, 1)
                turn_input(1)
                pe.wait_ge(n_sb, 4)
                for n in range(FT * NHALF):
                    f, half = divmod(n, 2)
                    if n >= 4:
                        pe.wait_ge(gelu, n - 3)
                    for c in range(2):
                        mm = pe.matmul(ps[:, n % 4, :], w1[:, c * FF + f * P:c * FF + (f + 1) * P],
                                       nT[:, c, half * BANK:(half + 1) * BANK], start=(c == 0), stop=(c == 1))
                    mm.then_inc(up, 1)
                pe.wait_ge(hq, FT * NHALF)
                for t in range(NT):
                    if t >= 4:
                        pe.wait_ge(down_read, t - 3)
                    for f in range(FT):
                        mm = pe.matmul(ps[:, 4 + t % 4, 0:C], hi[:, f, t * P:(t + 1) * P], w2[:, f * C:(f + 1) * C],
                                       start=(f == 0), stop=(f == FT - 1))
                    mm.then_inc(down, 1)


class Turned:

    def __init__(self, ctx):
        self.turned, self.copied = ctx.sem("uT_turned"), ctx.sem("uT_copied")

    def tensor(self, pe, use, ln, ln_use, U, ps, ident):
        for n in range(4):
            for t in range(4):
                ln.done(pe, ln_use, (n // 2) * 4 + t)
                mm = pe.transpose(ps[0:CH, n, t * P:(t + 1) * P], U[:, (n // 2) * 4 + t, (n % 2) * CH:(n % 2 + 1) * CH],
                                  ident[:, :])
            mm.then_inc(self.turned, 1)

    def scalar(self, act, use, uT, ps):
        for n in range(4):
            act.wait_ge(self.turned, 4 * use + n + 1)
            act.activation(uT[:, n % 2, (n // 2) * BANK:(n // 2 + 1) * BANK], ps[0:CH, n, :], ACT.Copy).then_inc(self.copied, 1)

    def wait(self, eng, use):
        eng.wait_ge(self.copied, 4 * (use + 1))


CA = P
CB = C - CA
XS = 16.0
WS = 256.0


def expert_layer(nc, K, X, D, ln, tr, pre, use, experts, routed, tiles, gated):
    WU = 2 if gated else 1
    MI = 4 * tiles
    NU = WU * tiles * P
    ND = tiles * C
    with ExitStack() as stack:
        ctx = Ctx(nc, stack)
        U = ctx.sb(f"{pre}_U", [P, NT, C])
        uT = ctx.sb(f"{pre}_uT", [CH, 2, T])
        U2 = ctx.sb(f"{pre}_U2", [P, NT, 2 * CB])
        xa_hi = ctx.sb(f"{pre}_xa_hi", [CA, T], F16)
        xa_lo = ctx.sb(f"{pre}_xa_lo", [CA, T], F16)
        xb_hi = ctx.sb(f"{pre}_xb_hi", [2 * CB, T], F16)
        xb_lo = ctx.sb(f"{pre}_xb_lo", [CB, T], F16)
        gate = ctx.sb(f"{pre}_gate", [CH, 2 * routed])
        iota = ctx.sb(f"{pre}_iota", [P, routed])
        lg = ctx.sb(f"{pre}_lg", [P, NT, routed])
        mx = ctx.sb(f"{pre}_mx", [P, NT])
        best = ctx.sb(f"{pre}_best", [P, NT, 8])
        besti = ctx.sb(f"{pre}_besti", [P, NT, 8], U32)
        bestf = ctx.sb(f"{pre}_bestf", [P, NT, 8])
        wts = ctx.sb(f"{pre}_wts", [P, NT, 2])
        t0 = ctx.sb(f"{pre}_t0", [P, NT, routed])
        t1 = ctx.sb(f"{pre}_t1", [P, NT, routed])
        comb = ctx.sb(f"{pre}_comb", [P, experts * NT])
        combs = ctx.sb(f"{pre}_combs", [P, experts * NT])
        st_up = [ctx.sb(f"{pre}_stup{a}", [P, 2 * NU]) for a in range(2)]
        st_dn = [ctx.sb(f"{pre}_stdn{a}", [P, ND]) for a in range(2)]
        st_b = [ctx.sb(f"{pre}_stb{a}", [P, tiles]) for a in range(2)]
        wa_hi = [ctx.sb(f"{pre}_wa_hi{a}", [CA, NU], F16) for a in range(2)]
        wa_lo = [ctx.sb(f"{pre}_wa_lo{a}", [CA, NU], F16) for a in range(2)]
        wb = [ctx.sb(f"{pre}_wb{a}", [2 * CB, NU], F16) for a in range(2)]
        wd_hi = [ctx.sb(f"{pre}_wd_hi{a}", [P, ND], F16) for a in range(2)]
        wd_lo = [ctx.sb(f"{pre}_wd_lo{a}", [P, ND], F16) for a in range(2)]
        b_up = [ctx.sb(f"{pre}_bup{a}", [P, tiles]) for a in range(2)]
        act_out = ctx.sb(f"{pre}_act", [P, 4, BANK])
        h32 = ctx.sb(f"{pre}_h32", [P, 2, BANK])
        h_hi = ctx.sb(f"{pre}_h_hi", [P, 2, tiles, BANK], F16)
        h_lo = ctx.sb(f"{pre}_h_lo", [P, 2, tiles, BANK], F16)
        bo = ctx.sb(f"{pre}_bo", [routed, C])
        combT = ctx.sb(f"{pre}_combT", [routed, T])
        ps = ctx.ps(f"ps_{pre}", [P, 8, BANK])
        S = lambda n: ctx.sem(f"{pre}_{n}")
        loaded, logits, route, route_act, top = S("loaded"), S("logits"), S("route"), S("route_act"), S("top")
        comb_turned, comb_sb, bias_ps, bias_added = S("comb_turned"), S("comb_sb"), S("bias_ps"), S("bias_added")
        doubled, sync_past = S("doubled"), S("sync_past")
        x_turned, x_hi, x_lo, split_hi, split_lo, b_copied = (
            S("x_turned"), S("x_hi"), S("x_lo"), S("split_hi"), S("split_lo"), S("b_copied"))
        w_ready = [S(f"w_ready{a}") for a in range(2)]
        up, activated, h_part, h_done, down, acc = S("up"), S("activated"), S("h_part"), S("h_done"), S("down"), S("acc")
        WD = 2 if gated else 3
        PAIRS = experts // 2
        SP = 3
        HP = 2 if gated else 1
        splits = {(0, 1): (1, 0, SP), (0, 2): (1, 1, SP + 1), (0, 3): (1, 2, SP + 2),
                  (2, 1): (0, 0, 2 * SP), (2, 2): (0, 1, 2 * SP + 1), (3, 0): (0, 2, 2 * SP + 2)}
        comb3 = comb[:, 0:routed * NT].rearrange("p (e t) -> p t e", t=NT)

        with nc.Block() as block:
            @block.sync
            def _(sync):
                def load(i, a):
                    sync.dma_start(st_up[a][:, :], D[f"{pre}_up"][ds((2 * i + a) * P, P), :]).then_inc(w_ready[a], 16)
                    sync.dma_start(st_dn[a][:, :], D[f"{pre}_dn"][ds((2 * i + a) * P, P), :]).then_inc(w_ready[a], 16)
                    if not gated:
                        sync.dma_start(st_b[a][:, :], D[f"{pre}_b"][ds((2 * i + a) * P, P), :]).then_inc(w_ready[a], 16)

                for dst, src in ((gate, f"{pre}_gate"), (iota, "iota")):
                    sync.dma_start(dst[:], D[src][:, 0:dst.shape[1]]).then_inc(loaded, 16)
                if not gated:
                    sync.dma_start(bo[:, :], D[f"{pre}_bo"]).then_inc(loaded, 16)
                for a in range(2):
                    load(0, a)
                with sync.Fori(0, PAIRS) as i:
                    for a in range(2):
                        sync.wait_ge(split_lo, i * 2 * SP + (a + 1) * SP)
                        sync.sem_inc(sync_past, 1)
                        load(i + 1, a)
                for a in range(2):
                    sync.wait_ge(w_ready[a], (PAIRS + 1) * 16 * WD)

            @block.gpsimd
            def _(pool):
                ln.done(pool, use, NT - 1)
                for n in range(2):
                    pool.tensor_copy(U2[:, :, n * CB:(n + 1) * CB], U[:, :, CA:C]).then_inc(doubled, 1)

            @block.vector
            def _(v):
                step = Chain(v, route)

                def split(i, a, part, n):
                    v.wait_ge(split_hi, i * 2 * SP + n + 1)
                    lo, st, hi = ((wa_lo[a][:, :], st_up[a][:, 0:NU], wa_hi[a][:, :]),
                                  (wb[a][CB:2 * CB, :], st_up[a][CB:2 * CB, NU:2 * NU], wb[a][CB:2 * CB, :]),
                                  (wd_lo[a][:, :], st_dn[a][:, :], wd_hi[a][:, :]))[part]
                    v.scalar_tensor_tensor(lo, st, WS, hi, ALU.mult, ALU.subtract).then_inc(split_lo, 1)

                ln.vector(v, use, X, U, 1e-5)
                for half in range(NHALF):
                    at = slice(half * BANK, (half + 1) * BANK)
                    v.wait_ge(x_hi, 2 * half + 1)
                    v.scalar_tensor_tensor(xa_lo[:, at], ps[:, 4 + half, :], XS, xa_hi[:, at], ALU.mult, ALU.subtract).then_inc(x_lo, 1)
                    v.wait_ge(x_hi, 2 * half + 2)
                    v.scalar_tensor_tensor(xb_lo[:, at], ps[0:CB, 6 + half, :], XS, xb_hi[0:CB, at], ALU.mult,
                                           ALU.subtract).then_inc(x_lo, 1)
                for part in range(SP):
                    split(0, 0, part, part)
                v.wait_ge(loaded, 32 if gated else 48)
                v.wait_ge(logits, 1)
                lp = ps[:, 4, 0:NT * routed].rearrange("p (t e) -> p t e", t=NT)
                if gated:
                    step(v.tensor_reduce(mx[:, :], lp, AX.X, ALU.max))
                    step(v.tensor_tensor(lg[:], lp, mx[:, :].unsqueeze(2).broadcast_to([P, NT, routed]), ALU.subtract))
                    v.wait_ge(route_act, 1)
                    step(v.tensor_reduce(mx[:, :], lg[:], AX.X, ALU.add))
                    step(v.reciprocal(mx[:, :], mx[:, :]))
                    step(v.tensor_tensor(lg[:], lg[:], mx[:, :].unsqueeze(2).broadcast_to([P, NT, routed]), ALU.mult))
                else:
                    step(v.tensor_copy(lg[:], lp))
                for t in range(NT):
                    v.max(best[:, t, :], lg[:, t, :]).then_inc(top, 1)
                for t in range(NT):
                    v.wait_ge(top, t + 1)
                    v.max_index(besti[:, t, :], best[:, t, :], lg[:, t, :]).then_inc(top, 1)
                v.wait_ge(top, 2 * NT)
                step(v.tensor_copy(bestf[:], besti[:]))
                if gated:
                    step(v.tensor_copy(wts[:], best[:, :, 0:2]))
                else:
                    step(v.tensor_tensor(wts[:, :, 1], best[:, :, 1], best[:, :, 0], ALU.subtract))
                    v.wait_ge(route_act, 1)
                    step(v.tensor_scalar(wts[:, :, 0], wts[:, :, 1], 1.0, None, ALU.add))
                    step(v.reciprocal(wts[:, :, 0], wts[:, :, 0]))
                    step(v.tensor_tensor(wts[:, :, 1], wts[:, :, 1], wts[:, :, 0], ALU.mult))
                grid = iota[:, :].unsqueeze(1).broadcast_to([P, NT, routed])
                for j, dst in ((0, t0), (1, t1)):
                    step(v.tensor_tensor(dst[:], grid, bestf[:, :, j:j + 1].broadcast_to([P, NT, routed]), ALU.is_equal))
                    step(v.tensor_tensor(dst[:], dst[:], wts[:, :, j:j + 1].broadcast_to([P, NT, routed]), ALU.mult))
                step(v.tensor_tensor(comb3, t0[:], t1[:], ALU.add))
                if experts > routed:
                    step(v.memset(comb[:, routed * NT:experts * NT], 1.0))
                if not gated:
                    for half in range(NHALF):
                        v.wait_ge(comb_turned, half + 1)
                        v.tensor_copy(combT[:, half * BANK:(half + 1) * BANK], ps[0:routed, half, :]).then_inc(comb_sb, 1)
                    for q in range(NT // 2):
                        v.wait_ge(bias_ps, q + 1)
                        v.tensor_tensor(X[:, 2 * q:2 * q + 2, :], X[:, 2 * q:2 * q + 2, :],
                                        ps[:, 4 + q, 0:2 * C].rearrange("p (a c) -> p a c", a=2), ALU.add).then_inc(bias_added, 1)
                    v.wait_ge(bias_added, NT // 2)
                step(v.tensor_scalar(combs[:, :], comb[:, :], 1 / WS, None, ALU.mult))
                with v.Fori(0, PAIRS) as i:
                    def hidden(u):
                        v.wait_ge(down, i * 2 * NT + 4 * max(u - 1, 0))
                        for f in range(tiles):
                            m = u * tiles + f
                            v.wait_ge(activated, i * MI + m + 1)
                            if gated:
                                v.scalar_tensor_tensor(h32[:, m % 2, :], ps[:, 2 * (m % 2) + 1, :], 1 / (XS * WS), act_out[:, m % 4, :],
                                                       ALU.mult, ALU.mult).then_inc(h_part, 1)
                                v.wait_ge(h_part, (i * MI + m) * HP + 1)
                                src = h32[:, m % 2, :]
                            else:
                                src = act_out[:, m % 4, :]
                            v.tensor_copy(h_hi[:, u % 2, f, :], src).then_inc(h_part, 1)
                            v.wait_ge(h_part, (i * MI + m + 1) * HP)
                            v.tensor_tensor(h_lo[:, u % 2, f, :], src, h_hi[:, u % 2, f, :], ALU.subtract).then_inc(h_done, 1)
                            if gated:
                                v.wait_ge(h_done, i * MI + m)
                            if (u, f) in splits:
                                split(i, *splits[u, f])

                    def accumulate(u):
                        for t in range(4):
                            n = 4 * u + t
                            tok = 4 * (u % 2) + t
                            v.wait_ge(down, i * 2 * NT + n + 1)
                            v.wait_ge(acc, i * 2 * NT + max(n - 7, 0))
                            v.scalar_tensor_tensor(X[:, tok, :], ps[:, 4 + t, 0:C],
                                                   combs[:, ds(i * 2 * NT + (u // 2) * NT + tok, 1)], X[:, tok, :],
                                                   ALU.mult, ALU.add).then_inc(acc, 1)

                    for u in range(4):
                        hidden(u)
                        if u >= 1:
                            accumulate(u - 1)
                    accumulate(3)
                v.wait_ge(acc, PAIRS * 2 * NT)

            @block.scalar
            def _(act):
                def split(a, part):
                    if part == 0 and not gated:
                        act.activation(b_up[a][:, :], st_b[a][:, :], ACT.Copy).then_inc(b_copied, 1)
                    hi, st = ((wa_hi[a][:, :], st_up[a][:, 0:NU]), (wb[a][:, :], st_up[a][:, NU:2 * NU]),
                              (wd_hi[a][:, :], st_dn[a][:, :]))[part]
                    act.activation(hi, st, ACT.Copy, scale=WS).then_inc(split_hi, 1)

                ln.scalar(act, use)
                tr.scalar(act, use - 3, uT, ps)
                for half in range(NHALF):
                    at = slice(half * BANK, (half + 1) * BANK)
                    act.wait_ge(x_turned, half + 1)
                    act.activation(xa_hi[:, at], ps[:, 4 + half, :], ACT.Copy, scale=XS).then_inc(x_hi, 1)
                    act.activation(xb_hi[:, at], ps[:, 6 + half, :], ACT.Copy, scale=XS).then_inc(x_hi, 1)
                act.wait_ge(w_ready[0], 16 * WD)
                for part in range(SP):
                    split(0, part)
                if gated:
                    act.wait_ge(route, 2)
                    act.activation(lg[:], lg[:], ACT.Exp).then_inc(route_act, 1)
                else:
                    act.wait_ge(route, 3)
                    act.activation(wts[:, :, 1], wts[:, :, 1], ACT.Exp).then_inc(route_act, 1)
                with act.Fori(0, PAIRS) as i:
                    for u in range(4):
                        a = u // 2
                        for f in range(tiles):
                            m = u * tiles + f
                            act.wait_ge(up, i * MI + m + 1)
                            act.wait_ge(h_done, i * MI + max(m - 3, 0))
                            act.activation(act_out[:, m % 4, :], ps[:, 2 * (m % 2) if gated else m % 4, :], ACT.Silu if gated else ACT.Gelu,
                                           scale=1 / (XS * WS), bias=0.0 if gated else b_up[a][:, f:f + 1]).then_inc(activated, 1)
                            if (u, f) in splits:
                                b, part, _ = splits[u, f]
                                if part == 0:
                                    act.wait_ge(w_ready[b], (i + 2 - b) * 16 * WD)
                                    act.wait_ge(split_lo, i * 2 * SP + (2 - b) * SP)
                                    act.wait_ge(activated, i * MI + 2 * tiles * (1 - b))
                                if part < 2:
                                    act.wait_ge(up, i * MI + 2 * tiles * (1 - b))
                                else:
                                    act.wait_ge(down, i * 2 * NT + 2 * 4 * (1 - b))
                                split(b, part)

            @block.tensor
            def _(pe):
                tr.tensor(pe, use - 3, ln, use, U, ps, K["ident"])
                pe.wait_ge(doubled, 2)
                for half in range(NHALF):
                    for t in range(4):
                        tok = 4 * half + t
                        at = slice(t * P, (t + 1) * P)
                        pe.transpose(ps[:, 4 + half, at], U[:, tok, 0:CA], K["ident"][:, :])
                        mm = pe.transpose(ps[:, 6 + half, at], U2[:, tok, :], K["ident"][:, :])
                    mm.then_inc(x_turned, 1)
                tr.wait(pe, use - 3)
                pe.wait_ge(loaded, 32 if gated else 48)
                pe.wait_ge(x_lo, 4)
                for t in range(NT):
                    for c in range(2):
                        mm = pe.matmul(ps[:, 4, t * routed:(t + 1) * routed], uT[:, c, t * P:(t + 1) * P],
                                       gate[:, c * routed:(c + 1) * routed], start=(c == 0), stop=(c == 1))
                mm.then_inc(logits, 1)
                if not gated:
                    pe.wait_ge(route, 11)
                    for t in range(NT):
                        mm = pe.transpose(ps[0:routed, t // 4, (t % 4) * P:(t % 4 + 1) * P], comb3[:, t, :], K["ident"][:, :])
                        if t % 4 == 3:
                            mm.then_inc(comb_turned, 1)
                    pe.wait_ge(comb_sb, 2)
                    for t in range(NT):
                        mm = pe.matmul(ps[:, 4 + t // 2, (t % 2) * C:(t % 2 + 1) * C], combT[:, t * P:(t + 1) * P], bo[:, :],
                                       start=True, stop=True)
                        if t % 2:
                            mm.then_inc(bias_ps, 1)
                    pe.wait_ge(bias_added, NT // 2)
                else:
                    pe.wait_ge(route, 2)
                with pe.Fori(0, PAIRS) as i:
                    def up_unit(u):
                        a, half = divmod(u, 2)
                        at = slice(half * BANK, (half + 1) * BANK)
                        if half == 0:
                            pe.wait_ge(split_lo, i * 2 * SP + SP + 2 * a)
                        for f in range(tiles):
                            m = u * tiles + f
                            if gated:
                                pe.wait_ge(h_part, i * MI * HP + max(2 * m - 3, 0))
                            else:
                                pe.wait_ge(activated, i * MI + max(m - 3, 0))
                            for w in range(WU):
                                out = ps[:, 2 * (m % 2) + w if gated else m % 4, :]
                                col = slice((w * tiles + f) * P, (w * tiles + f + 1) * P)
                                pe.matmul(out, wa_hi[a][:, col], xa_hi[:, at], start=True, stop=False)
                                pe.matmul(out, wa_hi[a][:, col], xa_lo[:, at], start=False, stop=False)
                                pe.matmul(out, wa_lo[a][:, col], xa_hi[:, at], start=False, stop=False)
                                pe.matmul(out, wb[a][:, col], xb_hi[:, at], start=False, stop=False)
                                mm = pe.matmul(out, wb[a][0:CB, col], xb_lo[:, at], start=False, stop=True)
                            mm.then_inc(up, 1)

                    def down_unit(u):
                        a, half = divmod(u, 2)
                        if half == 0 and a == 1:
                            pe.wait_ge(split_lo, i * 2 * SP + 2 * SP)
                        pe.wait_ge(h_done, i * MI + (u + 1) * tiles)
                        for t in range(4):
                            pe.wait_ge(acc, i * 2 * NT + max(4 * u + t - 3, 0))
                            out = ps[:, 4 + t, 0:C]
                            for f in range(tiles):
                                tok, col = slice(t * P, (t + 1) * P), slice(f * C, (f + 1) * C)
                                pe.matmul(out, h_hi[:, u % 2, f, tok], wd_hi[a][:, col], start=(f == 0), stop=False)
                                pe.matmul(out, h_hi[:, u % 2, f, tok], wd_lo[a][:, col], start=False, stop=False)
                                mm = pe.matmul(out, h_lo[:, u % 2, f, tok], wd_hi[a][:, col], start=False, stop=(f == tiles - 1))
                            mm.then_inc(down, 1)

                    for u in range(4):
                        up_unit(u)
                        if u >= 1:
                            down_unit(u - 1)
                    down_unit(3)


def attention_layer(nc, K, X, D, ln, tr, use):
    with ExitStack() as stack:
        ctx = Ctx(nc, stack)
        U = ctx.sb("a_U", [P, NT, C])
        uT = ctx.sb("a_uT", [CH, 2, T])
        wqk = ctx.sb("a_wqk", [CH, 2, 4 * CH])
        wv = ctx.sb("a_wv", [CH, 2, C])
        wo = ctx.sb("a_wo", [CH, 2, C])
        bqk = ctx.sb("a_bqk", [CH, 4])
        rows = ctx.sb("a_rows", [P, 2, C])
        qk = ctx.sb("a_qk", [CH, 4, T])
        vt = ctx.sb("a_v", [P, NT, C])
        nm = ctx.sb("a_nm", [P, NT])
        sums = ctx.sb("a_sums", [P, NT])
        rs = ctx.sb("a_rs", [P, NT])
        Pr = ctx.sb("a_P", [P, 2, QT, L])
        Pn = ctx.sb("a_Pn", [P, 2, QT, L])
        PT = ctx.sb("a_PT", [P, 2, QT, L])
        OT = ctx.sb("a_OT", [CH, 2, 2, L])
        ps = ctx.ps("ps_l5", [P, 8, BANK])
        S = lambda n: ctx.sem(f"l5_{n}")
        loaded, biased, proj, evac, vals, v_sb = S("loaded"), S("biased"), S("proj"), S("evac"), S("vals"), S("v_sb")
        scores, peak, expd, norm, normed, turned, turned_sb, out_ps, out_sb, res_ps, res = (
            S("scores"), S("peak"), S("expd"), S("norm"), S("normed"), S("turned"), S("turned_sb"), S("out_ps"), S("out_sb"),
            S("res_ps"), S("res"))

        with nc.Block() as block:
            @block.sync
            def _(sync):
                for dst, src in ((wqk, "a_wqk"), (wv, "a_wv"), (wo, "a_wo"), (bqk, "a_bqk")):
                    sync.dma_start(dst[:], D[src]).then_inc(loaded, 16)
                sync.dma_start(rows[:], D["a_rows"].partition_broadcast(P)).then_inc(loaded, 16)

            @block.vector
            def _(v):
                ln.vector(v, use, X, U, 1e-5)
                v.wait_ge(ln.out, NT * (use + 1))
                v.wait_ge(loaded, 80)
                v.tensor_tensor(X[:], X[:], rows[:, 1, :].unsqueeze(1).broadcast_to([P, NT, C]), ALU.add).then_inc(biased, 1)
                v.tensor_scalar(bqk[:, 0:2], bqk[:, 0:2], C ** -0.5, None, ALU.mult).then_inc(biased, 1)
                for q in range(NT // 2):
                    v.wait_ge(vals, q + 1)
                    v.tensor_tensor(vt[:, 2 * q:2 * q + 2, :], ps[:, 4 + q, 0:2 * C].rearrange("p (a c) -> p a c", a=2),
                                    rows[:, 0, :].unsqueeze(1).broadcast_to([P, 2, C]), ALU.add).then_inc(v_sb, 1)
                v.wait_ge(biased, 2)
                for n in range(NB + 2):
                    if n < NB:
                        b = n
                        v.wait_ge(scores, b + 1)
                        v.tensor_reduce(nm[:, 2 * b:2 * b + 2], ps[:, b % 2, :].rearrange("p (q k) -> p q k", q=QT), AX.X, ALU.max,
                                        negate=True).then_inc(peak, 1)
                    if 1 <= n <= NB:
                        b = n - 1
                        v.wait_ge(expd, 2 * b + 2)
                        v.reciprocal(rs[:, 2 * b:2 * b + 2], sums[:, 2 * b:2 * b + 2]).then_inc(norm, 1)
                        v.wait_ge(norm, b + 1)
                        if b >= 2:
                            v.wait_ge(turned, b - 1)
                        for q in range(QT):
                            v.tensor_scalar(Pn[:, b % 2, q, :], Pr[:, b % 2, q, :], rs[:, 2 * b + q:2 * b + q + 1], None,
                                            ALU.mult).then_inc(normed, 1)
                        v.wait_ge(turned, b + 1)
                        if b >= 2:
                            v.wait_ge(out_ps, b - 1)
                        v.tensor_copy(PT[:, b % 2, :, :], ps[:, 2 + b % 2, :].rearrange("p (k q) -> p k q", k=QT)).then_inc(turned_sb, 1)
                    if n >= 2:
                        b = n - 2
                        v.wait_ge(res_ps, b + 1)
                        v.tensor_tensor(X[:, 2 * b:2 * b + 2, :], X[:, 2 * b:2 * b + 2, :],
                                        ps[:, 6 + b % 2, 0:2 * C].rearrange("p (a c) -> p a c", a=2), ALU.add).then_inc(res, 1)

            @block.scalar
            def _(act):
                ln.scalar(act, use)
                tr.scalar(act, use - 3, uT, ps)
                act.wait_ge(biased, 2)
                for o in range(4):
                    for half in range(NHALF):
                        n = 2 * o + half
                        act.wait_ge(proj, n + 1)
                        act.activation(qk[:, o, half * BANK:(half + 1) * BANK], ps[0:CH, n % 4, :], ACT.Identity,
                                       scale=C ** -0.5 if o < 2 else 1.0, bias=bqk[:, o:o + 1]).then_inc(evac, 1)
                for n in range(NB + 1):
                    if n < NB:
                        b = n
                        act.wait_ge(peak, b + 1)
                        if b >= 2:
                            act.wait_ge(normed, 2 * b - 2)
                        for q in range(QT):
                            act.activation(Pr[:, b % 2, q, :], ps[:, b % 2, q * L:(q + 1) * L], ACT.Exp,
                                           bias=nm[:, 2 * b + q:2 * b + q + 1],
                                           accum_out=sums[:, 2 * b + q:2 * b + q + 1]).then_inc(expd, 1)
                    if n >= 1:
                        b = n - 1
                        act.wait_ge(out_ps, b + 1)
                        if b >= 2:
                            act.wait_ge(res_ps, b - 1)
                        act.activation(OT[:, b % 2, :, :], ps[0:CH, 4 + b % 2, :].rearrange("p (c t) -> p c t", c=2),
                                       ACT.Copy).then_inc(out_sb, 1)

            @block.tensor
            def _(pe):
                tr.tensor(pe, use - 3, ln, use, U, ps, K["ident"])
                tr.wait(pe, use - 3)
                pe.wait_ge(loaded, 80)
                for o in range(4):
                    for half in range(NHALF):
                        n = 2 * o + half
                        if n >= 4:
                            pe.wait_ge(evac, n - 3)
                        for c in range(2):
                            mm = pe.matmul(ps[0:CH, n % 4, :], wqk[:, c, o * CH:(o + 1) * CH], uT[:, c, half * BANK:(half + 1) * BANK],
                                           start=(c == 0), stop=(c == 1))
                        mm.then_inc(proj, 1)
                for t in range(NT):
                    for c in range(2):
                        mm = pe.matmul(ps[:, 4 + t // 2, (t % 2) * C:(t % 2 + 1) * C], uT[:, c, t * P:(t + 1) * P], wv[:, c, :],
                                       start=(c == 0), stop=(c == 1))
                    if t % 2:
                        mm.then_inc(vals, 1)
                pe.wait_ge(evac, 8)
                pe.wait_ge(v_sb, NT // 2)
                for n in range(NB + 1):
                    if n < NB:
                        b = n
                        if b >= 2:
                            pe.wait_ge(expd, 2 * b - 2)
                        for q in range(QT):
                            for c in range(2):
                                mm = pe.matmul(ps[:, b % 2, q * L:(q + 1) * L], qk[:, c, b * L + q * P:b * L + (q + 1) * P],
                                               qk[:, 2 + c, b * L:(b + 1) * L], start=(c == 0), stop=(c == 1))
                        mm.then_inc(scores, 1)
                    if n >= 1:
                        b = n - 1
                        pe.wait_ge(normed, 2 * b + 2)
                        if b >= 2:
                            pe.wait_ge(turned_sb, b - 1)
                        for k in range(QT):
                            for q in range(QT):
                                mm = pe.transpose(ps[:, 2 + b % 2, k * L + q * P:k * L + (q + 1) * P],
                                                  Pn[:, b % 2, q, k * P:(k + 1) * P], K["ident"][:, :])
                        mm.then_inc(turned, 1)
                        pe.wait_ge(turned_sb, b + 1)
                        if b >= 2:
                            pe.wait_ge(out_sb, b - 1)
                        for c in range(2):
                            for k in range(QT):
                                mm = pe.matmul(ps[0:CH, 4 + b % 2, c * L:(c + 1) * L], vt[:, 2 * b + k, c * CH:(c + 1) * CH],
                                               PT[:, b % 2, k, :], start=(k == 0), stop=(k == QT - 1))
                        mm.then_inc(out_ps, 1)
                        pe.wait_ge(out_sb, b + 1)
                        if b >= 2:
                            pe.wait_ge(res, b - 1)
                        for q in range(QT):
                            for c in range(2):
                                mm = pe.matmul(ps[:, 6 + b % 2, q * C:(q + 1) * C], OT[:, b % 2, c, q * P:(q + 1) * P], wo[:, c, :],
                                               start=(c == 0), stop=(c == 1))
                        mm.then_inc(res_ps, 1)


LAYERS = 6


def program(nc, D, out):
    with ExitStack() as stack:
        ctx = Ctx(nc, stack)
        X = ctx.sb("X", [P, NT, C])
        K = {"ident": ctx.sb("ident", [P, P]), "identb": ctx.sb("identb", [P, P], BF16)}
        constants = ctx.sem("constants")
        with nc.Block() as block:
            @block.sync
            def _(sync):
                sync.dma_start(K["ident"][:, :], D["ident"]).then_inc(constants, 16)

            @block.vector
            def _(v):
                v.wait_ge(constants, 16)
                v.tensor_copy(K["identb"][:, :], K["ident"][:, :]).then_inc(constants, 1)
        scan_layer(nc, K, X, D)
        if LAYERS > 1:
            neighbour_layer(nc, K, X, D)
        ln = LayerNorm(ctx)
        tr = Turned(ctx)
        if LAYERS > 2:
            quantised_layer(nc, K, X, D, ln)
        if LAYERS > 3:
            expert_layer(nc, K, X, D, ln, tr, "m", 3, 18, 16, 4, True)
        if LAYERS > 4:
            attention_layer(nc, K, X, D, ln, tr, 4)
        if LAYERS > 5:
            expert_layer(nc, K, X, D, ln, tr, "g", 5, 8, 8, 6, False)
        stored = ctx.sem("stored")
        with nc.Block() as block:
            @block.sync
            def _(sync):
                for t in range(NT):
                    sync.dma_start(out[t * P:(t + 1) * P, :], X[:, t, :]).then_inc(stored, 16)
                sync.wait_ge(stored, 16 * NT)


def _layouts(i):
    import numpy as np
    g = lambda n: np.asarray(i[n])
    con = np.ascontiguousarray
    halves = lambda a: con(a.reshape(2, CH, -1).transpose(1, 0, 2))
    o = {}
    x = g("x").reshape(T, C)
    o["x"] = con(x)
    o["xT"] = halves(x.T)
    o["w_in"] = halves(g("L0_conv_in_proj_w").T)
    o["cw"] = con(g("L0_conv_conv_w").reshape(DI, 9))
    o["cb"] = con(g("L0_conv_conv_b").reshape(DI, 1))
    xp = g("L0_conv_x_proj_w")
    o["wdt"] = con(xp[:, :RK].transpose(2, 0, 1))
    o["wB"] = con(np.repeat(xp[:, RK:RK + NS], CG, axis=1).transpose(2, 0, 1))
    o["wC"] = con(np.repeat(xp[:, RK + NS:], CG, axis=1).transpose(2, 0, 1))
    o["dtw"] = con(g("L0_conv_dt_projs_w").transpose(2, 0, 1))
    o["dtb"] = con(g("L0_conv_dt_projs_b").T)
    o["Alog"] = con(g("L0_conv_A_logs").reshape(KD, NG, CG, NS).transpose(3, 2, 0, 1).reshape(P, KD * NG))
    o["Dk"] = con(g("L0_conv_Ds").reshape(KD, DI).T)
    o["out_g"] = con(g("L0_conv_out_norm_g").reshape(DI, 1))
    o["out_b"] = con(g("L0_conv_out_norm_b").reshape(DI, 1))
    o["w_out0"] = con(g("L0_conv_out_proj_w").T)
    def padded_heads(w):
        z = np.zeros((C, 3, HG, 32), w.dtype)
        z[..., :HE] = w.reshape(C, 3, HG, HE)
        return z.reshape(2, CH, 3, P).transpose(1, 0, 2, 3)
    w = g("L1_conv_w_qkv")
    o["n_wqk"] = con(np.concatenate([padded_heads(w[:, :C]), padded_heads(w[:, C:2 * C])], axis=2))
    o["n_wv"] = halves(w[:, 2 * C:])
    o["n_wo"] = halves(g("L1_conv_w_out"))
    w = g("L2_attn_w_qkv").T
    o["q_wqk"] = con(np.concatenate([padded_heads(w[:, :C]), padded_heads(w[:, C:2 * C])], axis=2).reshape(CH, -1))
    o["q_wv"] = halves(w[:, 2 * C:]).reshape(CH, -1)
    o["q_wp"] = halves(g("L2_attn_w_proj").T).reshape(CH, -1)
    o["q_w1"] = halves(g("L2_attn_w_fc1").T).reshape(CH, -1)
    o["q_w2"] = con(g("L2_attn_w_fc2").T.reshape(FT, P, C).transpose(1, 0, 2).reshape(P, -1))
    o["q_scales"] = con(g("L2_attn_scales"))
    bq = g("L2_attn_b_qkv")
    z = np.zeros((2, 3, HG, 32), bq.dtype)
    z[..., :HE] = bq[:2 * C].reshape(2, 3, HG, HE)
    o["q_bqk"] = con(z.reshape(6, P).T)
    o["q_b1"] = con(g("L2_attn_b_fc1").reshape(FT, P).T)
    o["q_rows"] = con(np.stack([g("L2_attn_g1"), g("L2_attn_beta1"), g("L2_attn_g2"), g("L2_attn_beta2"), bq[2 * C:],
                                g("L2_attn_b_proj"), g("L2_attn_b_fc2")]))
    w1 = np.concatenate([g("L2_ffn_w1"), g("L2_ffn_sw1").reshape(2, -1, C)])
    w3 = np.concatenate([g("L2_ffn_w3"), g("L2_ffn_sw3").reshape(2, -1, C)])
    w2 = np.concatenate([g("L2_ffn_w2"), g("L2_ffn_sw2").reshape(C, 2, -1).transpose(1, 0, 2)])
    def first_weights(*ws):
        w = np.concatenate(ws, axis=1).transpose(0, 2, 1)
        w = np.concatenate([w[:, :CA], np.concatenate([w[:, CA:], w[:, CA:]], axis=1)], axis=2)
        return con(again(w).reshape(-1, w.shape[2]))
    again = lambda w: np.concatenate([w, w[:2]])
    E, F = w1.shape[:2]
    o["m_up"] = first_weights(w1, w3)
    o["m_dn"] = con(again(w2).transpose(0, 2, 1).reshape(E + 2, F // P, P, C).transpose(0, 2, 1, 3).reshape((E + 2) * P, -1))
    o["m_gate"] = halves(g("L2_ffn_gate_w").T).reshape(CH, -1)
    w = g("L3_attn_w_qkv")
    o["a_wqk"] = halves(w[:, :2 * C])
    o["a_wv"] = halves(w[:, 2 * C:])
    o["a_wo"] = halves(g("L3_attn_w_out"))
    bq = g("L3_attn_b_qkv")
    o["a_bqk"] = con(bq[:2 * C].reshape(4, CH).T)
    o["a_rows"] = con(np.stack([bq[2 * C:], g("L3_attn_b_out")]))
    wi = g("L3_ffn_Wi")
    E, F = wi.shape[:2]
    o["g_up"] = first_weights(wi)
    o["g_dn"] = con(again(g("L3_ffn_Wo")).transpose(0, 2, 1).reshape(E + 2, F // P, P, C).transpose(0, 2, 1, 3).reshape((E + 2) * P, -1))
    o["g_b"] = con(again(g("L3_ffn_bi")).reshape(E + 2, F // P, P).transpose(0, 2, 1).reshape((E + 2) * P, -1))
    o["g_bo"] = con(g("L3_ffn_bo"))
    o["g_gate"] = halves(g("L3_ffn_Wr").T).reshape(CH, -1)
    o["iota"] = con(np.tile(np.arange(16, dtype=np.float32), (P, 1)))
    ch = np.arange(CH)
    p = np.arange(P)
    f = lambda a: con(a.astype(np.float32))
    o["group"] = f((ch[:, None] // 6 == ch[None, :] // 6) / np.float32(6))
    o["avg"] = f(np.ones((DI, DI)) / DI)
    o["selT"] = f((ch[:, None, None] == CG * np.arange(NG)[None, :, None] + p[None, None, :] % CG).transpose(2, 1, 0))
    o["sel"] = f(ch[:, None, None] % SG == CG * np.arange(SG // CG)[None, :, None] + p[None, None, :] % CG).reshape(CH, -1)
    o["ident"] = f(np.eye(P))
    start = np.clip(np.arange(HW) - HK // 2, 0, HW - HK)
    near = (np.arange(HW)[None, :] >= start[:, None]) & (np.arange(HW)[None, :] < start[:, None] + HK)
    inside = (near[:, None, :, None] & near[None, :, None, :]).reshape(QT, P, L)
    o["n_mask"] = f(np.where(inside, 0, -1e30).transpose(1, 0, 2))
    return o


def kernel(**inputs):
    import numpy as _np
    import concourse.bacc as _bacc
    from concourse.bass_utils import run_bass_kernel_spmd as _run

    nc = _bacc.Bacc("TRN2", target_bir_lowering=False, num_devices=1)
    arrays = _layouts(inputs)
    D = {n: nc.dram_tensor(f"in_{n}", a.shape, mybir.dt.from_np(a.dtype), kind="ExternalInput").ap()
         for n, a in arrays.items()}
    out = nc.dram_tensor("out", (T, C), F32, kind="ExternalOutput").ap()
    program(nc, D, out)
    r = _run(nc, [{f"in_{n}": a for n, a in arrays.items()}], core_ids=[0])
    return r.results[0]["out"].reshape(NB, HW, HW, C)
```

```python
import concourse.bass as bass
from concourse import mybir
from contextlib import ExitStack

F32 = mybir.dt.float32
BF16 = mybir.dt.bfloat16
F16 = mybir.dt.float16
I16 = mybir.dt.int16
I32 = mybir.dt.int32
U32 = mybir.dt.uint32
ALU = mybir.AluOpType
ACT = mybir.ActivationFunctionType
AX = mybir.AxisListType
ds = bass.ds

NB = 4
HW = 16
L = HW * HW
T = NB * L
C = 192
P = 128
CH = C // 2
NT = T // P
BANK = 512
NHALF = T // BANK
MAGIC = 12582912.0


class Ctx:

    def __init__(self, nc, stack):
        self.nc, self.stack, self.sems = nc, stack, []

    def sb(self, name, shape, dt=F32):
        return self.stack.enter_context(self.nc.sbuf_tensor(name, shape, dt))

    def ps(self, name, shape, dt=F32):
        return self.stack.enter_context(self.nc.psum_tensor(name, shape, dt))

    def sem(self, name):
        self.sems.append(self.stack.enter_context(self.nc.semaphore(name)))
        return self.sems[-1]

    def clear(self):
        with self.nc.Block() as block:
            @block.sync
            def _(sync):
                for s in self.sems:
                    sync.sem_clear(s)


class Chain:

    def __init__(self, eng, sem):
        self.eng, self.sem, self.base, self.k = eng, sem, 0, 0

    def __call__(self, ins):
        ins.then_inc(self.sem, 1)
        self.k += 1
        self.eng.wait_ge(self.sem, self.base + self.k)

    def loop(self, i, steps):
        self.start, self.base, self.k, self.steps = self.k, self.k + i * steps, 0, steps

    def end(self, times):
        assert self.k == self.steps, (self.k, self.steps)
        self.base, self.k = 0, self.start + times * self.steps


class GroupNorm:
    N = 2 * NB

    def __init__(self, ctx, pre, buffers=None):
        s = lambda n: ctx.sem(f"{pre}_{n}")
        self.stats, self.gmean, self.spread, self.gvar = s("gn_stats"), s("gn_gmean"), s("gn_spread"), s("gn_gvar")
        self.var, self.std, self.scale, self.out = s("gn_var"), s("gn_std"), s("gn_scale"), s("gn_out")
        sb = lambda n, sh: (buffers or ctx).sb(f"{pre}_{n}", sh)
        self.st = sb("gn_st", [CH, self.N, 6])
        self.mv = sb("gn_mv", [CH, self.N, 2])
        self.gm = sb("gn_gm", [CH, self.N])
        self.d = sb("gn_d", [CH, self.N])
        self.e = sb("gn_e", [CH, self.N])
        self.sd = sb("gn_sd", [CH, self.N])
        self.rs = sb("gn_rs", [CH, self.N])

    def vector(self, v, src, dst, ps, ready):
        N = self.N
        for i in range(N):
            h, b = divmod(i, NB)
            ready(v, i)
            v.bn_stats(self.st[:, i, :], src[:, h, b * L:(b + 1) * L]).then_inc(self.stats, 1)
        for i in range(N):
            v.wait_ge(self.stats, i + 1)
            v.bn_aggr(self.mv[:, i, :], self.st[:, i, :]).then_inc(self.stats, 1)
        v.wait_ge(self.gmean, 1)
        v.tensor_copy(self.gm[:, :], ps[:, 0:N]).then_inc(self.spread, 1)
        v.wait_ge(self.spread, 1)
        v.tensor_tensor(self.d[:, :], self.mv[:, :, 0], self.gm[:, :], ALU.subtract).then_inc(self.spread, 1)
        v.wait_ge(self.spread, 2)
        v.tensor_tensor(self.e[:, :], self.d[:, :], self.d[:, :], ALU.mult).then_inc(self.spread, 1)
        v.wait_ge(self.spread, 3)
        v.tensor_tensor(self.e[:, :], self.e[:, :], self.mv[:, :, 1], ALU.add).then_inc(self.spread, 1)
        v.wait_ge(self.gvar, 1)
        v.tensor_scalar(self.sd[:, :], ps[:, N:2 * N], 1e-5, None, ALU.add).then_inc(self.var, 1)
        v.wait_ge(self.std, 1)
        v.reciprocal(self.rs[:, :], self.sd[:, :]).then_inc(self.scale, 1)
        v.wait_ge(self.scale, 1)
        for i in range(N):
            h, b = divmod(i, NB)
            v.tensor_scalar(dst[:, h, b * L:(b + 1) * L], src[:, h, b * L:(b + 1) * L],
                            self.gm[:, i:i + 1], self.rs[:, i:i + 1], ALU.subtract, ALU.mult).then_inc(self.out, 1)

    def tensor(self, pe, group, ps):
        N = self.N
        pe.wait_ge(self.stats, 2 * N)
        pe.matmul(ps[:, 0:N], group[:, :], self.mv[:, :, 0], start=True, stop=True).then_inc(self.gmean, 1)
        pe.wait_ge(self.spread, 4)
        pe.matmul(ps[:, N:2 * N], group[:, :], self.e[:, :], start=True, stop=True).then_inc(self.gvar, 1)

    def scalar(self, act):
        act.wait_ge(self.var, 1)
        act.activation(self.sd[:, :], self.sd[:, :], ACT.Sqrt).then_inc(self.std, 1)


class LayerNorm:

    def __init__(self, ctx):
        self.stats, self.var, self.std, self.rstd, self.out = (
            ctx.sem(f"ln_{n}") for n in ("stats", "var", "std", "rstd", "out"))
        self.st = ctx.sb("ln_st", [P, NT, 6])
        self.mv = ctx.sb("ln_mv", [P, NT, 2])
        self.sd = ctx.sb("ln_sd", [P, NT])
        self.rs = ctx.sb("ln_rs", [P, NT])

    def vector(self, v, use, src, dst, eps, ready=None):
        if use:
            v.wait_ge(self.out, NT * use)
        for t in range(NT):
            if ready:
                ready(v, t)
            v.bn_stats(self.st[:, t, :], src[:, t, :]).then_inc(self.stats, 1)
        for t in range(NT):
            v.wait_ge(self.stats, 2 * NT * use + t + 1)
            v.bn_aggr(self.mv[:, t, :], self.st[:, t, :]).then_inc(self.stats, 1)
        v.wait_ge(self.stats, 2 * NT * (use + 1))
        v.tensor_scalar(self.sd[:, :], self.mv[:, :, 1], eps, None, ALU.add).then_inc(self.var, 1)
        v.wait_ge(self.std, use + 1)
        v.reciprocal(self.rs[:, :], self.sd[:, :]).then_inc(self.rstd, 1)
        v.wait_ge(self.rstd, use + 1)
        for t in range(NT):
            v.tensor_scalar(dst[:, t, :], src[:, t, :], self.mv[:, t, 0:1], self.rs[:, t:t + 1],
                            ALU.subtract, ALU.mult).then_inc(self.out, 1)

    def scalar(self, act, use):
        act.wait_ge(self.var, use + 1)
        act.activation(self.sd[:, :], self.sd[:, :], ACT.Sqrt).then_inc(self.std, 1)

    def done(self, eng, use, t):
        eng.wait_ge(self.out, NT * use + t + 1)


DI = C // 2
NS = 16
RK = C // 16
CG = P // NS
NG = DI // CG
KD = 4
PW = HW + 2
PR = NB * (HW + 1) + 2
OR = NB * (HW + 1)


SG = 32
NSET = DI // SG
PARTS = 3


def scan_layer(nc, const, X, D):
    with ExitStack() as stack:
        ctx = Ctx(nc, stack)
        wdt = ctx.sb("wdt", [DI, KD, RK])
        wB = ctx.sb("wB", [DI, KD, P])
        wC = ctx.sb("wC", [DI, KD, P])
        dtw = ctx.sb("dtw", [RK, KD, DI])
        dtb = ctx.sb("dtb", [DI, KD])
        Dk = ctx.sb("Dk", [DI, KD])
        Dsum = ctx.sb("Dsum", [DI, 1])
        Alog = ctx.sb("Alog", [P, KD * NG])
        Am = ctx.sb("Am", [P, KD * NG])
        sel32 = ctx.sb("sel32", [PARTS * SG, SG // CG * P])
        sel = ctx.sb("sel", [PARTS * SG, SG // CG * P], BF16)
        selT = ctx.sb("selT", [P, NG, DI])
        gamma = ctx.sb("gamma", [DI, 1])
        beta = ctx.sb("beta", [DI, 1])
        avg = ctx.sb("avg", [DI, DI])
        w_out = ctx.sb("w_out", [DI, C])
        xc = ctx.sb("xc", [DI, 2, T])
        zs = ctx.sb("zs", [DI, T])
        Bb = ctx.sb("Bb", [P, KD, T])
        Cb = ctx.sb("Cb", [P, KD, T])
        d_st = ctx.sb("d_st", [PARTS * SG, KD, NSET, T], BF16)
        du_st = ctx.sb("du_st", [PARTS * SG, KD, NSET, T], BF16)
        ps = ctx.ps("ps_l1", [P, 8, BANK])
        S = lambda n: ctx.sem(f"l1_{n}")
        loaded_x, loaded_w, loaded_p, loaded_s = S("loaded_x"), S("loaded_w"), S("loaded_p"), S("loaded_s")
        cleared, proj, padded, convd, activated, ordered = (
            S("cleared"), S("proj"), S("padded"), S("convd"), S("activated"), S("ordered"))
        dt_low, dt_low_sb, dt_full, bc_ps, bc_sb = S("dt_low"), S("dt_low_sb"), S("dt_full"), S("bc_ps"), S("bc_sb")
        sp_act, sp_vec, sp_pool, A_done = S("sp_act"), S("sp_vec"), S("sp_pool"), S("A_done")
        stacked = [S(f"stacked{b}") for b in range(2)]
        d_bc, du_bc, dA_done, dBu_done, scanned, weighted, y_added, y_out = (
            S("d_bc"), S("du_bc"), S("dA_done"), S("dBu_done"), S("scanned"), S("weighted"), S("y_added"),
            S("y_out"))
        pool_past = S("pool_past")
        fin, fin_ps, fin_act, res_ps, res = S("fin"), S("fin_ps"), S("fin_act"), S("res_ps"), S("res")
        flat = lambda a: a[:, :, :].rearrange("p k t -> p (k t)")
        B_flat, C_flat = flat(Bb), flat(Cb)
        STEPS = 2 * NG

        front = stack.enter_context(ExitStack())
        inner = Ctx(nc, front)
        xT = inner.sb("xT", [CH, 2, T])
        xn = inner.sb("xn", [CH, 2, T])
        w_in = inner.sb("w_in", [CH, 2, 2 * DI])
        group = inner.sb("group", [CH, CH])
        pad = inner.sb("pad", [DI, PR, PW])
        cw = inner.sb("cw", [DI, 9])
        cb = inner.sb("cb", [DI, 1])
        conv = inner.sb("conv", [DI, OR, HW])
        gn = GroupNorm(ctx, "l1", inner)
        with nc.Block() as block:
            @block.sync
            def _(sp_):
                for h in range(2):
                    sp_.dma_start(xT[:, h, :], D["xT"][:, h, :]).then_inc(loaded_x, 16)
                sp_.dma_start(group[:, :], D["group"]).then_inc(loaded_x, 16)
                for dst, src in ((w_in, "w_in"), (cw, "cw"), (cb, "cb")):
                    sp_.dma_start(dst[:], D[src]).then_inc(loaded_w, 16)
                for dst, src in ((wdt, "wdt"), (wB, "wB"), (wC, "wC"), (dtw, "dtw"), (dtb, "dtb")):
                    sp_.dma_start(dst[:], D[src]).then_inc(loaded_p, 16)
                for dst, src in ((Alog, "Alog"), (sel32, "sel"), (selT, "selT"), (Dk, "Dk"), (gamma, "out_g"),
                                 (beta, "out_b"), (avg, "avg"), (w_out, "w_out0")):
                    sp_.dma_start(dst[:], D[src]).then_inc(loaded_s, 16)
                for t in range(NT):
                    sp_.dma_start(X[:, t, :], D["x"][t * P:(t + 1) * P, :]).then_inc(loaded_s, 16)

            @block.gpsimd
            def _(pool):
                pool.memset(pad[:], 0.0).then_inc(cleared, 1)

            @block.vector
            def _(v):
                gn.vector(v, xT, xn, ps[0:CH, 7, :], lambda e, i: e.wait_ge(loaded_x, 48))
                v.wait_ge(loaded_w, 48)
                v.wait_ge(padded, 4)
                for n in range(9):
                    tap = pad[:, n // 3:n // 3 + OR, n % 3:n % 3 + HW]
                    if n == 0:
                        v.tensor_scalar(conv[:, :, :], tap, cw[:, 0:1], None, ALU.mult).then_inc(convd, 1)
                    else:
                        v.wait_ge(convd, n)
                        v.scalar_tensor_tensor(conv[:, :, :], tap, cw[:, n:n + 1], conv[:, :, :],
                                               ALU.mult, ALU.add).then_inc(convd, 1)
                v.wait_ge(activated, NB)
                v.tensor_copy(xc[:, 1, :].rearrange("p (b w h) -> p b h w", b=NB, w=HW),
                              xc[:, 0, :].rearrange("p (b h w) -> p b h w", b=NB, h=HW)).then_inc(ordered, 1)
                v.wait_ge(loaded_s, 16 * (8 + NT))
                v.tensor_reduce(Dsum[:, :], Dk[:, :], AX.X, ALU.add).then_inc(ordered, 1)
                v.wait_ge(A_done, 1)
                v.tensor_scalar(Am[:, :], Am[:, :], -1.0, None, ALU.mult).then_inc(ordered, 1)
                v.tensor_copy(sel[:, :], sel32[:, :]).then_inc(ordered, 1)

            @block.scalar
            def _(act):
                gn.scalar(act)
                act.wait_ge(cleared, 1)
                rows = pad[:, 1:1 + OR, 1:1 + HW].rearrange("p (b r) w -> p b r w", b=NB)
                for half in range(NHALF):
                    act.wait_ge(proj, half + 1)
                    for b in range(2):
                        act.activation(rows[:, 2 * half + b, 0:HW, :],
                                       ps[0:DI, half, b * L:(b + 1) * L].rearrange("p (h w) -> p h w", h=HW),
                                       ACT.Copy).then_inc(padded, 1)
                act.wait_ge(proj, 4)
                for half in range(NHALF):
                    act.activation(zs[:, half * BANK:(half + 1) * BANK], ps[0:DI, 2 + half, :], ACT.Silu).then_inc(padded, 1)
                act.wait_ge(convd, 9)
                cr = conv[:, :, :].rearrange("p (b r) w -> p b r w", b=NB)
                for b in range(NB):
                    act.activation(xc[:, 0, b * L:(b + 1) * L].rearrange("p (h w) -> p h w", h=HW),
                                   cr[:, b, 0:HW, :], ACT.Silu, bias=cb[:, 0:1]).then_inc(activated, 1)
                act.wait_ge(loaded_s, 16 * (8 + NT))
                act.activation(Am[:, :], Alog[:, :], ACT.Exp).then_inc(A_done, 1)

            @block.tensor
            def _(pe):
                gn.tensor(pe, group, ps[0:CH, 7, :])
                pe.wait_ge(loaded_w, 48)
                pe.wait_ge(gn.out, 8)
                for o in range(2):
                    for half in range(NHALF):
                        for h in range(2):
                            mm = pe.matmul(ps[0:DI, 2 * o + half, :], w_in[:, h, o * DI:(o + 1) * DI],
                                           xn[:, h, half * BANK:(half + 1) * BANK], start=(h == 0), stop=(h == 1))
                        mm.then_inc(proj, 1)
        front.close()

        mids = stack.enter_context(ExitStack())
        inner = Ctx(nc, mids)
        dtr = inner.sb("dtr", [RK, T])
        ab = inner.sb("ab", [DI, 2, T])
        rl = inner.sb("rl", [DI, 2, T])
        up = inner.sb("up", [DI, 2, T])
        du = inner.sb("du", [DI, 2, T])
        tmp = inner.sb("tmp", [DI, T])
        d_pt = inner.sb("d_pt", [DI, 2, PARTS, T], BF16)
        du_pt = inner.sb("du_pt", [DI, 2, PARTS, T], BF16)
        VS, AS, PS = 11, 4, 3
        MOVES = 2 * PARTS * NSET
        with nc.Block() as block:
            @block.sync
            def _(sync):
                def move(k, part, dst, src):
                    for s in range(NSET):
                        sync.dma_start(dst[part * SG:(part + 1) * SG, k, s, :],
                                       src[s * SG:(s + 1) * SG, k % 2, part, :]).then_inc(stacked[k % 2], 16)

                for k in range(KD):
                    sync.wait_ge(sp_vec, k * VS + 6)
                    move(k, 0, d_st, d_pt)
                    sync.wait_ge(sp_vec, k * VS + 8)
                    move(k, 0, du_st, du_pt)
                    sync.wait_ge(sp_vec, k * VS + 11)
                    move(k, 1, du_st, du_pt)
                    move(k, 1, d_st, d_pt)
                    if k == KD - 1:
                        sync.wait_ge(sp_vec, KD * VS + 1)
                        move(k, 2, d_st, d_pt)
                    sync.wait_ge(sp_pool, k * PS + 2)
                    move(k, 2, du_st, du_pt)
                    if k < KD - 1:
                        sync.wait_ge(sp_pool, k * PS + 3)
                        move(k, 2, d_st, d_pt)
                for b in range(2):
                    sync.wait_ge(stacked[b], KD // 2 * MOVES * 16)

            @block.gpsimd
            def _(pool):
                for k in range(KD):
                    b = k % 2
                    pool.wait_ge(sp_vec, k * VS + 6)
                    pool.tensor_tensor(ab[:, b, :], rl[:, b, :], d_pt[:, b, 0, :], ALU.subtract).then_inc(sp_pool, 1)
                    pool.wait_ge(sp_vec, k * VS + 10)
                    pool.tensor_tensor(du_pt[:, b, 2, :], up[:, b, :], du_pt[:, b, 1, :], ALU.subtract).then_inc(sp_pool, 1)
                    if k == KD - 1:
                        continue
                    pool.wait_ge(sp_vec, k * VS + 11)
                    pool.tensor_tensor(d_pt[:, b, 2, :], ab[:, b, :], d_pt[:, b, 1, :], ALU.subtract).then_inc(sp_pool, 1)

            @block.vector
            def _(v):
                step = Chain(v, sp_vec)
                for k in range(KD):
                    b = k % 2
                    v.wait_ge(sp_act, k * AS + 3)
                    if k >= 2:
                        v.wait_ge(sp_pool, (k - 1) * PS)
                        v.wait_ge(stacked[b], k // 2 * MOVES * 16)
                    step(v.tensor_scalar(up[:, b, :], ab[:, b, :], 1.0, None, ALU.add))
                    step(v.tensor_scalar(tmp[:, :], up[:, b, :], -1.0, None, ALU.add))
                    step(v.tensor_tensor(ab[:, b, :], ab[:, b, :], tmp[:, :], ALU.subtract))
                    v.wait_ge(sp_act, k * AS + 4)
                    step(v.tensor_tensor(tmp[:, :], up[:, b, :], ab[:, b, :], ALU.add))
                    step(v.tensor_tensor(rl[:, b, :], tmp[:, :], rl[:, b, :], ALU.add))
                    step(v.tensor_copy(d_pt[:, b, 0, :], rl[:, b, :]))
                    step(v.tensor_tensor(du[:, b, :], rl[:, b, :], xc[:, k % 2, :], ALU.mult))
                    step(v.tensor_copy(du_pt[:, b, 0, :], du[:, b, :]))
                    step(v.tensor_tensor(up[:, b, :], du[:, b, :], du_pt[:, b, 0, :], ALU.subtract))
                    step(v.tensor_copy(du_pt[:, b, 1, :], up[:, b, :]))
                    v.wait_ge(sp_pool, k * PS + 1)
                    step(v.tensor_copy(d_pt[:, b, 1, :], ab[:, b, :]))
                step(v.tensor_tensor(d_pt[:, b, 2, :], ab[:, b, :], d_pt[:, b, 1, :], ALU.subtract))

            @block.scalar
            def _(act):
                act.wait_ge(loaded_p, 80)
                dt = ps[0:DI, 2:4, :].rearrange("p a b -> p (a b)")
                for k in range(KD):
                    b = k % 2
                    act.wait_ge(dt_low, k + 1)
                    act.activation(dtr[:, :], ps[0:RK, 0:2, :].rearrange("p a b -> p (a b)"), ACT.Copy).then_inc(dt_low_sb, 1)
                    act.wait_ge(dt_full, k + 1)
                    if k >= 2:
                        act.wait_ge(sp_vec, (k - 1) * VS)
                        act.wait_ge(sp_pool, (k - 1) * PS)
                    act.activation(ab[:, b, :], dt, ACT.Abs, bias=dtb[:, k:k + 1]).then_inc(sp_act, 1)
                    act.activation(rl[:, b, :], dt, ACT.Relu, bias=dtb[:, k:k + 1]).then_inc(sp_act, 1)
                    act.wait_ge(sp_act, k * AS + 1)
                    act.activation(ab[:, b, :], ab[:, b, :], ACT.Exp, scale=-1.0).then_inc(sp_act, 1)
                    for j in range(2):
                        act.wait_ge(bc_ps, 4 * k + 2 * j + 2)
                        act.activation((Bb, Cb)[j][:, k, :], ps[:, 4 + 2 * j:6 + 2 * j, :].rearrange("p a b -> p (a b)"),
                                       ACT.Copy).then_inc(bc_sb, 1)
                    act.wait_ge(sp_vec, k * VS + 2)
                    act.activation(up[:, b, :], up[:, b, :], ACT.Ln).then_inc(sp_act, 1)

            @block.tensor
            def _(pe):
                pe.wait_ge(loaded_p, 80)
                for k in range(KD):
                    rhs = lambda half: xc[:, k % 2, half * BANK:(half + 1) * BANK]
                    if k >= 1:
                        pe.wait_ge(dt_low_sb, k)
                    for half in range(NHALF):
                        mm = pe.matmul(ps[0:RK, half, :], wdt[:, k, :], rhs(half), start=True, stop=True)
                    mm.then_inc(dt_low, 1)

                    def spread_rows(j, w):
                        if k >= 1:
                            pe.wait_ge(bc_sb, 2 * (k - 1) + j + 1)
                        for half in range(NHALF):
                            pe.matmul(ps[:, 4 + 2 * j + half, :], w[:, k, :], rhs(half), start=True, stop=True).then_inc(bc_ps, 1)

                    if k:
                        spread_rows(0, wB)
                    pe.wait_ge(dt_low_sb, k + 1)
                    if k >= 1:
                        pe.wait_ge(sp_act, (k - 1) * AS + 2)
                    for half in range(NHALF):
                        mm = pe.matmul(ps[0:DI, 2 + half, :], dtw[:, k, :], dtr[:, half * BANK:(half + 1) * BANK],
                                       start=True, stop=True)
                    mm.then_inc(dt_full, 1)
                    if not k:
                        spread_rows(0, wB)
                    spread_rows(1, wC)
        mids.close()

        sp = ctx.sb("sp", [DI, 4, T])
        dA = ctx.sb("dA", [P, 2, 2, T])
        dBu = ctx.sb("dBu", [P, 2, T])
        hs = ctx.sb("hs", [P, 2, T])
        hC = ctx.sb("hC", [P, 2, T])
        ysum = ctx.sb("ysum", [DI, 2, T])
        ysd = ctx.sb("ysd", [P, NT])
        yrs = ctx.sb("yrs", [P, NT, DI])
        with nc.Block() as block:
            @block.gpsimd
            def _(pool):
                starts = dA[:].rearrange("p d n (b t) -> p d n b t", t=L)
                for d in range(2):
                    for n in range(2):
                        at = 0 if d == 0 else L - 1
                        pool.memset(starts[:, d, n, :, at:at + 1], 0.0).then_inc(cleared, 1)
                with pool.Fori(0, 2) as r:
                    for m in range(STEPS):
                        pool.wait_ge(scanned, r * STEPS + m + 1)
                        pool.wait_ge(y_added, r * STEPS + max(m - 1, 0))
                        pool.sem_inc(pool_past, 1)
                        pool.tensor_tensor(hC[:, m % 2, :], hs[:, m % 2, :], C_flat[:, ds((r + 2 * (m // NG)) * T, T)],
                                           ALU.mult).then_inc(weighted, 1)

            @block.vector
            def _(v):
                with v.Fori(0, 2) as r:
                    for m in range(STEPS):
                        for half in range(NHALF):
                            u = NHALF * m + half
                            v.wait_ge(du_bc, r * NHALF * STEPS + u + 1)
                            v.tensor_tensor(dBu[:, m % 2, half * BANK:(half + 1) * BANK], ps[:, 3 + u % 3, :],
                                            B_flat[:, ds((r + 2 * (m // NG)) * T + half * BANK, BANK)],
                                            ALU.mult).then_inc(dBu_done, 1)
                        v.wait_ge(dBu_done, (r * STEPS + m + 1) * NHALF)
                        v.wait_ge(dA_done, (r * STEPS + m + 1) * NHALF)
                        v.wait_ge(weighted, r * STEPS + max(m - 1, 0))
                        step = 1 if m < NG else -1
                        v.tensor_tensor_scan(hs[:, m % 2, ::step], dA[:, m // NG, m % 2, ::step],
                                             dBu[:, m % 2, ::step], 0.0, ALU.mult, ALU.add).then_inc(scanned, 1)
                v.wait_ge(y_out, 4)
                v.scalar_tensor_tensor(sp[:, 0, :], xc[:, 0, :], Dsum[:, 0:1], ysum[:, 0, :], ALU.mult, ALU.add).then_inc(fin, 1)
                v.wait_ge(fin, 1)
                v.tensor_tensor(sp[:, 1, :].rearrange("p (b h w) -> p b h w", b=NB, h=HW),
                                sp[:, 0, :].rearrange("p (b h w) -> p b h w", b=NB, h=HW),
                                ysum[:, 1, :].rearrange("p (b w h) -> p b h w", b=NB, w=HW), ALU.add).then_inc(fin, 1)
                v.wait_ge(fin_ps, 2)
                v.tensor_tensor(sp[:, 0, :], sp[:, 1, :], ps[0:DI, 0:2, :].rearrange("p a b -> p (a b)"),
                                ALU.subtract).then_inc(fin, 1)
                v.wait_ge(fin_ps, 3)
                v.tensor_scalar(ysd[:, :], ps[:, 2, 0:NT], 1e-5, None, ALU.add).then_inc(fin, 1)
                v.wait_ge(fin_act, 2)
                v.reciprocal(ysd[:, :], ysd[:, :]).then_inc(fin, 1)
                v.wait_ge(fin, 5)
                v.tensor_copy(yrs[:, :, :], ysd[:, :].unsqueeze(2).broadcast_to([P, NT, DI])).then_inc(fin, 1)
                v.wait_ge(fin_ps, 4)
                v.tensor_tensor(sp[:, 0, :], sp[:, 0, :], ps[0:DI, 4:6, :].rearrange("p a b -> p (a b)"), ALU.mult).then_inc(fin, 1)
                v.wait_ge(fin, 7)
                v.tensor_scalar(sp[:, 1, :], sp[:, 0, :], gamma[:, 0:1], beta[:, 0:1], ALU.mult, ALU.add).then_inc(fin, 1)
                v.wait_ge(fin, 8)
                v.tensor_tensor(sp[:, 2, :], sp[:, 1, :], zs[:, :], ALU.mult).then_inc(fin, 1)
                for q in range(NT // 2):
                    v.wait_ge(res_ps, q + 1)
                    v.tensor_tensor(X[:, 2 * q:2 * q + 2, :], X[:, 2 * q:2 * q + 2, :],
                                    ps[:, 4 + q, 0:2 * C].rearrange("p (a c) -> p a c", a=2), ALU.add).then_inc(res, 1)

            @block.scalar
            def _(act):
                act.wait_ge(cleared, 5)

                def take_sums(r):
                    act.wait_ge(y_added, (r + 1) * STEPS)
                    for half in range(NHALF):
                        act.activation(ysum[:, r, half * BANK:(half + 1) * BANK], ps[0:DI, 6 + half, :], ACT.Copy).then_inc(y_out, 1)

                for n in range(2 * STEPS):
                    r, m = divmod(n, STEPS)
                    for half in range(NHALF):
                        u = NHALF * n + half
                        act.wait_ge(d_bc, u + 1)
                        if n >= 2:
                            act.wait_ge(scanned, n - 1)
                        o = 1 if m < NG else 0
                        dst = dA[:, m // NG, m % 2, half * BANK:(half + 1) * BANK].rearrange("p (b t) -> p b t", t=L)
                        src = ps[:, u % 3, :].rearrange("p (b t) -> p b t", t=L)
                        col = (r + 2 * (m // NG)) * NG + m % NG
                        act.activation(dst[:, :, o:o + L - 1], src[:, :, o:o + L - 1], ACT.Exp, scale=Am[:, col:col + 1]).then_inc(dA_done, 1)
                    if n == STEPS + 1:
                        take_sums(0)
                take_sums(1)
                act.wait_ge(fin, 3)
                act.activation(sp[:, 2, :], sp[:, 0, :], ACT.Square).then_inc(fin_act, 1)
                act.wait_ge(fin, 4)
                act.activation(ysd[:, :], ysd[:, :], ACT.Sqrt).then_inc(fin_act, 1)

            @block.tensor
            def _(pe):
                d_flat = d_st[:, :, :, :].rearrange("p k s t -> p (k s t)")
                du_flat = du_st[:, :, :, :].rearrange("p k s t -> p (k s t)")

                def spread(r, m):
                    for half in range(NHALF):
                        u = NHALF * m + half
                        g = m % NG
                        s, j = divmod(g, SG // CG)
                        at = ds((r + 2 * (m // NG)) * NSET * T + s * T + half * BANK, BANK)
                        spreading = sel[:, j * P:(j + 1) * P]
                        pe.wait_ge(dA_done, r * NHALF * STEPS + max(u - 2, 0))
                        pe.matmul(ps[:, u % 3, :], spreading, d_flat[:, at], start=True, stop=True).then_inc(d_bc, 1)
                        pe.wait_ge(dBu_done, r * NHALF * STEPS + max(u - 2, 0))
                        pe.matmul(ps[:, 3 + u % 3, :], spreading, du_flat[:, at], start=True, stop=True).then_inc(du_bc, 1)

                def add(r, m):
                    pe.wait_ge(weighted, r * STEPS + m + 1)
                    for half in range(NHALF):
                        mm = pe.matmul(ps[0:DI, 6 + half, :], selT[:, m % NG, :], hC[:, m % 2, half * BANK:(half + 1) * BANK],
                                       start=(m == 0), stop=(m == STEPS - 1))
                    mm.then_inc(y_added, 1)

                for n in range(2 * STEPS + 2):
                    if n < 2 * STEPS:
                        spread(*divmod(n, STEPS))
                    if n == STEPS + 2:
                        pe.wait_ge(y_out, 2)
                    if n >= 2:
                        add(*divmod(n - 2, STEPS))
                pe.wait_ge(fin, 2)
                pe.wait_ge(dA_done, 2 * 2 * NG * NHALF)
                for half in range(NHALF):
                    pe.matmul(ps[0:DI, half, :], avg[:, :], sp[:, 1, half * BANK:(half + 1) * BANK], start=True, stop=True).then_inc(fin_ps, 1)
                pe.wait_ge(fin_act, 1)
                pe.wait_ge(dBu_done, 2 * 2 * NG * NHALF)
                for t in range(NT):
                    mm = pe.matmul(ps[:, 2, t:t + 1], sp[:, 2, t * P:(t + 1) * P], avg[:, 0:1], start=True, stop=True)
                mm.then_inc(fin_ps, 1)
                pe.wait_ge(fin, 6)
                for t in range(NT):
                    mm = pe.matmul(ps[0:DI, 4 + t // 4, (t % 4) * P:(t % 4 + 1) * P], yrs[:, t, :], const["ident"][:, :],
                                   start=True, stop=True)
                mm.then_inc(fin_ps, 1)
                pe.wait_ge(fin, 9)
                pe.wait_ge(y_out, 4)
                for t in range(NT):
                    mm = pe.matmul(ps[:, 4 + t // 2, (t % 2) * C:(t % 2 + 1) * C], sp[:, 2, t * P:(t + 1) * P], w_out[:, :],
                                   start=True, stop=True)
                    if t % 2:
                        mm.then_inc(res_ps, 1)
        ctx.clear()


NH = 12
HE = 16
HG = 4
HK = 7
QT = L // P
KW = 12 * HW
KX = KW - P
CP = 3 * P


def neighbour_layer(nc, K, X, D):
    with ExitStack() as stack:
        ctx = Ctx(nc, stack)
        xT = ctx.sb("n_xT", [CH, 2, T])
        xn = ctx.sb("n_xn", [CH, 2, T])
        group = ctx.sb("n_group", [CH, CH])
        lowsel = ctx.sb("n_lowsel", [P, 2])
        wqk = ctx.sb("n_wqk", [CH, 2, 6, P])
        wv = ctx.sb("n_wv", [CH, 2, C])
        wo = ctx.sb("n_wo", [P, 3, C])
        maskf = ctx.sb("n_maskf", [P, QT, KW])
        mask = ctx.sb("n_mask", [P, QT, KW], BF16)
        hi = ctx.sb("n_hi", [P, 6, T], F16)
        signed = ctx.sb("n_signed", [P, 2, BANK], F16)
        lo = ctx.sb("n_lo", [P, 6, T], F16)
        qb = ctx.sb("n_qb", [P, 3, L], F16)
        kb_hi = ctx.sb("n_kb_hi", [P, 3, L], F16)
        kb_lo = ctx.sb("n_kb_lo", [P, 3, L], F16)
        vt = ctx.sb("n_v", [P, NT * CP])
        vb = ctx.sb("n_vb", [P, QT * CP])
        vx = ctx.sb("n_vx", [KX, NB * CP])
        vxb = ctx.sb("n_vxb", [KX, CP])
        nm = ctx.sb("n_nm", [P, NH, QT])
        sums = ctx.sb("n_sums", [P, NH, QT])
        rs = ctx.sb("n_rs", [P, NH, QT])
        Pr = ctx.sb("n_P", [P, 3, QT, KW])
        PT = ctx.sb("n_PT", [P, 2, 2, P])
        PX = ctx.sb("n_PX", [KX, 2, 2, P])
        OT = ctx.sb("n_OT", [P, 3, T])
        gn = GroupNorm(ctx, "l2")
        ps = ctx.ps("ps_l2", [P, 8, BANK])
        S = lambda n: ctx.sem(f"l2_{n}")
        loaded, masked, x_turned, x_sb, taken, v_taken, past = (
            S("loaded"), S("masked"), S("x_turned"), S("x_sb"), S("taken"), S("v_taken"), S("past"))
        cleared, moved = S("cleared"), S("moved")
        proj, high, signs, split, v_proj, v_sb = S("proj"), S("high"), S("signs"), S("split"), S("v_proj"), S("v_sb")
        scores, peak, expd, turned, turned_sb, summed, inverse, scaled = (
            S("scores"), S("peak"), S("expd"), S("turned"), S("turned_sb"), S("summed"), S("inverse"), S("scaled"))
        o_sb, o_proj, added = S("o_sb"), S("o_proj"), S("added")
        QS = HE ** -0.5
        PROJ = 6 * NHALF
        keys0 = (0, L - KW)

        with nc.Block() as block:
            @block.sync
            def _(sync):
                for dst, src in ((group, "group"), (wqk, "n_wqk"), (lowsel, "n_lowsel"), (wv, "n_wv"), (wo, "n_wo"), (maskf, "n_mask")):
                    sync.dma_start(dst[:], D[src]).then_inc(loaded, 16)
                sync.wait_ge(v_sb, NT // 2)
                sync.dma_start(vx[:, :].rearrange("p (b c) -> p b c", c=CP),
                               vt[P - KX:P, :].rearrange("p (b q c) -> p b q c", q=QT, c=CP)[:, :, 0, :]).then_inc(moved, 16)

            @block.gpsimd
            def _(pool):
                pool.memset(vt[:, :], 0.0).then_inc(cleared, 1)
                pool.wait_ge(loaded, 96)
                pool.tensor_copy(mask[:], maskf[:]).then_inc(masked, 1)

                def take(b, g):
                    for dst, src, o in ((qb, lo, g), (kb_hi, hi, 3 + g), (kb_lo, lo, 3 + g)):
                        pool.sem_inc(past, 1)
                        pool.tensor_copy(dst[:, g, :], src[:, :, :].rearrange("p g t -> p (g t)")[:, ds(b * L + o * T, L)]).then_inc(taken, 1)

                def take_values(b, g):
                    for dst, o, src, at in ((vb, 0, vt, b * QT), (vb, 1, vt, b * QT + 1), (vxb, 0, vx, b)):
                        pool.sem_inc(past, 1)
                        pool.tensor_copy(dst[:, o * CP + g * P:o * CP + (g + 1) * P], src[:, ds(at * CP + g * P, P)]).then_inc(v_taken, 1)

                pool.wait_ge(split, PROJ)
                for g in range(3):
                    take(0, g)
                pool.wait_ge(v_sb, NT // 2)
                pool.wait_ge(moved, 16)
                for g in range(3):
                    take_values(0, g)
                with pool.Fori(0, NB - 1) as b:
                    for g in range(3):
                        pool.wait_ge(scores, b * NH + (g + 1) * HG)
                        take(b + 1, g)
                        pool.wait_ge(summed, b * NH + (g + 1) * HG)
                        take_values(b + 1, g)

            @block.vector
            def _(v):
                gn.vector(v, xT, xn, ps[0:CH, 7, :], lambda e, i: e.wait_ge(x_sb, 2 * NHALF))
                v.wait_ge(loaded, 96)
                for n in range(PROJ):
                    o, half = divmod(n, NHALF)
                    at = slice(half * BANK, (half + 1) * BANK)
                    src = ps[:, n % 4, :]
                    v.wait_ge(high, n + 1)
                    if o < 3:
                        v.wait_ge(split, max(n - 1, 0))
                        v.tensor_scalar(signed[:, half, :], hi[:, o, at], lowsel[:, 0:1], None, ALU.mult).then_inc(signs, 1)
                        v.wait_ge(signs, n + 1)
                        v.scalar_tensor_tensor(lo[:, o, at], src, lowsel[:, 1:2], signed[:, half, :], ALU.mult, ALU.add).then_inc(split, 1)
                    else:
                        v.tensor_tensor(lo[:, o, at], src, hi[:, o, at], ALU.subtract).then_inc(split, 1)

                def copy_turned(s):
                    v.tensor_copy(PT[:, s % 2, :, :], ps[:, 3 + s % 2, 0:2 * P].rearrange("p (n q) -> p n q", n=2)).then_inc(turned_sb, 1)
                    v.tensor_copy(PX[:, s % 2, :, :], ps[0:KX, 3 + s % 2, 2 * P:4 * P].rearrange("p (n q) -> p n q", n=2)).then_inc(turned_sb, 1)

                def take_outputs(b):
                    v.wait_ge(summed, (b + 1) * NH)
                    v.tensor_copy(OT[:, :, ds(b * L, L)], ps[:, 5:7, :].rearrange("p a (g t) -> p (a g) t", t=L)[:, 0:3, :]).then_inc(o_sb, 1)

                def invert(b, h):
                    v.wait_ge(expd, (b * NH + h + 1) * QT)
                    v.reciprocal(rs[:, h, :], sums[:, h, :]).then_inc(inverse, 1)

                def slot(b, s, late):
                    v.wait_ge(scores, b * NH + s + 1)
                    v.tensor_reduce(nm[:, s, :], ps[:, s % 3, 0:QT * KW].rearrange("p (q k) -> p q k", q=QT), AX.X, ALU.max,
                                    negate=True).then_inc(peak, 1)
                    if s >= 1:
                        invert(b, s - 1)
                    elif late:
                        invert(b - 1, NH - 1)
                    if late or s >= 2:
                        v.wait_ge(turned, b * NH + s - 1)
                        v.wait_ge(summed, b * NH + (s - 3 if late else max(s - 3, 0)))
                        copy_turned(s)
                    if late and s == 2:
                        take_outputs(b - 1)

                for s in range(NH):
                    slot(0, s, False)
                with v.Fori(1, NB) as b:
                    for s in range(NH):
                        slot(b, s, True)
                invert(NB - 1, NH - 1)
                for s in (0, 1):
                    v.wait_ge(turned, NB * NH + s - 1)
                    v.wait_ge(summed, NB * NH + s - 3)
                    copy_turned(s)
                take_outputs(NB - 1)
                for n in range(NT // 2):
                    v.wait_ge(o_proj, n + 1)
                    v.tensor_tensor(X[:, 2 * n:2 * n + 2, :], X[:, 2 * n:2 * n + 2, :],
                                    ps[:, n, 0:2 * C].rearrange("p (t c) -> p t c", t=2), ALU.add).then_inc(added, 1)

            @block.scalar
            def _(act):
                for n in range(2 * NHALF):
                    act.wait_ge(x_turned, n + 1)
                    act.activation(xT[:, n % 2, (n // 2) * BANK:(n // 2 + 1) * BANK], ps[0:CH, n, :], ACT.Copy).then_inc(x_sb, 1)
                gn.scalar(act)
                for n in range(PROJ):
                    o, half = divmod(n, NHALF)
                    act.wait_ge(proj, n + 1)
                    act.activation(hi[:, o, half * BANK:(half + 1) * BANK], ps[:, n % 4, :], ACT.Copy,
                                   scale=QS if o < 3 else 1.0).then_inc(high, 1)
                act.wait_ge(cleared, 1)
                for n in range(NT // 2):
                    act.wait_ge(v_proj, n + 1)
                    act.activation(vt[:, 2 * n * CP:2 * (n + 1) * CP].rearrange("p (h e) -> p h e", e=32)[:, :, 0:HE],
                                   ps[:, 4 + n, 0:2 * C].rearrange("p (h e) -> p h e", e=HE), ACT.Copy).then_inc(v_sb, 1)

                def exponentials(b, s, late):
                    act.wait_ge(peak, b * NH + s + 1)
                    act.wait_ge(turned, b * NH + (s - 2 if late or s >= 2 else 0))
                    for q in range(QT):
                        act.activation(Pr[:, s % 3, q, :], ps[:, s % 3, q * KW:(q + 1) * KW], ACT.Exp,
                                       bias=nm[:, s, q:q + 1], accum_out=sums[:, s, q:q + 1]).then_inc(expd, 1)

                def probabilities(b, h):
                    act.wait_ge(inverse, b * NH + h + 1)
                    for q in range(QT):
                        act.activation(Pr[:, h % 3, q, :], Pr[:, h % 3, q, :], ACT.Copy, scale=rs[:, h, q:q + 1]).then_inc(scaled, 1)

                for s in range(NH):
                    exponentials(0, s, False)
                    if s >= 1:
                        probabilities(0, s - 1)
                with act.Fori(1, NB) as b:
                    for s in range(NH):
                        exponentials(b, s, True)
                        if s >= 1:
                            probabilities(b, s - 1)
                        else:
                            probabilities(b - 1, NH - 1)
                probabilities(NB - 1, NH - 1)

            @block.tensor
            def _(pe):
                for n in range(2 * NHALF):
                    for t in range(4):
                        mm = pe.transpose(ps[0:CH, n, t * P:(t + 1) * P],
                                          X[:, (n // 2) * 4 + t, (n % 2) * CH:(n % 2 + 1) * CH], K["ident"][:, :])
                    mm.then_inc(x_turned, 1)
                pe.wait_ge(loaded, 96)
                gn.tensor(pe, group, ps[0:CH, 7, :])
                pe.wait_ge(gn.out, 8)
                for n in range(PROJ):
                    o, half = divmod(n, NHALF)
                    if n >= 4:
                        pe.wait_ge(split, n - 3)
                    for c in range(2):
                        mm = pe.matmul(ps[:, n % 4, :], wqk[:, c, o, :], xn[:, c, half * BANK:(half + 1) * BANK],
                                       start=(c == 0), stop=(c == 1))
                    mm.then_inc(proj, 1)
                for t in range(NT):
                    for c in range(2):
                        mm = pe.matmul(ps[:, 4 + t // 2, (t % 2) * C:(t % 2 + 1) * C], xn[:, c, t * P:(t + 1) * P], wv[:, c, :],
                                       start=(c == 0), stop=(c == 1))
                    if t % 2:
                        mm.then_inc(v_proj, 1)
                pe.wait_ge(split, PROJ)
                pe.wait_ge(v_sb, NT // 2)
                pe.wait_ge(masked, 1)

                def score(b, h, late):
                    pe.wait_ge(expd, (b * NH + (h - 2 if late or h >= 2 else 0)) * QT)
                    if h % HG == 0:
                        pe.wait_ge(taken, b * 9 + 3 * (h // HG) + 3)
                    both, one = slice(32 * (h % HG), 32 * (h % HG + 1)), slice(32 * (h % HG), 32 * (h % HG) + HE)
                    g = h // HG
                    for q in range(QT):
                        out = ps[:, h % 3, q * KW:(q + 1) * KW]
                        qs, ks = slice(q * P, (q + 1) * P), slice(keys0[q], keys0[q] + KW)
                        pe.matmul(out, K["identb"][:, :], mask[:, q, :], start=True, stop=False)
                        pe.matmul(out, qb[both, g, qs], kb_hi[both, g, ks], start=False, stop=False)
                        mm = pe.matmul(out, qb[one, g, qs], kb_lo[one, g, ks], start=False, stop=True)
                    mm.then_inc(scores, 1)

                def turn(b, h, late):
                    pe.wait_ge(scaled, (b * NH + h + 1) * QT)
                    pe.wait_ge(turned_sb, 2 * (b * NH + (h - 1 if late or h >= 1 else 0)))
                    out = ps[:, 3 + h % 2, :]
                    src = Pr[:, h % 3, :, :]
                    pe.transpose(out[:, 0:P], src[:, 0, 0:P], K["ident"][:, :])
                    pe.transpose(out[:, P:2 * P], src[:, 1, KX:KW], K["ident"][:, :])
                    pe.transpose(out[0:KX, 2 * P:3 * P], src[:, 0, P:KW], K["ident"][:, :])
                    mm = pe.transpose(out[0:KX, 3 * P:4 * P], src[:, 1, 0:KX], K["ident"][:, :])
                    mm.then_inc(turned, 1)

                def output(b, h, late):
                    pe.wait_ge(turned_sb, 2 * (b * NH + h + 1))
                    if h % HG == 0:
                        pe.wait_ge(v_taken, b * 9 + 3 * (h // HG) + 3)
                        if late and h == 0:
                            pe.wait_ge(o_sb, b)
                    vcol = lambda t: slice(t * CP + h * 32, t * CP + (h + 1) * 32)
                    rows, g = slice(32 * (h % HG), 32 * (h % HG + 1)), h // HG
                    for q, other in ((0, vb[0:KX, vcol(1)]), (1, vxb[:, vcol(0)])):
                        out = ps[rows, 5 + g // 2, (g % 2) * L + q * P:(g % 2) * L + (q + 1) * P]
                        pe.matmul(out, vb[:, vcol(q)], PT[:, h % 2, q, :], start=True, stop=False)
                        mm = pe.matmul(out, other, PX[:, h % 2, q, :], start=False, stop=True)
                    mm.then_inc(summed, 1)

                def slot(b, s, late):
                    if s < NH:
                        score(b, s, late)
                    for stage, lag in ((turn, 2), (output, 3)):
                        if s >= lag:
                            stage(b, s - lag, late)
                        elif late:
                            stage(b - 1, s - lag + NH, True)

                for s in range(NH):
                    slot(0, s, False)
                with pe.Fori(1, NB) as b:
                    for s in range(NH):
                        slot(b, s, True)
                turn(NB - 1, NH - 2, True)
                output(NB - 1, NH - 3, True)
                turn(NB - 1, NH - 1, True)
                output(NB - 1, NH - 2, True)
                output(NB - 1, NH - 1, True)
                pe.wait_ge(o_sb, NB)
                for t in range(NT):
                    for g in range(3):
                        mm = pe.matmul(ps[:, t // 2, (t % 2) * C:(t % 2 + 1) * C], OT[:, g, t * P:(t + 1) * P], wo[:, g, :],
                                       start=(g == 0), stop=(g == 2))
                    if t % 2:
                        mm.then_inc(o_proj, 1)


FF = 4 * C
FT = FF // P
EXP_N = 30
(S_N1, S_WQKV, S_QKV, S_ATTN, S_WPROJ, S_SV, S_R1, S_N2, S_WFC1, S_ACT, S_WFC2, S_M2, S_R2) = range(13)
(K_QKV, K_ATTN, K_X0, K_BI, K_CI, K_INV, K_QB, K_CLAMP, K_NX0, K_PROJ, K_FC1, K_FC2, K_T0, K_T1, K_MAGIC, K_FLOOR) = range(16)


def quantised_layer(nc, K, X, D, ln):
    with ExitStack() as stack:
        ctx = Ctx(nc, stack)
        U = ctx.sb("q_U", [P, NT, C])
        N = ctx.sb("q_N", [P, NT, C])
        Ni = ctx.sb("q_Ni", [P, NT, C], BF16)
        nT = ctx.sb("q_nT", [CH, 2, T], BF16)
        sc = ctx.sb("q_sc", [P, 13])
        rc = ctx.sb("q_rc", [P, 13])
        kf = ctx.sb("q_kf", [P, 16])
        rows = ctx.sb("q_rows", [P, 7, C])
        bqk = ctx.sb("q_bqk", [P, 6])
        b1 = ctx.sb("q_b1", [P, FT])
        wqk_f = ctx.sb("q_wqk_f", [CH, 2 * 6 * P])
        wqk = ctx.sb("q_wqk", [CH, 2 * 6 * P], BF16)
        wv_f = ctx.sb("q_wv_f", [CH, 2 * C])
        wv = ctx.sb("q_wv", [CH, 2 * C], BF16)
        wp_f = ctx.sb("q_wp_f", [CH, 2 * C])
        w1_f = ctx.sb("q_w1_f", [CH, 2 * FF])
        w1 = ctx.sb("q_w1", [CH, 2 * FF], BF16)
        w2_f = ctx.sb("q_w2_f", [P, FT * C])
        w2 = ctx.sb("q_w2", [P, FT * C], BF16)
        qf = ctx.sb("q_qf", [P, 4, BANK])
        qk = ctx.sb("q_qk", [P, 6 * T], BF16)
        qkb = ctx.sb("q_qkb", [P, 6, L], BF16)
        vf = ctx.sb("q_vf", [P, NT, C])
        vi = ctx.sb("q_vi", [P, NT * C], BF16)
        lt = ctx.sb("q_lt", [P, 2, QT, L])
        nm = ctx.sb("q_nm", [P, 2, QT])
        xi = ctx.sb("q_xi", [P, 2, QT, L], BF16)
        qv = ctx.sb("q_qv", [P, 2, QT * L])
        qi = ctx.sb("q_qi", [P, 2, QT * L], BF16)
        ri = ctx.sb("q_ri", [P, 2, QT * L], BF16)
        e2 = ctx.sb("q_e2", [P, 2, QT, L], I16)
        zz = ctx.sb("q_zz", [P, 2, QT, L])
        ex = ctx.sb("q_ex", [P, NH, QT, L])
        sums = ctx.sb("q_sums", [P, NH, QT])
        f0 = ctx.sb("q_f0", [P, NH * QT])
        f1 = ctx.sb("q_f1", [P, NH * QT])
        fac = ctx.sb("q_fac", [P, NH, QT])
        pv = ctx.sb("q_pv", [P, 2, QT, L])
        pi = ctx.sb("q_pi", [P, 2, QT, L], BF16)
        PT = ctx.sb("q_PT", [P, 2, QT, L], BF16)
        Os = ctx.sb("q_Os", [P, NT, C])
        OT = ctx.sb("q_OT", [CH, 2, T])
        pj = ctx.sb("q_pj", [P, NT * C])
        hf = ctx.sb("q_hf", [P, 4, BANK])
        hi = ctx.sb("q_hi", [P, FT, T], BF16)
        ps = ctx.ps("ps_l3", [P, 8, BANK])
        S = lambda n: ctx.sem(f"l3_{n}")
        loaded, w_loaded, vec, w_quantised, quantised = (
            S("loaded"), S("w_loaded"), S("vec"), S("w_quantised"), S("quantised"))
        scaled, constants, normed, turned_n, n_sb = S("scaled"), S("constants"), S("normed"), S("turned_n"), S("n_sb")
        proj, evac, qk_ready, v_proj, v_ready = S("proj"), S("evac"), S("qk_ready"), S("v_proj"), S("v_ready")
        taken, pool_past = S("taken"), S("pool_past")
        scores, shifted, clipped, negmax, diff, quot, whole, rest, expo, square, expd, factor = (
            S("scores"), S("shifted"), S("clipped"), S("negmax"), S("diff"), S("quot"), S("whole"), S("rest"),
            S("expo"), S("square"), S("expd"), S("factor"))
        prob, floored, turned, turned_sb, summed, o_sb = (
            S("prob"), S("floored"), S("turned"), S("turned_sb"), S("summed"), S("o_sb"))
        o_turned, oT_sb, o_proj = S("o_turned"), S("oT_sb"), S("o_proj")
        act_past = S("act_past")
        h_steps = S("h_steps")
        up, gelu, hq, down, down_read = S("up"), S("gelu"), S("hq"), S("down"), S("down_read")
        identb = K["identb"]
        flat = lambda a: a[:, :, :].rearrange("p a b -> p (a b)")
        Os_flat = flat(Os)
        SLOTS = NH + 2

        with nc.Block() as block:
            @block.sync
            def _(sync):
                for dst, src in ((sc, "q_scales"), (rows, "q_rows"), (bqk, "q_bqk"), (b1, "q_b1")):
                    sync.dma_start(dst[:], D[src].partition_broadcast(P) if src in ("q_scales", "q_rows") else D[src]).then_inc(loaded, 16)
                for dst, src in ((wqk_f, "q_wqk"), (wv_f, "q_wv"), (wp_f, "q_wp"), (w1_f, "q_w1"), (w2_f, "q_w2")):
                    sync.dma_start(dst[:], D[src]).then_inc(w_loaded, 16)

            @block.gpsimd
            def _(pool):
                step = Chain(pool, w_quantised)
                pool.wait_ge(scaled, 1)
                pool.wait_ge(w_loaded, 80)

                def quantise(f, i, r):
                    n = f.shape[0]
                    step(pool.tensor_scalar(f[:], f[:], rc[0:n, r:r + 1], 127.0, ALU.mult, ALU.min))
                    step(pool.tensor_scalar(f[:], f[:], -128.0, MAGIC, ALU.max, ALU.add))
                    step(pool.tensor_scalar(i[:], f[:], -MAGIC, None, ALU.add))

                quantise(w1_f, w1, S_WFC1)
                quantise(w2_f, w2, S_WFC2)

                def take(b, group):
                    for o in (group, 3 + group):
                        pool.sem_inc(pool_past, 1)
                        pool.tensor_copy(qkb[:, o, :], qk[:, ds(b * L + o * T, L)]).then_inc(taken, 1)

                def powers(b, more):
                    for h in range(NH):
                        pool.wait_ge(whole, b * NH + h + 1)
                        pool.wait_ge(expd, (b * NH + max(h - 1, 0)) * QT)
                        pool.sem_inc(pool_past, 1)
                        pool.tensor_scalar(e2[:, h % 2, :, :].rearrange("p q k -> p (q k)"), qi[:, h % 2, :], -128.0,
                                           float((127 + EXP_N) * 128), ALU.mult, ALU.add).then_inc(expo, 1)
                        if more and h % HG == HG - 1:
                            pool.wait_ge(scores, b * NH + h + 1)
                            take(b + 1, h // HG)

                pool.wait_ge(qk_ready, 6 * NHALF)
                for group in range(3):
                    take(0, group)
                quantise(wp_f, wp_f, S_WPROJ)
                with pool.Fori(0, NB - 1) as b:
                    powers(b, True)
                powers(NB - 1, False)

            @block.vector
            def _(v):
                step = Chain(v, vec)

                def clip_round(dst, src, signal):
                    step(v.tensor_scalar(src, src, 127.0, -128.0, ALU.min, ALU.max))
                    return v.tensor_scalar(dst, src, MAGIC, -MAGIC, ALU.add, ALU.add).then_inc(signal, 1)

                def floor_of(col):
                    c = kf[:, col:col + 1]
                    step(v.tensor_scalar(kf[:, K_T0:K_T0 + 1], c, MAGIC, -MAGIC, ALU.add, ALU.add))
                    step(v.tensor_tensor(kf[:, K_T1:K_T1 + 1], kf[:, K_T0:K_T0 + 1], c, ALU.is_gt))
                    step(v.tensor_tensor(c, kf[:, K_T0:K_T0 + 1], kf[:, K_T1:K_T1 + 1], ALU.subtract))

                k = lambda i: kf[:, i:i + 1]
                s = lambda i: sc[:, i:i + 1]
                r = lambda i: rc[:, i:i + 1]
                ln.vector(v, 0, X, U, 1e-5)
                step(v.memset(kf[:, K_MAGIC:K_MAGIC + 1], MAGIC))
                step(v.memset(kf[:, K_FLOOR:K_FLOOR + 1], -0.5 + 2.0 ** -8))
                v.wait_ge(loaded, 64)
                v.reciprocal(rc[:], sc[:]).then_inc(scaled, 1)
                v.wait_ge(scaled, 1)
                for dst, a, m in ((K_QKV, S_N1, s(S_WQKV)), (K_ATTN, S_QKV, s(S_QKV)), (K_PROJ, S_QKV, s(S_WPROJ)),
                                  (K_FC1, S_N2, s(S_WFC1)), (K_FC2, S_ACT, s(S_WFC2))):
                    step(v.tensor_tensor(k(dst), s(a), m, ALU.mult))
                step(v.tensor_tensor(k(K_QKV), k(K_QKV), r(S_QKV), ALU.mult))
                step(v.tensor_scalar(k(K_ATTN), k(K_ATTN), r(S_ATTN), HE ** -0.5, ALU.mult, ALU.mult))
                step(v.tensor_scalar(k(K_PROJ), k(K_PROJ), r(S_SV), 1 / 128, ALU.mult, ALU.mult))
                step(v.tensor_scalar(k(K_FC2), k(K_FC2), r(S_M2), None, ALU.mult))
                step(v.tensor_scalar(k(K_X0), r(S_ATTN), -0.6931, None, ALU.mult))
                step(v.tensor_scalar(k(K_BI), r(S_ATTN), 1.353, None, ALU.mult))
                step(v.tensor_scalar(k(K_CI), r(S_ATTN), r(S_ATTN), 0.344 / 0.3585, ALU.mult, ALU.mult))
                for c in (K_X0, K_BI, K_CI):
                    floor_of(c)
                step(v.reciprocal(k(K_INV), k(K_X0)))
                step(v.tensor_scalar(k(K_QB), k(K_INV), -0.5, -0.5, ALU.mult, ALU.add))
                step(v.tensor_scalar(k(K_CLAMP), k(K_X0), float(EXP_N), None, ALU.mult))
                step(v.tensor_scalar(k(K_NX0), k(K_X0), -1.0, None, ALU.mult))
                step(v.tensor_scalar(bqk[:], bqk[:], r(S_QKV), None, ALU.mult))
                for row, unit in ((0, S_N1), (1, S_N1), (2, S_N2), (3, S_N2), (4, S_QKV), (5, S_SV), (6, S_M2)):
                    step(v.tensor_scalar(rows[:, row, :], rows[:, row, :], r(unit), None, ALU.mult))
                v.memset(kf[:, K_T0:K_T1 + 1], 0.0).then_inc(constants, 1)

                def row(i):
                    return rows[:, i, :].unsqueeze(1).broadcast_to([P, NT, C])

                def normed_ints(use, g, beta):
                    v.wait_ge(ln.out, NT * use)
                    ln.vector(v, use, U, N, 1e-6)
                    v.wait_ge(ln.out, NT * (use + 1))
                    step(v.tensor_tensor(N[:], N[:], row(g), ALU.mult))
                    step(v.tensor_tensor(N[:], N[:], row(beta), ALU.add))
                    clip_round(Ni[:], N[:], normed)

                normed_ints(1, 0, 1)
                v.wait_ge(w_loaded, 80)
                for f, i in ((wqk_f, wqk), (wv_f, wv)):
                    step(v.tensor_scalar(f[:], f[:], rc[0:CH, S_WQKV:S_WQKV + 1], 127.0, ALU.mult, ALU.min))
                    step(v.tensor_scalar(f[:], f[:], -128.0, MAGIC, ALU.max, ALU.add))
                    v.tensor_scalar(i[:], f[:], -MAGIC, None, ALU.add).then_inc(quantised, 1)
                for n in range(6 * NHALF):
                    v.wait_ge(evac, n + 1)
                    clip_round(qk[:, n * BANK:(n + 1) * BANK], qf[:, n % 4, :], qk_ready)
                for n in range(NT // 2):
                    v.wait_ge(v_proj, n + 1)
                    step(v.scalar_tensor_tensor(vf[:, 2 * n:2 * n + 2, :], ps[:, 4 + n, 0:2 * C].rearrange("p (t c) -> p t c", t=2),
                                                k(K_QKV), rows[:, 4, :].unsqueeze(1).broadcast_to([P, 2, C]), ALU.mult, ALU.add))
                clip_round(vi[:, :], flat(vf), v_ready)
                v.wait_ge(v_ready, 1)
                v.wait_ge(qk_ready, 6 * NHALF)

                def slots(b, first, second):
                    pb = b - 1
                    for n in range(SLOTS):
                        h, g = n, n - 1
                        if first and h < NH:
                            v.wait_ge(shifted, b * NH + h + 1)
                            v.tensor_scalar(lt[:, h % 2, :, :], lt[:, h % 2, :, :], MAGIC + 127.0, MAGIC - 128.0, ALU.min,
                                            ALU.max).then_inc(clipped, 1)
                        if first and 0 <= g < NH:
                            v.wait_ge(quot, b * NH + g + 1)
                            v.wait_ge(expo, b * NH + max(g - 1, 0))
                            v.tensor_scalar(qi[:, g % 2, :], qv[:, g % 2, :], MAGIC, -MAGIC, ALU.add, ALU.add).then_inc(whole, 1)
                        if first and h < NH:
                            v.wait_ge(clipped, b * NH + h + 1)
                            v.tensor_reduce(nm[:, h % 2, :], lt[:, h % 2, :, :], AX.X, ALU.max, negate=True).then_inc(negmax, 1)
                        if first and 0 <= g < NH:
                            v.wait_ge(whole, b * NH + g + 1)
                            v.scalar_tensor_tensor(ri[:, g % 2, :], qi[:, g % 2, :], k(K_NX0), xi[:, g % 2, :, :].rearrange("p q k -> p (q k)"),
                                                   ALU.mult, ALU.add).then_inc(rest, 1)
                        if first and h < NH:
                            v.wait_ge(negmax, b * NH + h + 1)
                            for q in range(QT):
                                v.tensor_scalar(xi[:, h % 2, q, :], lt[:, h % 2, q, :], nm[:, h % 2, q:q + 1], k(K_CLAMP), ALU.add,
                                                ALU.max).then_inc(diff, 1)
                        if second and 0 <= g < NH:
                            v.wait_ge(prob, (pb * NH + g + 1) * QT)
                            v.wait_ge(turned, pb * NH + max(g - 1, 0))
                            v.tensor_scalar(pi[:, g % 2, :, :], pv[:, g % 2, :, :], MAGIC, -MAGIC, ALU.add, ALU.add).then_inc(floored, 1)
                        if first and n >= 2:
                            e = n - 2
                            v.wait_ge(square, b * NH + e + 1)
                            v.wait_ge(expo, b * NH + e + 1)
                            if second:
                                v.wait_ge(prob, (pb * NH + e + 1) * QT)
                            for q in range(QT):
                                v.scalar_tensor_tensor(ex[:, e, q, :], zz[:, e % 2, q, :], k(K_CI), e2[:, e % 2, q, :].bitcast(BF16),
                                                       ALU.add, ALU.mult, accum_out=sums[:, e, q:q + 1]).then_inc(expd, 1)
                    if first:
                        v.wait_ge(expd, (b + 1) * NH * QT)
                        sf = sums[:, :, :].rearrange("p h q -> p (h q)")
                        step(v.reciprocal(f0[:, :], sf))
                        step(v.tensor_scalar(f0[:, :], f0[:, :], 2.0 ** 32, None, ALU.mult))
                        step(v.tensor_scalar(f1[:, :], f0[:, :], MAGIC, -MAGIC, ALU.add, ALU.add))
                        step(v.tensor_tensor(f0[:, :], f1[:, :], f0[:, :], ALU.is_gt))
                        step(v.tensor_tensor(f1[:, :], f1[:, :], f0[:, :], ALU.subtract))
                        v.tensor_scalar(fac[:, :, :].rearrange("p h q -> p (h q)"), f1[:, :], 2.0 ** -25, None, ALU.mult).then_inc(factor, 1)

                slots(0, True, False)
                with v.Fori(1, NB) as b:
                    step.loop(b - 1, 5)
                    slots(b, True, True)
                step.end(NB - 1)
                slots(NB, False, True)
                v.wait_ge(factor, NB)

                def requantised(src, unit, add_to, out_unit):
                    step(v.tensor_scalar(src, src, 127.0, -128.0, ALU.min, ALU.max))
                    step(v.tensor_scalar(src, src, MAGIC, -MAGIC, ALU.add, ALU.add))
                    step(v.scalar_tensor_tensor(src, src, s(unit), add_to, ALU.mult, ALU.add))
                    step(v.tensor_scalar(src, src, r(out_unit), 127.0, ALU.mult, ALU.min))
                    step(v.tensor_scalar(src, src, -128.0, MAGIC, ALU.max, ALU.add))
                    step(v.tensor_scalar(add_to, src, -MAGIC, s(out_unit), ALU.add, ALU.mult))

                for n in range(NT // 2):
                    v.wait_ge(o_proj, n + 1)
                    step(v.scalar_tensor_tensor(pj[:, 2 * n * C:2 * (n + 1) * C].rearrange("p (t c) -> p t c", c=C),
                                                ps[:, n, 0:2 * C].rearrange("p (t c) -> p t c", c=C), k(K_PROJ),
                                                rows[:, 5, :].unsqueeze(1).broadcast_to([P, 2, C]), ALU.mult, ALU.add))
                requantised(pj[:, :], S_SV, flat(U), S_R1)
                v.wait_ge(turned_n, 2)
                normed_ints(2, 2, 3)
                for m in range(FT):
                    for half in range(NHALF):
                        src = hf[:, 2 * (m % 2) + half, :]
                        v.wait_ge(gelu, NHALF * m + half + 1)
                        v.tensor_scalar(src, src, r(S_ACT), 127.0, ALU.mult, ALU.min).then_inc(h_steps, 1)
                    for half in range(NHALF):
                        src = hf[:, 2 * (m % 2) + half, :]
                        v.wait_ge(h_steps, 4 * m + half + 1)
                        v.tensor_scalar(src, src, -128.0, MAGIC, ALU.max, ALU.add).then_inc(h_steps, 1)
                    for half in range(NHALF):
                        src = hf[:, 2 * (m % 2) + half, :]
                        v.wait_ge(h_steps, 4 * m + half + 3)
                        v.tensor_scalar(hi[:, m, half * BANK:(half + 1) * BANK], src, -MAGIC, None, ALU.add).then_inc(hq, 1)
                v.wait_ge(hq, FT * NHALF)
                pj3 = pj[:, :].rearrange("p (t c) -> p t c", c=C)
                for half in range(NHALF):
                    for t in range(4 * half, 4 * half + 4):
                        v.wait_ge(down, t + 1)
                        v.scalar_tensor_tensor(pj3[:, t, :], ps[:, 4 + t % 4, 0:C], k(K_FC2), rows[:, 6, :], ALU.mult, ALU.add).then_inc(down_read, 1)
                    v.wait_ge(down_read, 4 * half + 4)
                    at = slice(half * 4 * C, (half + 1) * 4 * C)
                    requantised(pj[:, at], S_M2, flat(U)[:, at], S_R2)
                    step(v.tensor_tensor(flat(X)[:, at], flat(X)[:, at], flat(U)[:, at], ALU.add))

            @block.scalar
            def _(act):
                ln.scalar(act, 0)
                ln.scalar(act, 1)
                act.wait_ge(constants, 1)

                def turned_input(n):
                    for c in range(2):
                        act.wait_ge(turned_n, 2 * n + c + 1)
                        act.activation(nT[:, c, :], ps[0:CH, 6 + c, :].bitcast(BF16), ACT.Copy).then_inc(n_sb, 1)

                turned_input(0)
                for n in range(6 * NHALF):
                    act.wait_ge(proj, n + 1)
                    if n >= 4:
                        act.wait_ge(qk_ready, n - 3)
                    act.activation(qf[:, n % 4, :], ps[:, n % 4, :], ACT.Identity, scale=kf[:, K_QKV:K_QKV + 1],
                                   bias=bqk[:, n // NHALF:n // NHALF + 1]).then_inc(evac, 1)

                def shift(b, h):
                    act.wait_ge(scores, b * NH + h + 1)
                    act.wait_ge(diff, (b * NH + max(h - 1, 0)) * QT)
                    act.activation(lt[:, h % 2, :, :].rearrange("p q k -> p (q k)"), ps[:, h % 2, :], ACT.Identity,
                                   scale=kf[:, K_ATTN:K_ATTN + 1], bias=kf[:, K_MAGIC:K_MAGIC + 1]).then_inc(shifted, 1)

                def slots(b, first, second):
                    pb = b - 1
                    if second:
                        act.wait_ge(factor, pb + 1)
                    if first:
                        shift(b, 0)
                    for n in range(SLOTS):
                        h, g = n, n - 1
                        if first and h + 1 < NH:
                            shift(b, h + 1)
                        if second and h < NH:
                            act.wait_ge(floored, pb * NH + max(h - 1, 0))
                            for q in range(QT):
                                act.activation(pv[:, h % 2, q, :], ex[:, h, q, :], ACT.Identity, scale=fac[:, h, q:q + 1],
                                               bias=kf[:, K_FLOOR:K_FLOOR + 1]).then_inc(prob, 1)
                        if first and 0 <= g < NH:
                            act.wait_ge(rest, b * NH + g + 1)
                            act.wait_ge(expd, (b * NH + max(g - 1, 0)) * QT)
                            act.activation(zz[:, g % 2, :, :].rearrange("p q k -> p (q k)"), ri[:, g % 2, :], ACT.Square,
                                           bias=kf[:, K_BI:K_BI + 1]).then_inc(square, 1)
                        if first and h < NH:
                            act.wait_ge(diff, (b * NH + h + 1) * QT)
                            act.wait_ge(whole, b * NH + max(h - 1, 0))
                            act.activation(qv[:, h % 2, :], xi[:, h % 2, :, :].rearrange("p q k -> p (q k)"), ACT.Identity,
                                           scale=kf[:, K_INV:K_INV + 1], bias=kf[:, K_QB:K_QB + 1]).then_inc(quot, 1)
                        if second and 0 <= g < NH:
                            act.wait_ge(turned, pb * NH + g + 1)
                            act.wait_ge(summed, pb * NH + max(g - 1, 0))
                            act.activation(PT[:, g % 2, :, :], ps[:, 2 + g % 2, 0:L].bitcast(BF16).rearrange("p (k q) -> p k q", k=QT),
                                           ACT.Copy).then_inc(turned_sb, 1)
                    if second:
                        act.wait_ge(summed, (pb + 1) * NH)
                        act.sem_inc(act_past, 1)
                        act.activation(Os_flat[:, ds(pb * QT * C, QT * C)], ps[:, 4, 0:QT * C], ACT.Copy).then_inc(o_sb, 1)

                act.wait_ge(constants, 1)
                slots(0, True, False)
                with act.Fori(1, NB) as b:
                    slots(b, True, True)
                slots(NB, False, True)
                for n in range(2 * NHALF):
                    act.wait_ge(o_turned, n + 1)
                    act.activation(OT[:, n % 2, (n // 2) * BANK:(n // 2 + 1) * BANK], ps[0:CH, 4 + n, :], ACT.Copy).then_inc(oT_sb, 1)
                ln.scalar(act, 2)
                turned_input(1)
                for n in range(FT * NHALF):
                    act.wait_ge(up, n + 1)
                    act.wait_ge(hq, max(n - 3, 0))
                    act.activation(hf[:, n % 4, :], ps[:, n % 4, :], ACT.Gelu, scale=kf[:, K_FC1:K_FC1 + 1],
                                   bias=b1[:, n // 2:n // 2 + 1]).then_inc(gelu, 1)

            @block.tensor
            def _(pe):
                def turn_input(n):
                    pe.wait_ge(normed, n + 1)
                    for c in range(2):
                        for t in range(NT):
                            mm = pe.transpose(ps[0:CH, 6 + c, :].bitcast(BF16)[:, t * P:(t + 1) * P], Ni[:, t, c * CH:(c + 1) * CH],
                                              identb[:, :])
                        mm.then_inc(turned_n, 1)

                turn_input(0)
                pe.wait_ge(quantised, 2)
                pe.wait_ge(n_sb, 2)
                for n in range(6 * NHALF):
                    o, half = divmod(n, NHALF)
                    if n >= 4:
                        pe.wait_ge(evac, n - 3)
                    for c in range(2):
                        mm = pe.matmul(ps[:, n % 4, :], wqk[:, (c * 6 + o) * P:(c * 6 + o + 1) * P],
                                       nT[:, c, half * BANK:(half + 1) * BANK], start=(c == 0), stop=(c == 1))
                    mm.then_inc(proj, 1)
                for t in range(NT):
                    for c in range(2):
                        mm = pe.matmul(ps[:, 4 + t // 2, (t % 2) * C:(t % 2 + 1) * C], nT[:, c, t * P:(t + 1) * P],
                                       wv[:, c * C:(c + 1) * C], start=(c == 0), stop=(c == 1))
                    if t % 2:
                        mm.then_inc(v_proj, 1)
                pe.wait_ge(evac, 6 * NHALF)
                pe.wait_ge(qk_ready, 6 * NHALF)
                pe.wait_ge(v_ready, 1)

                def slots(b, first, second):
                    pb = b - 1
                    for n in range(SLOTS + 1):
                        h, g, e = n, n - 2, n - 3
                        if first and h < NH:
                            if second or h >= 2:
                                pe.wait_ge(shifted, b * NH + h - 1)
                            if h % HG == 0:
                                pe.wait_ge(taken, b * 6 + 2 * (h // HG) + 2)
                            at = slice(32 * (h % HG), 32 * (h % HG) + HE)
                            for q in range(QT):
                                mm = pe.matmul(ps[:, h % 2, q * L:(q + 1) * L],
                                               qkb[at, h // HG, q * P:(q + 1) * P], qkb[at, 3 + h // HG, :], start=True, stop=True)
                            mm.then_inc(scores, 1)
                        if second and 0 <= g < NH:
                            pe.wait_ge(floored, pb * NH + g + 1)
                            pe.wait_ge(turned_sb, pb * NH + max(g - 1, 0))
                            for kt in range(QT):
                                for q in range(QT):
                                    mm = pe.transpose(ps[:, 2 + g % 2, 0:L].bitcast(BF16)[:, kt * L + q * P:kt * L + (q + 1) * P],
                                                      pi[:, g % 2, q, kt * P:(kt + 1) * P], identb[:, :])
                            mm.then_inc(turned, 1)
                        if second and 0 <= e < NH:
                            pe.wait_ge(turned_sb, pb * NH + e + 1)
                            if e == 0:
                                pe.wait_ge(o_sb, pb)
                            for q in range(QT):
                                for kt in range(QT):
                                    mm = pe.matmul(ps[:, 4, q * C + e * HE:q * C + (e + 1) * HE], PT[:, e % 2, kt, q * P:(q + 1) * P],
                                                   vi[:, ds(pb * QT * C + kt * C + e * HE, HE)], start=(kt == 0), stop=(kt == QT - 1))
                            mm.then_inc(summed, 1)

                slots(0, True, False)
                with pe.Fori(1, NB) as b:
                    slots(b, True, True)
                slots(NB, False, True)
                pe.wait_ge(o_sb, NB)
                for n in range(2 * NHALF):
                    half, c = divmod(n, 2)
                    for t in range(4):
                        mm = pe.transpose(ps[0:CH, 4 + n, t * P:(t + 1) * P], Os[:, 4 * half + t, c * CH:(c + 1) * CH], K["ident"][:, :])
                    mm.then_inc(o_turned, 1)
                pe.wait_ge(w_quantised, 9)
                pe.wait_ge(oT_sb, 2 * NHALF)
                for t in range(NT):
                    for c in range(2):
                        mm = pe.matmul(ps[:, t // 2, (t % 2) * C:(t % 2 + 1) * C], OT[:, c, t * P:(t + 1) * P], wp_f[:, c * C:(c + 1) * C],
                                       start=(c == 0), stop=(c == 1))
                    if t % 2:
                        mm.then_inc(o_proj, 1)
                turn_input(1)
                pe.wait_ge(n_sb, 4)
                for n in range(FT * NHALF):
                    f, half = divmod(n, 2)
                    if n >= 4:
                        pe.wait_ge(gelu, n - 3)
                    for c in range(2):
                        mm = pe.matmul(ps[:, n % 4, :], w1[:, c * FF + f * P:c * FF + (f + 1) * P],
                                       nT[:, c, half * BANK:(half + 1) * BANK], start=(c == 0), stop=(c == 1))
                    mm.then_inc(up, 1)
                pe.wait_ge(hq, FT * NHALF)
                for t in range(NT):
                    if t >= 4:
                        pe.wait_ge(down_read, t - 3)
                    for f in range(FT):
                        mm = pe.matmul(ps[:, 4 + t % 4, 0:C], hi[:, f, t * P:(t + 1) * P], w2[:, f * C:(f + 1) * C],
                                       start=(f == 0), stop=(f == FT - 1))
                    mm.then_inc(down, 1)


class Turned:

    def __init__(self, ctx):
        self.turned, self.copied = ctx.sem("uT_turned"), ctx.sem("uT_copied")

    def tensor(self, pe, use, ln, ln_use, U, ps, ident):
        for n in range(4):
            for t in range(4):
                ln.done(pe, ln_use, (n // 2) * 4 + t)
                mm = pe.transpose(ps[0:CH, n, t * P:(t + 1) * P], U[:, (n // 2) * 4 + t, (n % 2) * CH:(n % 2 + 1) * CH],
                                  ident[:, :])
            mm.then_inc(self.turned, 1)

    def scalar(self, act, use, uT, ps):
        for n in range(4):
            act.wait_ge(self.turned, 4 * use + n + 1)
            act.activation(uT[:, n % 2, (n // 2) * BANK:(n // 2 + 1) * BANK], ps[0:CH, n, :], ACT.Copy).then_inc(self.copied, 1)

    def wait(self, eng, use):
        eng.wait_ge(self.copied, 4 * (use + 1))


CA = P
CB = C - CA
XS = 16.0
WS = 256.0


def expert_layer(nc, K, X, D, ln, tr, pre, use, experts, routed, tiles, gated):
    WU = 2 if gated else 1
    MI = 4 * tiles
    NU = WU * tiles * P
    ND = tiles * C
    with ExitStack() as stack:
        ctx = Ctx(nc, stack)
        U = ctx.sb(f"{pre}_U", [P, NT, C])
        uT = ctx.sb(f"{pre}_uT", [CH, 2, T])
        U2 = ctx.sb(f"{pre}_U2", [P, NT, 2 * CB])
        xa_hi = ctx.sb(f"{pre}_xa_hi", [CA, T], F16)
        xa_lo = ctx.sb(f"{pre}_xa_lo", [CA, T], F16)
        xb_hi = ctx.sb(f"{pre}_xb_hi", [2 * CB, T], F16)
        xb_lo = ctx.sb(f"{pre}_xb_lo", [CB, T], F16)
        gate = ctx.sb(f"{pre}_gate", [CH, 2 * routed])
        iota = ctx.sb(f"{pre}_iota", [P, routed])
        lg = ctx.sb(f"{pre}_lg", [P, NT, routed])
        mx = ctx.sb(f"{pre}_mx", [P, NT])
        best = ctx.sb(f"{pre}_best", [P, NT, 8])
        besti = ctx.sb(f"{pre}_besti", [P, NT, 8], U32)
        bestf = ctx.sb(f"{pre}_bestf", [P, NT, 8])
        wts = ctx.sb(f"{pre}_wts", [P, NT, 2])
        t0 = ctx.sb(f"{pre}_t0", [P, NT, routed])
        t1 = ctx.sb(f"{pre}_t1", [P, NT, routed])
        comb = ctx.sb(f"{pre}_comb", [P, experts * NT])
        combs = ctx.sb(f"{pre}_combs", [P, experts * NT])
        st_up = [ctx.sb(f"{pre}_stup{a}", [P, 2 * NU]) for a in range(2)]
        st_dn = [ctx.sb(f"{pre}_stdn{a}", [P, ND]) for a in range(2)]
        st_b = [ctx.sb(f"{pre}_stb{a}", [P, tiles]) for a in range(2)]
        wa_hi = [ctx.sb(f"{pre}_wa_hi{a}", [CA, NU], F16) for a in range(2)]
        wa_lo = [ctx.sb(f"{pre}_wa_lo{a}", [CA, NU], F16) for a in range(2)]
        wb = [ctx.sb(f"{pre}_wb{a}", [2 * CB, NU], F16) for a in range(2)]
        wd_hi = [ctx.sb(f"{pre}_wd_hi{a}", [P, ND], F16) for a in range(2)]
        wd_lo = [ctx.sb(f"{pre}_wd_lo{a}", [P, ND], F16) for a in range(2)]
        b_up = [ctx.sb(f"{pre}_bup{a}", [P, tiles]) for a in range(2)]
        act_out = ctx.sb(f"{pre}_act", [P, 4, BANK])
        h32 = ctx.sb(f"{pre}_h32", [P, 2, BANK])
        h_hi = ctx.sb(f"{pre}_h_hi", [P, 2, tiles, BANK], F16)
        h_lo = ctx.sb(f"{pre}_h_lo", [P, 2, tiles, BANK], F16)
        bo = ctx.sb(f"{pre}_bo", [routed, C])
        combT = ctx.sb(f"{pre}_combT", [routed, T])
        ps = ctx.ps(f"ps_{pre}", [P, 8, BANK])
        S = lambda n: ctx.sem(f"{pre}_{n}")
        loaded, logits, route, route_act, top = S("loaded"), S("logits"), S("route"), S("route_act"), S("top")
        comb_turned, comb_sb, bias_ps, bias_added = S("comb_turned"), S("comb_sb"), S("bias_ps"), S("bias_added")
        doubled, sync_past = S("doubled"), S("sync_past")
        x_turned, x_hi, x_lo, split_hi, split_lo, b_copied = (
            S("x_turned"), S("x_hi"), S("x_lo"), S("split_hi"), S("split_lo"), S("b_copied"))
        w_ready = [S(f"w_ready{a}") for a in range(2)]
        up, activated, h_part, h_done, down, acc = S("up"), S("activated"), S("h_part"), S("h_done"), S("down"), S("acc")
        WD = 2 if gated else 3
        PAIRS = experts // 2
        SP = 3
        HP = 2 if gated else 1
        splits = {(0, 1): (1, 0, SP), (0, 2): (1, 1, SP + 1), (0, 3): (1, 2, SP + 2),
                  (2, 1): (0, 0, 2 * SP), (2, 2): (0, 1, 2 * SP + 1), (3, 0): (0, 2, 2 * SP + 2)}
        comb3 = comb[:, 0:routed * NT].rearrange("p (e t) -> p t e", t=NT)

        with nc.Block() as block:
            @block.sync
            def _(sync):
                def load(i, a):
                    sync.dma_start(st_up[a][:, :], D[f"{pre}_up"][ds((2 * i + a) * P, P), :]).then_inc(w_ready[a], 16)
                    sync.dma_start(st_dn[a][:, :], D[f"{pre}_dn"][ds((2 * i + a) * P, P), :]).then_inc(w_ready[a], 16)
                    if not gated:
                        sync.dma_start(st_b[a][:, :], D[f"{pre}_b"][ds((2 * i + a) * P, P), :]).then_inc(w_ready[a], 16)

                for dst, src in ((gate, f"{pre}_gate"), (iota, "iota")):
                    sync.dma_start(dst[:], D[src][:, 0:dst.shape[1]]).then_inc(loaded, 16)
                if not gated:
                    sync.dma_start(bo[:, :], D[f"{pre}_bo"]).then_inc(loaded, 16)
                for a in range(2):
                    load(0, a)
                with sync.Fori(0, PAIRS) as i:
                    for a in range(2):
                        sync.wait_ge(split_lo, i * 2 * SP + (a + 1) * SP)
                        sync.sem_inc(sync_past, 1)
                        load(i + 1, a)
                for a in range(2):
                    sync.wait_ge(w_ready[a], (PAIRS + 1) * 16 * WD)

            @block.gpsimd
            def _(pool):
                ln.done(pool, use, NT - 1)
                for n in range(2):
                    pool.tensor_copy(U2[:, :, n * CB:(n + 1) * CB], U[:, :, CA:C]).then_inc(doubled, 1)

            @block.vector
            def _(v):
                step = Chain(v, route)

                def split(i, a, part, n):
                    v.wait_ge(split_hi, i * 2 * SP + n + 1)
                    lo, st, hi = ((wa_lo[a][:, :], st_up[a][:, 0:NU], wa_hi[a][:, :]),
                                  (wb[a][CB:2 * CB, :], st_up[a][CB:2 * CB, NU:2 * NU], wb[a][CB:2 * CB, :]),
                                  (wd_lo[a][:, :], st_dn[a][:, :], wd_hi[a][:, :]))[part]
                    v.scalar_tensor_tensor(lo, st, WS, hi, ALU.mult, ALU.subtract).then_inc(split_lo, 1)

                ln.vector(v, use, X, U, 1e-5)
                for half in range(NHALF):
                    at = slice(half * BANK, (half + 1) * BANK)
                    v.wait_ge(x_hi, 2 * half + 1)
                    v.scalar_tensor_tensor(xa_lo[:, at], ps[:, 4 + half, :], XS, xa_hi[:, at], ALU.mult, ALU.subtract).then_inc(x_lo, 1)
                    v.wait_ge(x_hi, 2 * half + 2)
                    v.scalar_tensor_tensor(xb_lo[:, at], ps[0:CB, 6 + half, :], XS, xb_hi[0:CB, at], ALU.mult,
                                           ALU.subtract).then_inc(x_lo, 1)
                for part in range(SP):
                    split(0, 0, part, part)
                v.wait_ge(loaded, 32 if gated else 48)
                v.wait_ge(logits, 1)
                lp = ps[:, 4, 0:NT * routed].rearrange("p (t e) -> p t e", t=NT)
                if gated:
                    step(v.tensor_reduce(mx[:, :], lp, AX.X, ALU.max))
                    step(v.tensor_tensor(lg[:], lp, mx[:, :].unsqueeze(2).broadcast_to([P, NT, routed]), ALU.subtract))
                    v.wait_ge(route_act, 1)
                    step(v.tensor_reduce(mx[:, :], lg[:], AX.X, ALU.add))
                    step(v.reciprocal(mx[:, :], mx[:, :]))
                    step(v.tensor_tensor(lg[:], lg[:], mx[:, :].unsqueeze(2).broadcast_to([P, NT, routed]), ALU.mult))
                else:
                    step(v.tensor_copy(lg[:], lp))
                for t in range(NT):
                    v.max(best[:, t, :], lg[:, t, :]).then_inc(top, 1)
                for t in range(NT):
                    v.wait_ge(top, t + 1)
                    v.max_index(besti[:, t, :], best[:, t, :], lg[:, t, :]).then_inc(top, 1)
                v.wait_ge(top, 2 * NT)
                step(v.tensor_copy(bestf[:], besti[:]))
                if gated:
                    step(v.tensor_copy(wts[:], best[:, :, 0:2]))
                else:
                    step(v.tensor_tensor(wts[:, :, 1], best[:, :, 1], best[:, :, 0], ALU.subtract))
                    v.wait_ge(route_act, 1)
                    step(v.tensor_scalar(wts[:, :, 0], wts[:, :, 1], 1.0, None, ALU.add))
                    step(v.reciprocal(wts[:, :, 0], wts[:, :, 0]))
                    step(v.tensor_tensor(wts[:, :, 1], wts[:, :, 1], wts[:, :, 0], ALU.mult))
                grid = iota[:, :].unsqueeze(1).broadcast_to([P, NT, routed])
                for j, dst in ((0, t0), (1, t1)):
                    step(v.tensor_tensor(dst[:], grid, bestf[:, :, j:j + 1].broadcast_to([P, NT, routed]), ALU.is_equal))
                    step(v.tensor_tensor(dst[:], dst[:], wts[:, :, j:j + 1].broadcast_to([P, NT, routed]), ALU.mult))
                step(v.tensor_tensor(comb3, t0[:], t1[:], ALU.add))
                if experts > routed:
                    step(v.memset(comb[:, routed * NT:experts * NT], 1.0))
                if not gated:
                    for half in range(NHALF):
                        v.wait_ge(comb_turned, half + 1)
                        v.tensor_copy(combT[:, half * BANK:(half + 1) * BANK], ps[0:routed, half, :]).then_inc(comb_sb, 1)
                    for q in range(NT // 2):
                        v.wait_ge(bias_ps, q + 1)
                        v.tensor_tensor(X[:, 2 * q:2 * q + 2, :], X[:, 2 * q:2 * q + 2, :],
                                        ps[:, 4 + q, 0:2 * C].rearrange("p (a c) -> p a c", a=2), ALU.add).then_inc(bias_added, 1)
                    v.wait_ge(bias_added, NT // 2)
                step(v.tensor_scalar(combs[:, :], comb[:, :], 1 / WS, None, ALU.mult))
                with v.Fori(0, PAIRS) as i:
                    def hidden(u):
                        v.wait_ge(down, i * 2 * NT + 4 * max(u - 1, 0))
                        for f in range(tiles):
                            m = u * tiles + f
                            v.wait_ge(activated, i * MI + m + 1)
                            if gated:
                                v.scalar_tensor_tensor(h32[:, m % 2, :], ps[:, 2 * (m % 2) + 1, :], 1 / (XS * WS), act_out[:, m % 4, :],
                                                       ALU.mult, ALU.mult).then_inc(h_part, 1)
                                v.wait_ge(h_part, (i * MI + m) * HP + 1)
                                src = h32[:, m % 2, :]
                            else:
                                src = act_out[:, m % 4, :]
                            v.tensor_copy(h_hi[:, u % 2, f, :], src).then_inc(h_part, 1)
                            v.wait_ge(h_part, (i * MI + m + 1) * HP)
                            v.tensor_tensor(h_lo[:, u % 2, f, :], src, h_hi[:, u % 2, f, :], ALU.subtract).then_inc(h_done, 1)
                            if gated:
                                v.wait_ge(h_done, i * MI + m)
                            if (u, f) in splits:
                                split(i, *splits[u, f])

                    def accumulate(u):
                        for t in range(4):
                            n = 4 * u + t
                            tok = 4 * (u % 2) + t
                            v.wait_ge(down, i * 2 * NT + n + 1)
                            v.wait_ge(acc, i * 2 * NT + max(n - 7, 0))
                            v.scalar_tensor_tensor(X[:, tok, :], ps[:, 4 + t, 0:C],
                                                   combs[:, ds(i * 2 * NT + (u // 2) * NT + tok, 1)], X[:, tok, :],
                                                   ALU.mult, ALU.add).then_inc(acc, 1)

                    for u in range(4):
                        hidden(u)
                        if u >= 1:
                            accumulate(u - 1)
                    accumulate(3)
                v.wait_ge(acc, PAIRS * 2 * NT)

            @block.scalar
            def _(act):
                def split(a, part):
                    if part == 0 and not gated:
                        act.activation(b_up[a][:, :], st_b[a][:, :], ACT.Copy).then_inc(b_copied, 1)
                    hi, st = ((wa_hi[a][:, :], st_up[a][:, 0:NU]), (wb[a][:, :], st_up[a][:, NU:2 * NU]),
                              (wd_hi[a][:, :], st_dn[a][:, :]))[part]
                    act.activation(hi, st, ACT.Copy, scale=WS).then_inc(split_hi, 1)

                ln.scalar(act, use)
                tr.scalar(act, use - 3, uT, ps)
                for half in range(NHALF):
                    at = slice(half * BANK, (half + 1) * BANK)
                    act.wait_ge(x_turned, half + 1)
                    act.activation(xa_hi[:, at], ps[:, 4 + half, :], ACT.Copy, scale=XS).then_inc(x_hi, 1)
                    act.activation(xb_hi[:, at], ps[:, 6 + half, :], ACT.Copy, scale=XS).then_inc(x_hi, 1)
                act.wait_ge(w_ready[0], 16 * WD)
                for part in range(SP):
                    split(0, part)
                if gated:
                    act.wait_ge(route, 2)
                    act.activation(lg[:], lg[:], ACT.Exp).then_inc(route_act, 1)
                else:
                    act.wait_ge(route, 3)
                    act.activation(wts[:, :, 1], wts[:, :, 1], ACT.Exp).then_inc(route_act, 1)
                with act.Fori(0, PAIRS) as i:
                    for u in range(4):
                        a = u // 2
                        for f in range(tiles):
                            m = u * tiles + f
                            act.wait_ge(up, i * MI + m + 1)
                            act.wait_ge(h_done, i * MI + max(m - 3, 0))
                            act.activation(act_out[:, m % 4, :], ps[:, 2 * (m % 2) if gated else m % 4, :], ACT.Silu if gated else ACT.Gelu,
                                           scale=1 / (XS * WS), bias=0.0 if gated else b_up[a][:, f:f + 1]).then_inc(activated, 1)
                            if (u, f) in splits:
                                b, part, _ = splits[u, f]
                                if part == 0:
                                    act.wait_ge(w_ready[b], (i + 2 - b) * 16 * WD)
                                    act.wait_ge(split_lo, i * 2 * SP + (2 - b) * SP)
                                    act.wait_ge(activated, i * MI + 2 * tiles * (1 - b))
                                if part < 2:
                                    act.wait_ge(up, i * MI + 2 * tiles * (1 - b))
                                else:
                                    act.wait_ge(down, i * 2 * NT + 2 * 4 * (1 - b))
                                split(b, part)

            @block.tensor
            def _(pe):
                tr.tensor(pe, use - 3, ln, use, U, ps, K["ident"])
                pe.wait_ge(doubled, 2)
                for half in range(NHALF):
                    for t in range(4):
                        tok = 4 * half + t
                        at = slice(t * P, (t + 1) * P)
                        pe.transpose(ps[:, 4 + half, at], U[:, tok, 0:CA], K["ident"][:, :])
                        mm = pe.transpose(ps[:, 6 + half, at], U2[:, tok, :], K["ident"][:, :])
                    mm.then_inc(x_turned, 1)
                tr.wait(pe, use - 3)
                pe.wait_ge(loaded, 32 if gated else 48)
                pe.wait_ge(x_lo, 4)
                for t in range(NT):
                    for c in range(2):
                        mm = pe.matmul(ps[:, 4, t * routed:(t + 1) * routed], uT[:, c, t * P:(t + 1) * P],
                                       gate[:, c * routed:(c + 1) * routed], start=(c == 0), stop=(c == 1))
                mm.then_inc(logits, 1)
                if not gated:
                    pe.wait_ge(route, 11)
                    for t in range(NT):
                        mm = pe.transpose(ps[0:routed, t // 4, (t % 4) * P:(t % 4 + 1) * P], comb3[:, t, :], K["ident"][:, :])
                        if t % 4 == 3:
                            mm.then_inc(comb_turned, 1)
                    pe.wait_ge(comb_sb, 2)
                    for t in range(NT):
                        mm = pe.matmul(ps[:, 4 + t // 2, (t % 2) * C:(t % 2 + 1) * C], combT[:, t * P:(t + 1) * P], bo[:, :],
                                       start=True, stop=True)
                        if t % 2:
                            mm.then_inc(bias_ps, 1)
                    pe.wait_ge(bias_added, NT // 2)
                else:
                    pe.wait_ge(route, 2)
                with pe.Fori(0, PAIRS) as i:
                    def up_unit(u):
                        a, half = divmod(u, 2)
                        at = slice(half * BANK, (half + 1) * BANK)
                        if half == 0:
                            pe.wait_ge(split_lo, i * 2 * SP + SP + 2 * a)
                        for f in range(tiles):
                            m = u * tiles + f
                            if gated:
                                pe.wait_ge(h_part, i * MI * HP + max(2 * m - 3, 0))
                            else:
                                pe.wait_ge(activated, i * MI + max(m - 3, 0))
                            for w in range(WU):
                                out = ps[:, 2 * (m % 2) + w if gated else m % 4, :]
                                col = slice((w * tiles + f) * P, (w * tiles + f + 1) * P)
                                pe.matmul(out, wa_hi[a][:, col], xa_hi[:, at], start=True, stop=False)
                                pe.matmul(out, wa_hi[a][:, col], xa_lo[:, at], start=False, stop=False)
                                pe.matmul(out, wa_lo[a][:, col], xa_hi[:, at], start=False, stop=False)
                                pe.matmul(out, wb[a][:, col], xb_hi[:, at], start=False, stop=False)
                                mm = pe.matmul(out, wb[a][0:CB, col], xb_lo[:, at], start=False, stop=True)
                            mm.then_inc(up, 1)

                    def down_unit(u):
                        a, half = divmod(u, 2)
                        if half == 0 and a == 1:
                            pe.wait_ge(split_lo, i * 2 * SP + 2 * SP)
                        pe.wait_ge(h_done, i * MI + (u + 1) * tiles)
                        for t in range(4):
                            pe.wait_ge(acc, i * 2 * NT + max(4 * u + t - 3, 0))
                            out = ps[:, 4 + t, 0:C]
                            for f in range(tiles):
                                tok, col = slice(t * P, (t + 1) * P), slice(f * C, (f + 1) * C)
                                pe.matmul(out, h_hi[:, u % 2, f, tok], wd_hi[a][:, col], start=(f == 0), stop=False)
                                pe.matmul(out, h_hi[:, u % 2, f, tok], wd_lo[a][:, col], start=False, stop=False)
                                mm = pe.matmul(out, h_lo[:, u % 2, f, tok], wd_hi[a][:, col], start=False, stop=(f == tiles - 1))
                            mm.then_inc(down, 1)

                    for u in range(4):
                        up_unit(u)
                        if u >= 1:
                            down_unit(u - 1)
                    down_unit(3)


def attention_layer(nc, K, X, D, ln, tr, use):
    with ExitStack() as stack:
        ctx = Ctx(nc, stack)
        U = ctx.sb("a_U", [P, NT, C])
        uT = ctx.sb("a_uT", [CH, 2, T])
        wqk = ctx.sb("a_wqk", [CH, 2, 4 * CH])
        wv = ctx.sb("a_wv", [CH, 2, C])
        wo = ctx.sb("a_wo", [CH, 2, C])
        bqk = ctx.sb("a_bqk", [CH, 4])
        rows = ctx.sb("a_rows", [P, 2, C])
        qk = ctx.sb("a_qk", [CH, 4, T])
        vt = ctx.sb("a_v", [P, NT, C])
        nm = ctx.sb("a_nm", [P, NT])
        sums = ctx.sb("a_sums", [P, NT])
        rs = ctx.sb("a_rs", [P, NT])
        Pr = ctx.sb("a_P", [P, 2, QT, L])
        Pn = ctx.sb("a_Pn", [P, 2, QT, L])
        PT = ctx.sb("a_PT", [P, 2, QT, L])
        OT = ctx.sb("a_OT", [CH, 2, 2, L])
        ps = ctx.ps("ps_l5", [P, 8, BANK])
        S = lambda n: ctx.sem(f"l5_{n}")
        loaded, biased, proj, evac, vals, v_sb = S("loaded"), S("biased"), S("proj"), S("evac"), S("vals"), S("v_sb")
        scores, peak, expd, norm, normed, turned, turned_sb, out_ps, out_sb, res_ps, res = (
            S("scores"), S("peak"), S("expd"), S("norm"), S("normed"), S("turned"), S("turned_sb"), S("out_ps"), S("out_sb"),
            S("res_ps"), S("res"))

        with nc.Block() as block:
            @block.sync
            def _(sync):
                for dst, src in ((wqk, "a_wqk"), (wv, "a_wv"), (wo, "a_wo"), (bqk, "a_bqk")):
                    sync.dma_start(dst[:], D[src]).then_inc(loaded, 16)
                sync.dma_start(rows[:], D["a_rows"].partition_broadcast(P)).then_inc(loaded, 16)

            @block.vector
            def _(v):
                ln.vector(v, use, X, U, 1e-5)
                v.wait_ge(ln.out, NT * (use + 1))
                v.wait_ge(loaded, 80)
                v.tensor_tensor(X[:], X[:], rows[:, 1, :].unsqueeze(1).broadcast_to([P, NT, C]), ALU.add).then_inc(biased, 1)
                v.tensor_scalar(bqk[:, 0:2], bqk[:, 0:2], C ** -0.5, None, ALU.mult).then_inc(biased, 1)
                for q in range(NT // 2):
                    v.wait_ge(vals, q + 1)
                    v.tensor_tensor(vt[:, 2 * q:2 * q + 2, :], ps[:, 4 + q, 0:2 * C].rearrange("p (a c) -> p a c", a=2),
                                    rows[:, 0, :].unsqueeze(1).broadcast_to([P, 2, C]), ALU.add).then_inc(v_sb, 1)
                v.wait_ge(biased, 2)
                for n in range(NB + 3):
                    if n < NB:
                        b = n
                        v.wait_ge(scores, b + 1)
                        v.tensor_reduce(nm[:, 2 * b:2 * b + 2], ps[:, b % 2, :].rearrange("p (q k) -> p q k", q=QT), AX.X, ALU.max,
                                        negate=True).then_inc(peak, 1)
                    if 1 <= n <= NB:
                        b = n - 1
                        v.wait_ge(expd, 2 * b + 2)
                        v.reciprocal(rs[:, 2 * b:2 * b + 2], sums[:, 2 * b:2 * b + 2]).then_inc(norm, 1)
                        v.wait_ge(norm, b + 1)
                        if b >= 2:
                            v.wait_ge(turned, b - 1)
                        for q in range(QT):
                            v.tensor_scalar(Pn[:, b % 2, q, :], Pr[:, b % 2, q, :], rs[:, 2 * b + q:2 * b + q + 1], None,
                                            ALU.mult).then_inc(normed, 1)
                        v.wait_ge(turned, b + 1)
                        if b >= 2:
                            v.wait_ge(out_ps, b - 1)
                        v.tensor_copy(PT[:, b % 2, :, :], ps[:, 2 + b % 2, :].rearrange("p (k q) -> p k q", k=QT)).then_inc(turned_sb, 1)
                    if n >= 3:
                        b = n - 3
                        v.wait_ge(res_ps, b + 1)
                        v.tensor_tensor(X[:, 2 * b:2 * b + 2, :], X[:, 2 * b:2 * b + 2, :],
                                        ps[:, 6 + b % 2, 0:2 * C].rearrange("p (a c) -> p a c", a=2), ALU.add).then_inc(res, 1)

            @block.scalar
            def _(act):
                ln.scalar(act, use)
                tr.scalar(act, use - 3, uT, ps)
                act.wait_ge(biased, 2)
                for o in range(4):
                    for half in range(NHALF):
                        n = 2 * o + half
                        act.wait_ge(proj, n + 1)
                        act.activation(qk[:, o, half * BANK:(half + 1) * BANK], ps[0:CH, n % 4, :], ACT.Identity,
                                       scale=C ** -0.5 if o < 2 else 1.0, bias=bqk[:, o:o + 1]).then_inc(evac, 1)
                for n in range(NB + 2):
                    if n < NB:
                        b = n
                        act.wait_ge(peak, b + 1)
                        if b >= 2:
                            act.wait_ge(normed, 2 * b - 2)
                        for q in range(QT):
                            act.activation(Pr[:, b % 2, q, :], ps[:, b % 2, q * L:(q + 1) * L], ACT.Exp,
                                           bias=nm[:, 2 * b + q:2 * b + q + 1],
                                           accum_out=sums[:, 2 * b + q:2 * b + q + 1]).then_inc(expd, 1)
                    if n >= 2:
                        b = n - 2
                        act.wait_ge(out_ps, b + 1)
                        if b >= 2:
                            act.wait_ge(res_ps, b - 1)
                        act.activation(OT[:, b % 2, :, :], ps[0:CH, 4 + b % 2, :].rearrange("p (c t) -> p c t", c=2),
                                       ACT.Copy).then_inc(out_sb, 1)

            @block.tensor
            def _(pe):
                tr.tensor(pe, use - 3, ln, use, U, ps, K["ident"])
                tr.wait(pe, use - 3)
                pe.wait_ge(loaded, 80)
                for o in range(4):
                    for half in range(NHALF):
                        n = 2 * o + half
                        if n >= 4:
                            pe.wait_ge(evac, n - 3)
                        for c in range(2):
                            mm = pe.matmul(ps[0:CH, n % 4, :], wqk[:, c, o * CH:(o + 1) * CH], uT[:, c, half * BANK:(half + 1) * BANK],
                                           start=(c == 0), stop=(c == 1))
                        mm.then_inc(proj, 1)
                for t in range(NT):
                    for c in range(2):
                        mm = pe.matmul(ps[:, 4 + t // 2, (t % 2) * C:(t % 2 + 1) * C], uT[:, c, t * P:(t + 1) * P], wv[:, c, :],
                                       start=(c == 0), stop=(c == 1))
                    if t % 2:
                        mm.then_inc(vals, 1)
                pe.wait_ge(evac, 8)
                pe.wait_ge(v_sb, NT // 2)
                for n in range(NB + 3):
                    if n < NB:
                        b = n
                        if b >= 2:
                            pe.wait_ge(expd, 2 * b - 2)
                        for q in range(QT):
                            for c in range(2):
                                mm = pe.matmul(ps[:, b % 2, q * L:(q + 1) * L], qk[:, c, b * L + q * P:b * L + (q + 1) * P],
                                               qk[:, 2 + c, b * L:(b + 1) * L], start=(c == 0), stop=(c == 1))
                        mm.then_inc(scores, 1)
                    if 1 <= n <= NB:
                        b = n - 1
                        pe.wait_ge(normed, 2 * b + 2)
                        if b >= 2:
                            pe.wait_ge(turned_sb, b - 1)
                        for k in range(QT):
                            for q in range(QT):
                                mm = pe.transpose(ps[:, 2 + b % 2, k * L + q * P:k * L + (q + 1) * P],
                                                  Pn[:, b % 2, q, k * P:(k + 1) * P], K["ident"][:, :])
                        mm.then_inc(turned, 1)
                    if 2 <= n <= NB + 1:
                        b = n - 2
                        pe.wait_ge(turned_sb, b + 1)
                        if b >= 2:
                            pe.wait_ge(out_sb, b - 1)
                        for c in range(2):
                            for k in range(QT):
                                mm = pe.matmul(ps[0:CH, 4 + b % 2, c * L:(c + 1) * L], vt[:, 2 * b + k, c * CH:(c + 1) * CH],
                                               PT[:, b % 2, k, :], start=(k == 0), stop=(k == QT - 1))
                        mm.then_inc(out_ps, 1)
                    if n >= 3:
                        b = n - 3
                        pe.wait_ge(out_sb, b + 1)
                        if b >= 2:
                            pe.wait_ge(res, b - 1)
                        for q in range(QT):
                            for c in range(2):
                                mm = pe.matmul(ps[:, 6 + b % 2, q * C:(q + 1) * C], OT[:, b % 2, c, q * P:(q + 1) * P], wo[:, c, :],
                                               start=(c == 0), stop=(c == 1))
                        mm.then_inc(res_ps, 1)


def program(nc, D, out):
    with ExitStack() as stack:
        ctx = Ctx(nc, stack)
        X = ctx.sb("X", [P, NT, C])
        K = {"ident": ctx.sb("ident", [P, P]), "identb": ctx.sb("identb", [P, P], BF16)}
        constants = ctx.sem("constants")
        with nc.Block() as block:
            @block.sync
            def _(sync):
                sync.dma_start(K["ident"][:, :], D["ident"]).then_inc(constants, 16)

            @block.vector
            def _(v):
                v.wait_ge(constants, 16)
                v.tensor_copy(K["identb"][:, :], K["ident"][:, :]).then_inc(constants, 1)
        scan_layer(nc, K, X, D)
        neighbour_layer(nc, K, X, D)
        ln = LayerNorm(ctx)
        tr = Turned(ctx)
        quantised_layer(nc, K, X, D, ln)
        expert_layer(nc, K, X, D, ln, tr, "m", 3, 18, 16, 4, True)
        attention_layer(nc, K, X, D, ln, tr, 4)
        expert_layer(nc, K, X, D, ln, tr, "g", 5, 8, 8, 6, False)
        stored = ctx.sem("stored")
        with nc.Block() as block:
            @block.sync
            def _(sync):
                for t in range(NT):
                    sync.dma_start(out[t * P:(t + 1) * P, :], X[:, t, :]).then_inc(stored, 16)
                sync.wait_ge(stored, 16 * NT)


def _layouts(i):
    import numpy as np
    g = lambda n: np.asarray(i[n])
    con = np.ascontiguousarray
    halves = lambda a: con(a.reshape(2, CH, -1).transpose(1, 0, 2))
    o = {}
    x = g("x").reshape(T, C)
    o["x"] = con(x)
    o["xT"] = halves(x.T)
    o["w_in"] = halves(g("L0_conv_in_proj_w").T)
    o["cw"] = con(g("L0_conv_conv_w").reshape(DI, 9))
    o["cb"] = con(g("L0_conv_conv_b").reshape(DI, 1))
    xp = g("L0_conv_x_proj_w")
    o["wdt"] = con(xp[:, :RK].transpose(2, 0, 1))
    o["wB"] = con(np.repeat(xp[:, RK:RK + NS], CG, axis=1).transpose(2, 0, 1))
    o["wC"] = con(np.repeat(xp[:, RK + NS:], CG, axis=1).transpose(2, 0, 1))
    o["dtw"] = con(g("L0_conv_dt_projs_w").transpose(2, 0, 1))
    o["dtb"] = con(g("L0_conv_dt_projs_b").T)
    o["Alog"] = con(g("L0_conv_A_logs").reshape(KD, NG, CG, NS).transpose(3, 2, 0, 1).reshape(P, KD * NG))
    o["Dk"] = con(g("L0_conv_Ds").reshape(KD, DI).T)
    o["out_g"] = con(g("L0_conv_out_norm_g").reshape(DI, 1))
    o["out_b"] = con(g("L0_conv_out_norm_b").reshape(DI, 1))
    o["w_out0"] = con(g("L0_conv_out_proj_w").T)
    def padded_heads(w):
        z = np.zeros((C, 3, HG, 32), w.dtype)
        z[..., :HE] = w.reshape(C, 3, HG, HE)
        return z.reshape(2, CH, 3, P).transpose(1, 0, 2, 3)
    w = g("L1_conv_w_qkv")

    def doubled_heads(w):
        z = w.reshape(C, 3, HG, 1, HE)
        return np.concatenate([z, z], axis=3).reshape(2, CH, 3, P).transpose(1, 0, 2, 3)

    o["n_wqk"] = con(np.concatenate([doubled_heads(w[:, :C]), doubled_heads(w[:, C:2 * C])], axis=2))
    o["n_wv"] = halves(w[:, 2 * C:])
    w = g("L1_conv_w_out")
    o["n_wo"] = con(padded_heads(w.T).transpose(2, 3, 1, 0).reshape(3, P, C).transpose(1, 0, 2))
    w = g("L2_attn_w_qkv").T
    o["q_wqk"] = con(np.concatenate([padded_heads(w[:, :C]), padded_heads(w[:, C:2 * C])], axis=2).reshape(CH, -1))
    o["q_wv"] = halves(w[:, 2 * C:]).reshape(CH, -1)
    o["q_wp"] = halves(g("L2_attn_w_proj").T).reshape(CH, -1)
    o["q_w1"] = halves(g("L2_attn_w_fc1").T).reshape(CH, -1)
    o["q_w2"] = con(g("L2_attn_w_fc2").T.reshape(FT, P, C).transpose(1, 0, 2).reshape(P, -1))
    o["q_scales"] = con(g("L2_attn_scales"))
    bq = g("L2_attn_b_qkv")
    z = np.zeros((2, 3, HG, 32), bq.dtype)
    z[..., :HE] = bq[:2 * C].reshape(2, 3, HG, HE)
    o["q_bqk"] = con(z.reshape(6, P).T)
    o["q_b1"] = con(g("L2_attn_b_fc1").reshape(FT, P).T)
    o["q_rows"] = con(np.stack([g("L2_attn_g1"), g("L2_attn_beta1"), g("L2_attn_g2"), g("L2_attn_beta2"), bq[2 * C:],
                                g("L2_attn_b_proj"), g("L2_attn_b_fc2")]))
    w1 = np.concatenate([g("L2_ffn_w1"), g("L2_ffn_sw1").reshape(2, -1, C)])
    w3 = np.concatenate([g("L2_ffn_w3"), g("L2_ffn_sw3").reshape(2, -1, C)])
    w2 = np.concatenate([g("L2_ffn_w2"), g("L2_ffn_sw2").reshape(C, 2, -1).transpose(1, 0, 2)])
    def first_weights(*ws):
        w = np.concatenate(ws, axis=1).transpose(0, 2, 1)
        w = np.concatenate([w[:, :CA], np.concatenate([w[:, CA:], w[:, CA:]], axis=1)], axis=2)
        return con(again(w).reshape(-1, w.shape[2]))
    again = lambda w: np.concatenate([w, w[:2]])
    E, F = w1.shape[:2]
    o["m_up"] = first_weights(w1, w3)
    o["m_dn"] = con(again(w2).transpose(0, 2, 1).reshape(E + 2, F // P, P, C).transpose(0, 2, 1, 3).reshape((E + 2) * P, -1))
    o["m_gate"] = halves(g("L2_ffn_gate_w").T).reshape(CH, -1)
    w = g("L3_attn_w_qkv")
    o["a_wqk"] = halves(w[:, :2 * C])
    o["a_wv"] = halves(w[:, 2 * C:])
    o["a_wo"] = halves(g("L3_attn_w_out"))
    bq = g("L3_attn_b_qkv")
    o["a_bqk"] = con(bq[:2 * C].reshape(4, CH).T)
    o["a_rows"] = con(np.stack([bq[2 * C:], g("L3_attn_b_out")]))
    wi = g("L3_ffn_Wi")
    E, F = wi.shape[:2]
    o["g_up"] = first_weights(wi)
    o["g_dn"] = con(again(g("L3_ffn_Wo")).transpose(0, 2, 1).reshape(E + 2, F // P, P, C).transpose(0, 2, 1, 3).reshape((E + 2) * P, -1))
    o["g_b"] = con(again(g("L3_ffn_bi")).reshape(E + 2, F // P, P).transpose(0, 2, 1).reshape((E + 2) * P, -1))
    o["g_bo"] = con(g("L3_ffn_bo"))
    o["g_gate"] = halves(g("L3_ffn_Wr").T).reshape(CH, -1)
    o["iota"] = con(np.tile(np.arange(16, dtype=np.float32), (P, 1)))
    ch = np.arange(CH)
    p = np.arange(P)
    f = lambda a: con(a.astype(np.float32))
    o["group"] = f((ch[:, None] // 6 == ch[None, :] // 6) / np.float32(6))
    o["avg"] = f(np.ones((DI, DI)) / DI)
    o["selT"] = f((ch[:, None, None] == CG * np.arange(NG)[None, :, None] + p[None, None, :] % CG).transpose(2, 1, 0))
    o["sel"] = f(ch[:, None, None] % SG == CG * np.arange(SG // CG)[None, :, None] + p[None, None, :] % CG).reshape(CH, -1)
    o["ident"] = f(np.eye(P))
    start = np.clip(np.arange(HW) - HK // 2, 0, HW - HK)
    near = (np.arange(HW)[None, :] >= start[:, None]) & (np.arange(HW)[None, :] < start[:, None] + HK)
    inside = (near[:, None, :, None] & near[None, :, None, :]).reshape(QT, P, L)
    mask = np.where(inside, 0, -1e30).transpose(1, 0, 2)
    o["n_mask"] = f(np.stack([mask[:, 0, :KW], mask[:, 1, L - KW:]], axis=1))
    low = p[:, None] % (2 * HE) >= HE
    o["n_lowsel"] = f(np.concatenate([np.where(low, -1, 1), np.where(low, HE ** -0.5, 0)], axis=1))
    return o


def kernel(**inputs):
    import numpy as _np
    import concourse.bacc as _bacc
    from concourse.bass_utils import run_bass_kernel_spmd as _run

    nc = _bacc.Bacc("TRN2", target_bir_lowering=False, num_devices=1)
    arrays = _layouts(inputs)
    D = {n: nc.dram_tensor(f"in_{n}", a.shape, mybir.dt.from_np(a.dtype), kind="ExternalInput").ap()
         for n, a in arrays.items()}
    out = nc.dram_tensor("out", (T, C), F32, kind="ExternalOutput").ap()
    program(nc, D, out)
    r = _run(nc, [{f"in_{n}": a for n, a in arrays.items()}], core_ids=[0])
    return r.results[0]["out"].reshape(NB, HW, HW, C)
```
